# Optimizing a Trainium2 kernel written in Bass

```python
import numpy as np
import jax
import jax.numpy as jnp

def _softmax(x, axis=-1):
    return jax.nn.softmax(x, axis=axis)

def _gelu(x):
    return jax.nn.gelu(x, approximate=True)

def _silu(x):
    return jax.nn.silu(x)

def _sigmoid(x):
    return jax.nn.sigmoid(x)

def _layernorm(x, axis=-1, eps=1e-05):
    m = jnp.mean(x, axis=axis, keepdims=True)
    v = jnp.var(x, axis=axis, keepdims=True)
    return (x - m) / jnp.sqrt(v + eps)

def _scatter_add(tgt, idx, src, axis=0):
    return tgt.at[idx].add(src)

def _segment_sum(src, seg, n):
    return jax.ops.segment_sum(src, seg, n)
kernel_name = 'mk_xattn_seq_d2_seqx_r8_f0e6cd'

def setup_inputs(seed: int=0):
    np.random.seed(seed)
    _w = jnp.asarray

    def _rec_inputs():
        import jax
        import jax.numpy as jnp
        _rk = jax.random.key(seed)
        x = -0.0002928 + 1 * jax.random.normal(jax.random.fold_in(_rk, 1), (16, 128, 256), jnp.float32)
        _lenS = 128 - jax.random.randint(jax.random.fold_in(_rk, 7), (16,), 0, max(1, 128 // 4) + 1, jnp.int32)
        _lenS2 = 128 - jax.random.randint(jax.random.fold_in(_rk, 8), (16,), 0, max(1, 128 // 4) + 1, jnp.int32)
        _ctx_2048P = jax.random.normal(jax.random.fold_in(_rk, 11), (16, 16, 256), jnp.float32)
        _ctx_2048c = jax.random.dirichlet(jax.random.fold_in(_rk, 511), 0.3 * jnp.ones((16,), jnp.float32), (16, 128))
        _ctx_2048t = jnp.einsum('bsk,bkd->bsd', _ctx_2048c, _ctx_2048P)
        _ctx_2048t = _ctx_2048t * jax.lax.rsqrt(jnp.mean(jnp.square(_ctx_2048t)) + 1e-12) * 0.953939
        ctx_2048 = -1.39393e-06 + 0.999914 * (_ctx_2048t + 0.3 * jax.random.normal(jax.random.fold_in(_rk, 611), (16, 128, 256), jnp.float32))
        return (x, ctx_2048)
    x, ctx_2048 = _rec_inputs()

    def _L0_xattn_setup():
        import jax, jax.numpy as jnp
        import numpy as np
        D_MODEL = 128
        N_HEAD = 16
        D_HEAD = 64
        IDX_LIST = [128, 256]
        SCALE = 1.0 / D_HEAD ** 0.5
        LN_EPS = 1e-05
        key = jax.random.key(seed)
        ks = jax.random.split(key, 9)
        s = 0.02
        B, L = (2, 256)
        return {'z1ss': jax.random.normal(ks[0], (B, D_MODEL, L), dtype=jnp.float32), 'u1ss': jax.random.normal(ks[1], (B, D_MODEL, L), dtype=jnp.float32), 'Wqkv0': jax.random.normal(ks[2], (3 * N_HEAD * D_HEAD, D_MODEL), dtype=jnp.float32) * s, 'Wqkv1': jax.random.normal(ks[3], (3 * N_HEAD * D_HEAD, D_MODEL), dtype=jnp.float32) * s, 'Winj0': jax.random.normal(ks[4], (3 * N_HEAD * D_HEAD, D_MODEL), dtype=jnp.float32) * s, 'Winj1': jax.random.normal(ks[5], (3 * N_HEAD * D_HEAD, D_MODEL), dtype=jnp.float32) * s, 'Wo': jax.random.normal(ks[6], (D_MODEL, N_HEAD * D_HEAD), dtype=jnp.float32) * s, 'bo': jax.random.normal(ks[7], (D_MODEL,), dtype=jnp.float32) * s, 'r_w_bias': jax.random.uniform(ks[8], (N_HEAD, D_HEAD), minval=-0.05, maxval=0.05, dtype=jnp.float32)}
    _L0_xattn_all = _L0_xattn_setup()
    _L0_xattn_in = {k: v for k, v in _L0_xattn_all.items() if k in ('Wqkv0', 'Wqkv1', 'Winj0', 'Winj1', 'Wo', 'bo', 'r_w_bias')}
    del _L0_xattn_all

    def _L1_xattn_setup():
        import jax, jax.numpy as jnp
        import numpy as np
        B, Q, S1, S2 = (4, 32, 256, 256)
        D, H, K, F = (256, 16, 128, 1024)
        LN_EPS = 1e-05

        def _layer_norm(x, scale, offset):
            mu = jnp.mean(x, axis=-1, keepdims=True)
            var = jnp.var(x, axis=-1, keepdims=True)
            return (x - mu) * jax.lax.rsqrt(var + LN_EPS) * scale + offset

        def _cross_attention(q_in, kv_in, wq, bq, wk, bk, wv, bv, wo, bo, bias_k, bias_v):
            b, q_len, _ = q_in.shape
            t = kv_in.shape[1]
            qh = (q_in @ wq + bq).reshape(b, q_len, H, K)
            kh = (kv_in @ wk + bk).reshape(b, t, H, K)
            vh = (kv_in @ wv + bv).reshape(b, t, H, K)
            kh = jnp.concatenate([kh, jnp.broadcast_to(bias_k, (b, 1, H, K))], axis=1)
            vh = jnp.concatenate([vh, jnp.broadcast_to(bias_v, (b, 1, H, K))], axis=1)
            scale = jnp.sqrt(jnp.asarray(K, q_in.dtype))
            logits = jnp.einsum('bqhk,bthk->bhqt', qh, kh) / scale
            weights = jax.nn.softmax(logits, axis=-1)
            ctx = jnp.einsum('bhqt,bthk->bqhk', weights, vh).reshape(b, q_len, H * K)
            return ctx @ wo + bo

        def _forward(x, xf_1, xf_2, ln1_scale, ln1_offset, wq1, bq1, wk1, bk1, wv1, bv1, wo1, bo1, bias_k1, bias_v1, ln2_scale, ln2_offset, wq2, bq2, wk2, bk2, wv2, bv2, wo2, bo2, bias_k2, bias_v2, ln_mlp_scale, ln_mlp_offset, w_fc1, b_fc1, w_fc2, b_fc2):
            res = x
            h = _layer_norm(x, ln1_scale, ln1_offset)
            x = res + _cross_attention(h, xf_1, wq1, bq1, wk1, bk1, wv1, bv1, wo1, bo1, bias_k1, bias_v1)
            res = x
            h = _layer_norm(x, ln2_scale, ln2_offset)
            x = res + _cross_attention(h, xf_2, wq2, bq2, wk2, bk2, wv2, bv2, wo2, bo2, bias_k2, bias_v2)
            h = _layer_norm(x, ln_mlp_scale, ln_mlp_offset)
            h = jax.nn.gelu(h @ w_fc1 + b_fc1, approximate=False) @ w_fc2 + b_fc2
            return x + h
        key = jax.random.key(seed)
        ks = iter(jax.random.split(key, 64))

        def rn(shape, s=0.02):
            return jax.random.normal(next(ks), shape, jnp.float32) * s
        inp = {'x': rn((B, Q, D), 1.0), 'xf_1': rn((B, S1, D), 1.0), 'xf_2': rn((B, S2, D), 1.0)}
        for i in (1, 2):
            inp[f'ln{i}_scale'] = jnp.ones((D,), jnp.float32)
            inp[f'ln{i}_offset'] = jnp.zeros((D,), jnp.float32)
            inp[f'wq{i}'] = rn((D, H * K))
            inp[f'bq{i}'] = jnp.zeros((H * K,), jnp.float32)
            inp[f'wk{i}'] = rn((D, H * K))
            inp[f'bk{i}'] = jnp.zeros((H * K,), jnp.float32)
            inp[f'wv{i}'] = rn((D, H * K))
            inp[f'bv{i}'] = jnp.zeros((H * K,), jnp.float32)
            inp[f'wo{i}'] = rn((H * K, D))
            inp[f'bo{i}'] = jnp.zeros((D,), jnp.float32)
            inp[f'bias_k{i}'] = rn((1, 1, H, K))
            inp[f'bias_v{i}'] = rn((1, 1, H, K))
        inp['ln_mlp_scale'] = jnp.ones((D,), jnp.float32)
        inp['ln_mlp_offset'] = jnp.zeros((D,), jnp.float32)
        inp['w_fc1'] = rn((D, F))
        inp['b_fc1'] = jnp.zeros((F,), jnp.float32)
        inp['w_fc2'] = rn((F, D))
        inp['b_fc2'] = jnp.zeros((D,), jnp.float32)
        return inp
    _L1_xattn_all = _L1_xattn_setup()
    _L1_xattn_in = {k: v for k, v in _L1_xattn_all.items() if k in ('ln1_scale', 'ln1_offset', 'wq1', 'bq1', 'wk1', 'bk1', 'wv1', 'bv1', 'wo1', 'bo1', 'bias_k1', 'bias_v1', 'ln2_scale', 'ln2_offset', 'wq2', 'bq2', 'wk2', 'bk2', 'wv2', 'bv2', 'wo2', 'bo2', 'bias_k2', 'bias_v2', 'ln_mlp_scale', 'ln_mlp_offset', 'w_fc1', 'b_fc1', 'w_fc2', 'b_fc2')}
    del _L1_xattn_all
    return {'x': x, 'ctx_2048': ctx_2048, 'L0_xattn_Wqkv0': _L0_xattn_in['Wqkv0'], 'L0_xattn_Wqkv1': _L0_xattn_in['Wqkv1'], 'L0_xattn_Winj0': _L0_xattn_in['Winj0'], 'L0_xattn_Winj1': _L0_xattn_in['Winj1'], 'L0_xattn_Wo': _L0_xattn_in['Wo'], 'L0_xattn_bo': _L0_xattn_in['bo'], 'L0_xattn_r_w_bias': _L0_xattn_in['r_w_bias'], 'L1_xattn_ln1_scale': _L1_xattn_in['ln1_scale'], 'L1_xattn_ln1_offset': _L1_xattn_in['ln1_offset'], 'L1_xattn_wq1': _L1_xattn_in['wq1'], 'L1_xattn_bq1': _L1_xattn_in['bq1'], 'L1_xattn_wk1': _L1_xattn_in['wk1'], 'L1_xattn_bk1': _L1_xattn_in['bk1'], 'L1_xattn_wv1': _L1_xattn_in['wv1'], 'L1_xattn_bv1': _L1_xattn_in['bv1'], 'L1_xattn_wo1': _L1_xattn_in['wo1'], 'L1_xattn_bo1': _L1_xattn_in['bo1'], 'L1_xattn_bias_k1': _L1_xattn_in['bias_k1'], 'L1_xattn_bias_v1': _L1_xattn_in['bias_v1'], 'L1_xattn_ln2_scale': _L1_xattn_in['ln2_scale'], 'L1_xattn_ln2_offset': _L1_xattn_in['ln2_offset'], 'L1_xattn_wq2': _L1_xattn_in['wq2'], 'L1_xattn_bq2': _L1_xattn_in['bq2'], 'L1_xattn_wk2': _L1_xattn_in['wk2'], 'L1_xattn_bk2': _L1_xattn_in['bk2'], 'L1_xattn_wv2': _L1_xattn_in['wv2'], 'L1_xattn_bv2': _L1_xattn_in['bv2'], 'L1_xattn_wo2': _L1_xattn_in['wo2'], 'L1_xattn_bo2': _L1_xattn_in['bo2'], 'L1_xattn_bias_k2': _L1_xattn_in['bias_k2'], 'L1_xattn_bias_v2': _L1_xattn_in['bias_v2'], 'L1_xattn_ln_mlp_scale': _L1_xattn_in['ln_mlp_scale'], 'L1_xattn_ln_mlp_offset': _L1_xattn_in['ln_mlp_offset'], 'L1_xattn_w_fc1': _L1_xattn_in['w_fc1'], 'L1_xattn_b_fc1': _L1_xattn_in['b_fc1'], 'L1_xattn_w_fc2': _L1_xattn_in['w_fc2'], 'L1_xattn_b_fc2': _L1_xattn_in['b_fc2']}

def reference(x, ctx_2048, L0_xattn_Wqkv0, L0_xattn_Wqkv1, L0_xattn_Winj0, L0_xattn_Winj1, L0_xattn_Wo, L0_xattn_bo, L0_xattn_r_w_bias, L1_xattn_ln1_scale, L1_xattn_ln1_offset, L1_xattn_wq1, L1_xattn_bq1, L1_xattn_wk1, L1_xattn_bk1, L1_xattn_wv1, L1_xattn_bv1, L1_xattn_wo1, L1_xattn_bo1, L1_xattn_bias_k1, L1_xattn_bias_v1, L1_xattn_ln2_scale, L1_xattn_ln2_offset, L1_xattn_wq2, L1_xattn_bq2, L1_xattn_wk2, L1_xattn_bk2, L1_xattn_wv2, L1_xattn_bv2, L1_xattn_wo2, L1_xattn_bo2, L1_xattn_bias_k2, L1_xattn_bias_v2, L1_xattn_ln_mlp_scale, L1_xattn_ln_mlp_offset, L1_xattn_w_fc1, L1_xattn_b_fc1, L1_xattn_w_fc2, L1_xattn_b_fc2):
    import jax
    import jax.numpy as jnp

    def _L0_xattn_ref(z1ss, u1ss, Wqkv0, Wqkv1, Winj0, Winj1, Wo, bo, r_w_bias):
        import jax, jax.numpy as jnp
        import numpy as np
        D_MODEL = 128
        N_HEAD = 16
        D_HEAD = 64
        IDX_LIST = [128, 256]
        SCALE = 1.0 / D_HEAD ** 0.5
        LN_EPS = 1e-05
        bsz, d_model, qlen = z1ss.shape
        bounds = [0] + IDX_LIST
        Wq_list, Wi_list = ([Wqkv0, Wqkv1], [Winj0, Winj1])
        chunks = []
        for i in range(len(IDX_LIST)):
            s, e = (bounds[i], bounds[i + 1])
            h = jnp.einsum('od,bdl->bol', Wq_list[i], z1ss[:, :, s:e])
            h = h + jnp.einsum('od,bdl->bol', Wi_list[i], u1ss[:, :, s:e])
            chunks.append(h)
        w_heads = jnp.concatenate(chunks, axis=2)
        q, k, v = jnp.split(w_heads, 3, axis=1)
        q = q[:, :, -qlen:]
        klen = k.shape[2]
        q = q.reshape(bsz, N_HEAD, D_HEAD, qlen)
        k = k.reshape(bsz, N_HEAD, D_HEAD, klen)
        v = v.reshape(bsz, N_HEAD, D_HEAD, klen)
        rq = q + r_w_bias[None, :, :, None]
        score = jnp.einsum('bndi,bndj->bnij', rq, k) * SCALE
        prob = jax.nn.softmax(score, axis=-1)
        attn_vec = jnp.einsum('bnij,bndj->bndi', prob, v)
        attn_vec = attn_vec.reshape(bsz, N_HEAD * D_HEAD, qlen)
        attn_out = jnp.einsum('od,bdl->bol', Wo, attn_vec) + bo[None, :, None]
        x = attn_out + z1ss
        m = jnp.mean(x, axis=1, keepdims=True)
        var = jnp.var(x, axis=1, keepdims=True)
        return (x - m) * jax.lax.rsqrt(var + LN_EPS)

    def _L1_xattn_ref(x, xf_1, xf_2, ln1_scale, ln1_offset, wq1, bq1, wk1, bk1, wv1, bv1, wo1, bo1, bias_k1, bias_v1, ln2_scale, ln2_offset, wq2, bq2, wk2, bk2, wv2, bv2, wo2, bo2, bias_k2, bias_v2, ln_mlp_scale, ln_mlp_offset, w_fc1, b_fc1, w_fc2, b_fc2):
        import jax, jax.numpy as jnp
        import numpy as np
        B, Q, S1, S2 = (4, 32, 256, 256)
        D, H, K, F = (256, 16, 128, 1024)
        LN_EPS = 1e-05

        def _layer_norm(x, scale, offset):
            mu = jnp.mean(x, axis=-1, keepdims=True)
            var = jnp.var(x, axis=-1, keepdims=True)
            return (x - mu) * jax.lax.rsqrt(var + LN_EPS) * scale + offset

        def _cross_attention(q_in, kv_in, wq, bq, wk, bk, wv, bv, wo, bo, bias_k, bias_v):
            b, q_len, _ = q_in.shape
            t = kv_in.shape[1]
            qh = (q_in @ wq + bq).reshape(b, q_len, H, K)
            kh = (kv_in @ wk + bk).reshape(b, t, H, K)
            vh = (kv_in @ wv + bv).reshape(b, t, H, K)
            kh = jnp.concatenate([kh, jnp.broadcast_to(bias_k, (b, 1, H, K))], axis=1)
            vh = jnp.concatenate([vh, jnp.broadcast_to(bias_v, (b, 1, H, K))], axis=1)
            scale = jnp.sqrt(jnp.asarray(K, q_in.dtype))
            logits = jnp.einsum('bqhk,bthk->bhqt', qh, kh) / scale
            weights = jax.nn.softmax(logits, axis=-1)
            ctx = jnp.einsum('bhqt,bthk->bqhk', weights, vh).reshape(b, q_len, H * K)
            return ctx @ wo + bo

        def _forward(x, xf_1, xf_2, ln1_scale, ln1_offset, wq1, bq1, wk1, bk1, wv1, bv1, wo1, bo1, bias_k1, bias_v1, ln2_scale, ln2_offset, wq2, bq2, wk2, bk2, wv2, bv2, wo2, bo2, bias_k2, bias_v2, ln_mlp_scale, ln_mlp_offset, w_fc1, b_fc1, w_fc2, b_fc2):
            res = x
            h = _layer_norm(x, ln1_scale, ln1_offset)
            x = res + _cross_attention(h, xf_1, wq1, bq1, wk1, bk1, wv1, bv1, wo1, bo1, bias_k1, bias_v1)
            res = x
            h = _layer_norm(x, ln2_scale, ln2_offset)
            x = res + _cross_attention(h, xf_2, wq2, bq2, wk2, bk2, wv2, bv2, wo2, bo2, bias_k2, bias_v2)
            h = _layer_norm(x, ln_mlp_scale, ln_mlp_offset)
            h = jax.nn.gelu(h @ w_fc1 + b_fc1, approximate=False) @ w_fc2 + b_fc2
            return x + h
        return _forward(x, xf_1, xf_2, ln1_scale, ln1_offset, wq1, bq1, wk1, bk1, wv1, bv1, wo1, bo1, bias_k1, bias_v1, ln2_scale, ln2_offset, wq2, bq2, wk2, bk2, wv2, bv2, wo2, bo2, bias_k2, bias_v2, ln_mlp_scale, ln_mlp_offset, w_fc1, b_fc1, w_fc2, b_fc2)
    x = _L0_xattn_ref(x, ctx_2048, L0_xattn_Wqkv0, L0_xattn_Wqkv1, L0_xattn_Winj0, L0_xattn_Winj1, L0_xattn_Wo, L0_xattn_bo, L0_xattn_r_w_bias)
    x = _L1_xattn_ref(x, ctx_2048, ctx_2048, L1_xattn_ln1_scale, L1_xattn_ln1_offset, L1_xattn_wq1, L1_xattn_bq1, L1_xattn_wk1, L1_xattn_bk1, L1_xattn_wv1, L1_xattn_bv1, L1_xattn_wo1, L1_xattn_bo1, L1_xattn_bias_k1, L1_xattn_bias_v1, L1_xattn_ln2_scale, L1_xattn_ln2_offset, L1_xattn_wq2, L1_xattn_bq2, L1_xattn_wk2, L1_xattn_bk2, L1_xattn_wv2, L1_xattn_bv2, L1_xattn_wo2, L1_xattn_bo2, L1_xattn_bias_k2, L1_xattn_bias_v2, L1_xattn_ln_mlp_scale, L1_xattn_ln_mlp_offset, L1_xattn_w_fc1, L1_xattn_b_fc1, L1_xattn_w_fc2, L1_xattn_b_fc2)
    return x

_drawn_inputs = setup_inputs


def setup_inputs(seed=0):
    import zlib

    import numpy as np

    out = dict(_drawn_inputs(seed))
    spreads = {'L1_xattn_ln1_scale': (1.0, 0.6),
     'L1_xattn_ln1_offset': (0.0, 0.8),
     'L1_xattn_bq1': (0.0, 0.8),
     'L1_xattn_bk1': (0.0, 2.0),
     'L1_xattn_bv1': (0.0, 0.1),
     'L1_xattn_bo1': (0.0, 0.1),
     'L1_xattn_ln2_scale': (1.0, 0.6),
     'L1_xattn_ln2_offset': (0.0, 0.8),
     'L1_xattn_bq2': (0.0, 0.8),
     'L1_xattn_bk2': (0.0, 2.0),
     'L1_xattn_bv2': (0.0, 0.1),
     'L1_xattn_bo2': (0.0, 0.1),
     'L1_xattn_ln_mlp_scale': (1.0, 0.6),
     'L1_xattn_ln_mlp_offset': (0.0, 0.677),
     'L1_xattn_b_fc1': (0.0, 0.1),
     'L1_xattn_b_fc2': (0.0, 0.1)}
    factors = {'L0_xattn_Wqkv0': 8.0,
     'L0_xattn_Wqkv1': 8.0,
     'L0_xattn_Winj0': 8.0,
     'L0_xattn_Winj1': 8.0,
     'L0_xattn_Wo': 4.386,
     'L0_xattn_bo': 18.444,
     'L0_xattn_r_w_bias': 8.0,
     'L1_xattn_wq1': 8.0,
     'L1_xattn_wk1': 8.0,
     'L1_xattn_bias_k1': 64.0,
     'L1_xattn_bias_v1': 64.0,
     'L1_xattn_wq2': 8.0,
     'L1_xattn_wk2': 8.0,
     'L1_xattn_bias_k2': 64.0,
     'L1_xattn_bias_v2': 64.0}
    for name, (base, spread) in spreads.items():
        noise = np.random.default_rng([zlib.crc32(name.encode()), seed]).standard_normal(out[name].shape)
        drawn = base * np.exp(spread * noise) if base else spread * noise
        out[name] = jnp.asarray(drawn.astype(out[name].dtype))
    for name, factor in factors.items():
        out[name] = (out[name] * factor).astype(out[name].dtype)
    return out
```

```python
from contextlib import ExitStack

import concourse.bass as bass
from concourse import mybir

F32 = mybir.dt.float32
F32R = mybir.dt.float32r
I32 = mybir.dt.int32
ALU = mybir.AluOpType
ACT = mybir.ActivationFunctionType
AX_X = mybir.AxisListType.X
EPS = 1e-5
P = 128


class Mem:

    def __init__(self, nc, stack):
        self.nc, self.stack = nc, stack

    def sb(self, name, shape, dt=F32):
        return self.stack.enter_context(self.nc.sbuf_tensor(name, shape, dt))

    def psum(self, name):
        return self.stack.enter_context(self.nc.psum_tensor(name, [P, 512], F32))

    def sem(self, name):
        return self.stack.enter_context(self.nc.semaphore(name))

    def sems(self, *names):
        return [self.sem(n) for n in names]


def wait(eng, sem, value):
    if isinstance(value, int) and value <= 0:
        return
    eng.wait_ge(sem, value)


def three_pass(eng, out, w_hi, w_lo, m_hi, m_lo, start, stop, skip=False):
    eng.matmul(out, w_hi, m_lo, start=start, stop=False, skip_group_check=skip)
    eng.matmul(out, w_lo, m_hi, start=False, stop=False, skip_group_check=skip)
    return eng.matmul(out, w_hi, m_hi, start=False, stop=stop, skip_group_check=skip)



def attention0(nc, X, ident, banks, d, G):
    PAIRS, L, C = 8, 256, 2
    NB = 2 * PAIRS
    with ExitStack() as local:
        m = Mem(nc, local)
        names = ("wz0", "wz1", "wu0", "wu1")
        w_hi = {n: m.sb(f"{n}_hi", [P, 3072], F32R) for n in names}
        w_lo = {n: m.sb(f"{n}_lo", [P, 3072], F32R) for n in names}
        wo_hi = m.sb("wo0_hi", [P, PAIRS, P], F32R)
        wo_lo = m.sb("wo0_lo", [P, PAIRS, P], F32R)
        stage = [m.sb(f"stage0_{i}", [P, 1024]) for i in range(2)]
        u_raw = m.sb("u_raw", [P, 2, L])
        z_hi, z_lo = m.sb("z_hi", [P, 2, L], F32R), m.sb("z_lo", [P, 2, L], F32R)
        u_hi, u_lo = m.sb("u_hi", [P, 2, L], F32R), m.sb("u_lo", [P, 2, L], F32R)
        q_sb = [[m.sb(f"q{x}{i}", [P, 2, L]) for i in range(2)] for x in "AB"]
        k_sb = [m.sb(f"k{i}", [P, 2, L]) for i in range(2)]
        v_sb = m.sb("v0", [P, 2, C, 1024])
        probs = [[m.sb(f"p{x}{i}", [P, 2, L]) for i in range(2)] for x in "AB"]
        probsT = [m.sb(f"pT{x}", [P, 2, L]) for x in "AB"]
        nmax = [m.sb(f"nmax{x}", [P, 2, 2]) for x in "AB"]
        sums = [m.sb(f"sums{x}", [P, 2, 2]) for x in "AB"]
        rsum = [m.sb(f"rsum{x}", [P, 2, 2]) for x in "AB"]
        av_hi, av_lo = m.sb("av0_hi", [P, 2, L], F32R), m.sb("av0_lo", [P, 2, L], F32R)
        rwb, rwb8, bo = m.sb("rwb", [P, PAIRS]), m.sb("rwb8", [P, PAIRS]), m.sb("bo0", [P, 1])

        PJ, SB, TB, AVB, OUT = banks[0:2], banks[2:4], banks[4:6], banks[6], banks[7]

        (x_in, small_in, stage_in0, stage_in1, w_split_hi, w_split_lo, zeroed, rwb_ready,
         u_in, zu_hi, zu_lo, proj_done, qk_ready, v_ready, s_done, max_done,
         exp_done, rec_done, norm_done, t_done, ptA_ready, ptB_ready, av_done, avhi_ready,
         avlo_ready, w_done, out_done) = m.sems(*(f"a0_{n}" for n in (
             "x_in", "small_in", "stage_in0", "stage_in1", "w_split_hi", "w_split_lo", "zeroed", "rwb_ready",
             "u_in", "zu_hi", "zu_lo", "proj_done", "qk_ready", "v_ready", "s_done",
             "max_done", "exp_done", "rec_done", "norm_done", "t_done", "ptA_ready", "ptB_ready", "av_done",
             "avhi_ready", "avlo_ready", "w_done", "out_done")))
        stage_in = [stage_in0, stage_in1]

        pieces = []
        for j in (0, 1, 2):
            for n in names:
                cut = slice(1024 * j, 1024 * j + 1024)
                pieces.append((d[n][:, cut], w_hi[n][:, cut], w_lo[n][:, cut]))
        pieces.append((d["wo0"].rearrange("(p k) o -> k p o", k=P), wo_hi[:], wo_lo[:]))

        AHEAD, JOBS = 6, 3 * PAIRS

        def jobs(p, b):
            found = [("q" if b == 0 else "k", (p + 1) % PAIRS, int(p == PAIRS - 1))]
            if p in (1, 2):
                found.append(("v", 4 + 2 * (p - 1) + b, 0))
            if p == PAIRS - 1:
                found += [("v", 2 * b, 1), ("v", 2 * b + 1, 1)]
            return found

        def index_in_group(p, b):
            return sum(len(jobs(*divmod(i, 2))) for i in range(2 * p + b))

        in_order = [job for i in range(NB) for job in jobs(*divmod(i, 2))]
        K7_DONE = index_in_group(PAIRS - 2, 1) + 1

        def step_jobs(g, p, b, last):
            for i, job in enumerate(jobs(p, b), index_in_group(p, b)):
                if not (last and job[2]):
                    yield AHEAD + JOBS * g + i, (AHEAD + i) % 2, job, i

        ahead = [(n, n % 2, job) for n, job in enumerate([("q", 0, 0), ("k", 0, 0)] + [("v", c, 0) for c in range(4)])]

        def wait_emptied(eng, i, g):
            if i < 0 and isinstance(g, int) and g == 0:
                if i < -AHEAD:
                    return
                job, g = ahead[AHEAD + i][2], 0
            elif i < 0:
                job, g = in_order[JOBS + i], g - 1
            else:
                job = in_order[i]
            kind, which, further = job
            if kind == "v":
                eng.wait_ge(v_ready, 8 * (g + further) + which + 1)
            else:
                eng.wait_ge(qk_ready, 3 * (PAIRS * (g + further) + which) + (2 if kind == "q" else 3))

        def groups(eng, step):
            for i in range(NB):
                step(0, *divmod(i, 2), True, False)
            with eng.Fori(1, G - 1) as g:
                for i in range(NB):
                    step(g, *divmod(i, 2), False, False)
            for i in range(NB):
                step(G - 1, *divmod(i, 2), False, True)

        block = local.enter_context(nc.Block())

        @block.sync
        def _(sp):
            sp.dma_start(rwb[:], d["rwb"]).then_inc(small_in, 16)
            sp.dma_start(bo[:], d["bo0"]).then_inc(small_in, 16)
            sp.dma_start(ident[:], d["ident"]).then_inc(small_in, 16)
            sp.dma_start(u_raw[:], d["u"][0:2].rearrange("b d l -> d b l")).then_inc(u_in, 16)
            sp.dma_start(X[:, 0:2, :], d["x"][0:2].rearrange("b d l -> d b l")).then_inc(x_in, 16)
            for i, (src, _, _) in enumerate(pieces):
                if i >= 2:
                    sp.wait_ge(w_split_lo, i - 1)
                dst = stage[i % 2][:] if i < 12 else stage[i % 2][:].rearrange("k (p o) -> k p o", o=P)
                sp.dma_start(dst, src).then_inc(stage_in[i % 2], 16)
            sp.dma_start(X[:, 2:, :], d["x"][2:].rearrange("b d l -> d b l")).then_inc(x_in, 16)
            with sp.Fori(1, G) as g:
                sp.wait_ge(zu_lo, 2 * g)
                sp.dma_start(u_raw[:], d["u"][bass.ds(2 * g, 2)].rearrange("b d l -> d b l")).then_inc(u_in, 16)

        @block.gpsimd
        def _(pool):
            for i in range(2):
                pool.memset(q_sb[0][i][64:128], 0.0).then_inc(zeroed, 1)
                pool.memset(q_sb[1][i][0:64], 0.0).then_inc(zeroed, 1)

        @block.scalar
        def _(act):
            act.wait_ge(small_in, 48)
            act.mul(rwb8[:], rwb[:], 0.125).then_inc(rwb_ready, 1)
            act.wait_ge(rwb_ready, 1)

            def split_hi(g):
                act.wait_ge(u_in, 16 * (g + 1))
                act.activation(z_hi[:], X[:, bass.ds(2 * g, 2), :], ACT.Copy).then_inc(zu_hi, 1)
                act.activation(u_hi[:], u_raw[:], ACT.Copy).then_inc(zu_hi, 1)

            def evac(n, bank, job, g):
                if job[0] == "v":
                    return
                pair = PAIRS * (g + job[2]) + job[1]
                act.wait_ge(proj_done, n + 1)
                wait(act, s_done, 4 * (pair - 1))
                par = job[1] % 2
                src = PJ[bank][:].rearrange("p (c b l) -> p b c l", c=C, b=2)
                if job[0] == "q":
                    for x in range(2):
                        rows = slice(64 * x, 64 * x + 64)
                        act.activation(q_sb[x][par][rows].rearrange("p b (c l) -> p b c l", c=C), src[rows],
                                       ACT.Identity, bias=rwb8[rows, job[1]:job[1] + 1], scale=0.125).then_inc(qk_ready, 1)
                else:
                    act.activation(k_sb[par][:].rearrange("p b (c l) -> p b c l", c=C), src, ACT.Copy).then_inc(qk_ready, 1)

            act.wait_ge(x_in, 16)
            for i, (_, hi, _) in enumerate(pieces):
                act.wait_ge(stage_in[i % 2], 16 * (i // 2 + 1))
                src = stage[i % 2][:] if i < 12 else stage[i % 2][:].rearrange("k (p o) -> k p o", o=P)
                act.activation(hi, src, ACT.Copy).then_inc(w_split_hi, 1)
            split_hi(0)
            act.wait_ge(zeroed, 4)
            for n, bank, job in ahead:
                evac(n, bank, job, 0)

            def pt_b(u):
                act.wait_ge(t_done, 2 * u + 2)
                wait(act, av_done, u)
                act.activation(probsT[1][:].rearrange("p a l -> p (a l)"), TB[1][:], ACT.Copy).then_inc(ptB_ready, 1)

            def av_high(pair):
                act.wait_ge(av_done, 2 * pair + 2)
                wait(act, w_done, pair)
                act.activation(av_hi[:].rearrange("p b l -> p (b l)"), AVB[:], ACT.Copy).then_inc(avhi_ready, 1)

            def step(g, p, b, first, last):
                u = NB * g + 2 * p + b
                start = first and p == 0 and b == 0
                if p == PAIRS - 1 and b == 0 and not last:
                    act.wait_ge(proj_done, AHEAD + JOBS * g + K7_DONE)
                    split_hi(g + 1)
                for x in range(2):
                    act.wait_ge(max_done, 2 * u + x + 1)
                    if not (first and p == 0):
                        act.wait_ge(t_done, 2 * (u - 2) + x + 1)
                    for it in range(2):
                        ins = act.activation(probs[x][b][:, it, :], SB[x][:, L * it:L * it + L], ACT.Exp,
                                             bias=nmax[x][:, b, it:it + 1], accum_out=sums[x][:, b, it:it + 1])
                    ins.then_inc(exp_done, 1)
                if not start:
                    pt_b(u - 1)
                for n, bank, job, _ in step_jobs(g, p, b, last):
                    evac(n, bank, job, g)
                if b == 0 and not start:
                    av_high(PAIRS * g + p - 1)

            groups(act, step)
            pt_b(NB * G - 1)
            av_high(PAIRS * G - 1)

        @block.vector
        def _(dve):
            dve.wait_ge(x_in, 16)
            for i, (_, hi, lo) in enumerate(pieces):
                dve.wait_ge(w_split_hi, i + 1)
                src = stage[i % 2][:] if i < 12 else stage[i % 2][:].rearrange("k (p o) -> k p o", o=P)
                dve.tensor_tensor(lo, src, hi.bitcast(F32), ALU.subtract).then_inc(w_split_lo, 1)

            def split_lo(g):
                dve.wait_ge(zu_hi, 2 * g + 2)
                dve.tensor_tensor(z_lo[:], X[:, bass.ds(2 * g, 2), :], z_hi[:].bitcast(F32), ALU.subtract).then_inc(zu_lo, 1)
                dve.tensor_tensor(u_lo[:], u_raw[:], u_hi[:].bitcast(F32), ALU.subtract).then_inc(zu_lo, 1)

            def evac(n, bank, job, g):
                if job[0] != "v":
                    return
                c, gg = job[1], g + job[2]
                dve.wait_ge(proj_done, n + 1)
                wait(dve, av_done, NB * gg - (NB // 2 if c < 4 else 0) if not (isinstance(gg, int) and gg == 0) else 0)
                half_, rest = divmod(c, 4)
                dst = v_sb[:, rest // 2, rest % 2, 512 * half_:512 * half_ + 512]
                dve.tensor_copy(dst, PJ[bank][:]).then_inc(v_ready, 1)

            def pt_a(u):
                dve.wait_ge(t_done, 2 * u + 1)
                wait(dve, av_done, u)
                dve.tensor_copy(probsT[0][:].rearrange("p a l -> p (a l)"), TB[0][:]).then_inc(ptA_ready, 1)

            def av_low(pair):
                dve.wait_ge(avhi_ready, pair + 1)
                dve.tensor_tensor(av_lo[:].rearrange("p b l -> p (b l)"), AVB[:],
                                  av_hi[:].rearrange("p b l -> p (b l)").bitcast(F32), ALU.subtract).then_inc(avlo_ready, 1)

            def output(g):
                dve.wait_ge(w_done, PAIRS * (g + 1))
                Xg = X[:, bass.ds(2 * g, 2), :].rearrange("p b l -> p (b l)")
                dve.scalar_tensor_tensor(Xg, OUT[:], bo[:, 0:1], Xg, ALU.add, ALU.add).then_inc(out_done, 1)

            def step(g, p, b, first, last):
                u = NB * g + 2 * p + b
                start = first and p == 0 and b == 0
                if p == PAIRS - 1 and b == 0 and not last:
                    split_lo(g + 1)
                for x in range(2):
                    dve.wait_ge(s_done, 2 * u + x + 1)
                    dve.tensor_reduce(nmax[x][:, b, :], SB[x][:].rearrange("p (i j) -> p i j", i=2), AX_X, ALU.max,
                                      negate=True).then_inc(max_done, 1)
                if not start:
                    pt_a(u - 1)
                for x in range(2):
                    dve.wait_ge(exp_done, 2 * u + x + 1)
                    dve.reciprocal(rsum[x][:, b, :], sums[x][:, b, :]).then_inc(rec_done, 1)
                    dve.wait_ge(rec_done, 2 * u + x + 1)
                    for it in range(2):
                        row = probs[x][b][:, it, :]
                        ins = dve.tensor_scalar(row, row, rsum[x][:, b, it:it + 1], None, ALU.mult)
                    ins.then_inc(norm_done, 1)
                for n, bank, job, _ in step_jobs(g, p, b, last):
                    evac(n, bank, job, g)
                if b == 0 and not start:
                    av_low(PAIRS * g + p - 1)
                if not first and p == 1 and b == 0:
                    output(g - 1)

            split_lo(0)
            for n, bank, job in ahead:
                evac(n, bank, job, 0)
            groups(dve, step)
            pt_a(NB * G - 1)
            av_low(PAIRS * G - 1)
            output(G - 1)

        @block.tensor
        def _(pe):
            pe.wait_ge(w_split_lo, len(pieces))
            pe.wait_ge(small_in, 48)

            def project(n, bank, job, i, g):
                if job[2] or (isinstance(n, int) and n == 0):
                    pe.wait_ge(zu_lo, 2 * (g + job[2]) + 2)
                wait_emptied(pe, i - 2, g)
                if job[0] in "qk":
                    col = (0 if job[0] == "q" else 1024) + P * job[1]
                    cut = slice(col, col + P)
                    for c in range(C):
                        out = PJ[bank][:, 256 * c:256 * c + 256]
                        pos = slice(P * c, P * c + P)
                        three_pass(pe, out, w_hi[f"wz{c}"][:, cut], w_lo[f"wz{c}"][:, cut],
                                   z_hi[:, :, pos], z_lo[:, :, pos], True, False)
                        ins = three_pass(pe, out, w_hi[f"wu{c}"][:, cut], w_lo[f"wu{c}"][:, cut],
                                         u_hi[:, :, pos], u_lo[:, :, pos], False, True)
                else:
                    half_, rest = divmod(job[1], 4)
                    b, c = divmod(rest, 2)
                    pos = slice(P * c, P * c + P)
                    cut = slice(2048 + 512 * half_, 2048 + 512 * half_ + 512)
                    three_pass(pe, PJ[bank][:], z_hi[:, b, pos], z_lo[:, b, pos],
                               w_hi[f"wz{c}"][:, cut], w_lo[f"wz{c}"][:, cut], True, False)
                    ins = three_pass(pe, PJ[bank][:], u_hi[:, b, pos], u_lo[:, b, pos],
                                     w_hi[f"wu{c}"][:, cut], w_lo[f"wu{c}"][:, cut], False, True)
                ins.then_inc(proj_done, 1)

            def scores(g, p, b, first):
                u = NB * g + 2 * p + b
                pe.wait_ge(qk_ready, 3 * (PAIRS * g + p) + 3)
                for x in range(2):
                    if not (first and p == 0 and b == 0):
                        pe.wait_ge(exp_done, 2 * (u - 1) + x + 1)
                    for it in range(2):
                        ins = pe.matmul(SB[x][:, L * it:L * it + L], q_sb[x][p % 2][:, b, P * it:P * it + P],
                                        k_sb[p % 2][:, b, :], start=True, stop=True)
                    ins.then_inc(s_done, 1)

            def transposes(u, b):
                for x in range(2):
                    pe.wait_ge(norm_done, 2 * u + x + 1)
                    wait(pe, (ptA_ready, ptB_ready)[x], u)
                    for jt in range(2):
                        for it in range(2):
                            ins = pe.transpose(TB[x][:, L * jt + P * it:L * jt + P * it + P],
                                               probs[x][b][:, it, P * jt:P * jt + P], ident[:])
                    ins.then_inc(t_done, 1)

            def weighted(u, g, p, b):
                pe.wait_ge(v_ready, 8 * g + (8 if p >= 4 else 4))
                pe.wait_ge(ptA_ready, u + 1)
                pe.wait_ge(ptB_ready, u + 1)
                if b == 0:
                    wait(pe, avlo_ready, PAIRS * g + p)
                for jt in range(2):
                    for x in range(2):
                        col = P * p + 64 * x
                        ins = pe.matmul(AVB[64 * x:64 * x + 64, L * b:L * b + L], v_sb[:, b, jt, col:col + 64],
                                        probsT[x][:, jt, :], start=(jt == 0), stop=(jt == 1))
                ins.then_inc(av_done, 1)

            def out_product(pair, g, p):
                pe.wait_ge(avlo_ready, pair + 1)
                if p == 0:
                    wait(pe, out_done, g)
                flat = lambda t: t[:].rearrange("p b l -> p (b l)")
                three_pass(pe, OUT[:], wo_hi[:, p, :], wo_lo[:, p, :], flat(av_hi), flat(av_lo),
                           p == 0, p == PAIRS - 1).then_inc(w_done, 1)

            def step(g, p, b, first, last):
                u = NB * g + 2 * p + b
                start = first and p == 0 and b == 0
                scores(g, p, b, first)
                if not start:
                    transposes(u - 1, 1 - b)
                for n, bank, job, i in step_jobs(g, p, b, last):
                    project(n, bank, job, i, g)
                if not start:
                    if b == 1:
                        weighted(u - 1, g, p, 0)
                    elif p > 0:
                        weighted(u - 1, g, p - 1, 1)
                    else:
                        weighted(u - 1, g - 1, PAIRS - 1, 1)
                if b == 1 and not (first and p == 0):
                    if p > 0:
                        out_product(PAIRS * g + p - 1, g, p - 1)
                    else:
                        out_product(PAIRS * g - 1, g - 1, PAIRS - 1)

            for n, bank, job in ahead:
                project(n, bank, job, n - AHEAD, 0)
            groups(pe, step)
            transposes(NB * G - 1, 1)
            weighted(NB * G - 1, G - 1, PAIRS - 1, 1)
            out_product(PAIRS * G - 1, G - 1, PAIRS - 1)



def norm0(nc, X, banks, G):
    with ExitStack() as local:
        m = Mem(nc, local)
        mean_w, eps = m.sb("mean_w", [P, P]), m.sb("eps0", [P, 1])
        sq = [m.sb(f"sq{i}", [P, 512]) for i in range(2)]
        std = [m.sb(f"std{i}", [P, 512]) for i in range(2)]
        const, mean_done, centred, squared, var_done, std_ready, rstd_ready, normed = m.sems(
            "n0_const", "n0_mean_done", "n0_centred", "n0_squared", "n0_var_done", "n0_std_ready", "n0_rstd_ready", "n0_normed")
        Xg = [X[:, 2 * g:2 * g + 2, :].rearrange("p b l -> p (b l)") for g in range(G)]
        block = local.enter_context(nc.Block())

        @block.gpsimd
        def _(pool):
            pool.memset(mean_w[:], 1.0 / P).then_inc(const, 1)
            pool.memset(eps[:], EPS).then_inc(const, 1)

        @block.tensor
        def _(pe):
            pe.wait_ge(const, 2)
            for g in range(G):
                pe.matmul(banks[g][:], mean_w[:], Xg[g], start=True, stop=True).then_inc(mean_done, 1)
            for g in range(G):
                pe.wait_ge(squared, g + 1)
                pe.matmul(banks[g][:], mean_w[:], sq[g % 2][:], start=True, stop=True).then_inc(var_done, 1)

        @block.scalar
        def _(act):
            act.wait_ge(const, 2)
            for g in range(G + 1):
                if g < G:
                    act.wait_ge(centred, g + 1)
                    wait(act, var_done, g - 1)
                    act.activation(sq[g % 2][:], Xg[g], ACT.Square).then_inc(squared, 1)
                if g > 0:
                    act.wait_ge(var_done, g)
                    wait(act, normed, g - 2)
                    act.activation(std[(g - 1) % 2][:], banks[g - 1][:], ACT.Sqrt, bias=eps[:, 0:1]).then_inc(std_ready, 1)

        @block.vector
        def _(dve):
            for g in range(G + 2):
                if g < G:
                    dve.wait_ge(mean_done, g + 1)
                    dve.tensor_tensor(Xg[g], Xg[g], banks[g][:], ALU.subtract).then_inc(centred, 1)
                if g > 1:
                    n = g - 2
                    dve.wait_ge(std_ready, n + 1)
                    dve.reciprocal(std[n % 2][:], std[n % 2][:]).then_inc(rstd_ready, 1)
                    dve.wait_ge(rstd_ready, n + 1)
                    dve.tensor_tensor(Xg[n], Xg[n], std[n % 2][:], ALU.mult).then_inc(normed, 1)



class TokenNorm:

    STEPS = 16

    def __init__(self, m, name):
        self.stats, self.mv = m.sb(f"{name}_stats", [P, 2, 6]), m.sb(f"{name}_mv", [P, 2, 2])
        self.var, self.y, self.t = (m.sb(f"{name}_{n}", [P, 2]) for n in ("var", "y", "t"))
        self.waited = m.sb(f"{name}_waited", [P, 1])
        self.half = m.sb(f"{name}_half", [P, 2], I32)
        self.chain = m.sem(f"{name}_chain")

    def __call__(self, dve, Xg, out, base, done):
        count = 0

        def then(ins):
            nonlocal count
            ins.then_inc(self.chain, 1)
            count += 1

        def ready():
            dve.wait_ge(self.chain, base + count)

        for b in range(2):
            then(dve.bn_stats(self.stats[:, b, :], Xg[:, b, :]))
        ready()
        dve.memset(self.waited[:], 0.0)
        for b in range(2):
            then(dve.bn_aggr(self.mv[:, b, :], self.stats[:, b, :]))
        ready()
        then(dve.tensor_scalar(self.var[:], self.mv[:, :, 1], EPS, None, ALU.add))
        ready()
        then(dve.tensor_scalar(self.half[:], self.var[:].bitcast(I32), 1, None, ALU.logical_shift_right))
        ready()
        then(dve.tensor_scalar(self.y[:].bitcast(I32), self.half[:], -1.0, float(0x5F3759DF), ALU.mult, ALU.add))
        ready()
        for _ in range(3):
            then(dve.tensor_tensor(self.t[:], self.y[:], self.y[:], ALU.mult))
            ready()
            then(dve.scalar_tensor_tensor(self.t[:], self.t[:], -0.5, self.var[:], ALU.mult, ALU.mult))
            ready()
            then(dve.scalar_tensor_tensor(self.y[:], self.t[:], 1.5, self.y[:], ALU.add, ALU.mult))
            ready()
        for b in range(2):
            dve.tensor_scalar(out[:, b, :], Xg[:, b, :], self.mv[:, b, 0:1], self.y[:, b:b + 1],
                              ALU.subtract, ALU.mult).then_inc(done, 1)
        assert count == self.STEPS



def cross_layers(nc, X, ident, banks, d, G):
    H, KT, LAYERS = 16, 2, 2
    SCALE = P ** -0.5
    BIAS_ROW = 16

    def bias_row(h):
        return 32 * (h % 4) + h // 4

    with ExitStack() as local:
        m = Mem(nc, local)
        w_hi = {n: m.sb(f"{n}_hi", [P, KT, 2048], F32R) for n in ("wq", "wk", "wv")}
        w_lo = {n: m.sb(f"{n}_lo", [P, KT, 2048], F32R) for n in ("wq", "wk", "wv")}
        w_hi["wo"], w_lo["wo"] = m.sb("wo_hi", [P, H, 256], F32R), m.sb("wo_lo", [P, H, 256], F32R)
        stage = [m.sb(f"stage1_{i}", [P, 1024]) for i in range(2)]
        ln, bq, bqs, bk = m.sb("ln", [P, 2, KT]), m.sb("bq", [P, H]), m.sb("bqs", [P, H]), m.sb("bk", [P, H])
        bias_k, bias_v, bv = m.sb("bias_k", [P, H]), m.sb("bias_v", [P, H]), m.sb("bv", [P, 2048])
        diag = m.sb("diag", [P, 4, 16])
        tail_w = m.sb("tail_w", [P, 256])
        ctx_raw = m.sb("ctx_raw", [P, KT, 2, P])
        ctx_hi, ctx_lo = m.sb("ctx_hi", [P, KT, 2, P], F32R), m.sb("ctx_lo", [P, KT, 2, P], F32R)
        xn, hT = m.sb("xn", [P, 2, 256]), m.sb("hT", [P, KT, 256])
        hT_hi, hT_lo = m.sb("hT_hi", [P, KT, 256], F32R), m.sb("hT_lo", [P, KT, 256], F32R)
        q_sb = [m.sb(f"cq{i}", [P, 2, P]) for i in range(2)]
        k_sb = [m.sb(f"ck{i}", [P, 2, P + 1]) for i in range(2)]
        v_sb = m.sb("cv", [P, 2, 2048])
        probs = [m.sb(f"cp{i}", [P, 2, P + 1]) for i in range(2)]
        nmax, sums, rsum = (m.sb(f"c_{n}", [P, 2, 2]) for n in ("nmax", "sums", "rsum"))
        probsT = m.sb("cpT", [P, 2, P])
        wb, wbT = m.sb("wb", [P, 2, P]), m.sb("wbT", [P, 2, P])
        av_hi, av_lo = m.sb("cav_hi", [P, 2, P], F32R), m.sb("cav_lo", [P, 2, P], F32R)
        one = m.sb("one", [P, 1])
        norm = TokenNorm(m, "cn")

        PJ, SB, TB, AVB, AUX, OUT = banks[0:2], banks[2:4], banks[4], banks[5], banks[6], banks[7]
        (cleared, small_in, stage_in0, stage_in1, w_hi_out, w_lo_out, bqs_ready, diag_ready, tail_w_done, tail_w_ready,
         ctx_in, in_hi_ready, in_lo_ready, xn_ready, hT_done, hT_ready, proj_done, qk_ready, bias_k_ready,
         v_ready, s_done, max_done, exp_done, rec_done, norm_done, t_done, pT_ready, wbT_ready, av_done,
         avhi_ready, avlo_ready, o_done, out_added, tail_done, tail_added, layer_open) = m.sems(*(f"c_{n}" for n in (
             "cleared", "small_in", "stage_in0", "stage_in1", "w_hi_out", "w_lo_out", "bqs_ready", "diag_ready",
             "tail_w_done", "tail_w_ready", "ctx_in", "in_hi_ready", "in_lo_ready", "xn_ready", "hT_done",
             "hT_ready", "proj_done", "qk_ready", "bias_k_ready", "v_ready", "s_done", "max_done", "exp_done",
             "rec_done", "norm_done", "t_done", "pT_ready", "wbT_ready", "av_done", "avhi_ready", "avlo_ready",
             "o_done", "out_added", "tail_done", "tail_added", "layer_open")))
        stage_in = [stage_in0, stage_in1]

        pieces = [(n, kt, c) for c in range(2) for n in ("wq", "wk", "wv") for kt in range(KT)]
        pieces += [("wo", 0, c) for c in range(4)]
        NPIECE = len(pieces)

        def piece(i, tables):
            n, kt, c = pieces[i]
            return tables[n][:, 4 * c:4 * c + 4, :] if n == "wo" else tables[n][:, kt, 1024 * c:1024 * c + 1024]

        def staged(i):
            t = stage[i % 2][:]
            return t.rearrange("p (h o) -> p h o", o=256) if pieces[i][0] == "wo" else t

        def jobs(h):
            return [("qk", h)] * (h < H) + [("v", h)] * (h < 8)

        in_order = [job for h in range(H) for job in jobs(h)]
        JOBS = len(in_order)

        def step_jobs(h):
            return enumerate(jobs(h), sum(len(jobs(i)) for i in range(h)))

        def wait_emptied(eng, gg, i, first):
            if i < 0 and first:
                return
            kind, which = in_order[i]
            n = gg - 1 if i < 0 else gg
            if kind == "qk":
                eng.wait_ge(qk_ready, 2 * (H * n + which) + 2)
            else:
                eng.wait_ge(v_ready, 8 * n + which + 1)

        def layers(eng, begin, step, finish):
            with eng.Fori(0, LAYERS) as ly:
                begin(ly)
                for h in range(H):
                    step(ly, 0, h, True, False)
                with eng.Fori(1, G - 1) as g:
                    for h in range(H):
                        step(ly, g, h, False, False)
                for h in range(H + 4):
                    step(ly, G - 1, h, False, True)
                finish(ly)

        def unit(ly, g, h, lag, first):
            h -= lag
            if (h < 0 and first) or h >= H:
                return None
            return H * (G * ly + g) + h, h % H

        def ends_group(g, h, at, first, last):
            if h == at and not first:
                return g - 1
            if h == H + at:
                return g
            return None

        block = local.enter_context(nc.Block())

        @block.sync
        def _(sp):
            def load_ctx(g):
                sp.dma_start(ctx_raw[:], d["ctxT"][:, :, bass.ds(2 * g, 2), :]).then_inc(ctx_in, 16)

            sp.wait_ge(cleared, 2)
            with sp.Fori(0, LAYERS) as ly:
                sp.wait_ge(layer_open, ly + 1)
                one = bass.ds(ly, 1)
                sp.dma_start(ln[:], d["ln"][one].rearrange("a p i k -> p (a i) k")).then_inc(small_in, 16)
                for t, name in ((bq, "bq"), (bk, "bk"), (bias_k, "bias_k"), (bias_v, "bias_v")):
                    sp.dma_start(t[:], d[name][one].rearrange("a p h -> p (a h)")).then_inc(small_in, 16)
                sp.dma_start(tail_w[BIAS_ROW:BIAS_ROW + 1, :], d["bo"][one]).then_inc(small_in, 16)
                sp.dma_start(bv[:], d["bv"][one].to_broadcast([P, 2048])).then_inc(small_in, 16)
                load_ctx(0)
                for i, (n, kt, c) in enumerate(pieces):
                    if i >= 2:
                        sp.wait_ge(w_lo_out, NPIECE * ly + i - 1)
                    if n == "wo":
                        src = d[n][one].rearrange("a (h k) o -> k (a h) o", k=P)[:, 4 * c:4 * c + 4, :]
                    else:
                        src = d[n][one].rearrange("a (t p) n -> p (a t) n", p=P)[:, kt, 1024 * c:1024 * c + 1024]
                    sp.dma_start(staged(i), src).then_inc(stage_in[i % 2], 16)
                with sp.Fori(1, G) as g:
                    sp.wait_ge(in_lo_ready, 2 * (G * ly + g))
                    load_ctx(g)

        @block.gpsimd
        def _(pool):
            pool.memset(tail_w[:], 0.0).then_inc(cleared, 1)
            pool.memset(diag[:], 0.0).then_inc(cleared, 1)
            pool.memset(wb[:], 0.0).then_inc(cleared, 1)
            pool.wait_ge(cleared, 3)
            pool.memset(wb[:, :, BIAS_ROW:BIAS_ROW + 1], 1.0).then_inc(cleared, 1)
            pool.memset(one[:], 1.0).then_inc(cleared, 1)
            pool.wait_ge(cleared, 5)

            def begin(ly):
                pool.wait_ge(small_in, 16 * 7 * (ly + 1))

            def step(ly, g, h, first, last):
                if h >= H:
                    return
                n, _ = unit(ly, g, h, 0, first)
                if not (first and h < 2):
                    pool.wait_ge(s_done, n - 1)
                for b in range(2):
                    ins = pool.tensor_tensor(k_sb[h % 2][:, b, P:P + 1], bias_k[:, h:h + 1], one[:], ALU.mult)
                ins.then_inc(bias_k_ready, 1)

            layers(pool, begin, step, lambda ly: None)

        @block.scalar
        def _(act):
            def split_hi(ly, g):
                n = G * ly + g
                act.wait_ge(ctx_in, 16 * (n + 1))
                act.activation(ctx_hi[:], ctx_raw[:], ACT.Copy).then_inc(in_hi_ready, 1)
                act.wait_ge(hT_ready, KT * (n + 1))
                act.activation(hT_hi[:], hT[:], ACT.Copy).then_inc(in_hi_ready, 1)

            def transposed_norm(n):
                act.wait_ge(hT_done, n + 1)
                for kt in range(KT):
                    act.activation(hT[:, kt, :], AUX[:, 256 * kt:256 * kt + 256], ACT.Identity,
                                   bias=ln[:, 1, kt:kt + 1], scale=ln[:, 0, kt:kt + 1]).then_inc(hT_ready, 1)

            def begin(ly):
                act.wait_ge(small_in, 16 * 7 * (ly + 1))
                act.mul(bqs[:], bq[:], SCALE).then_inc(bqs_ready, 1)
                act.wait_ge(bqs_ready, ly + 1)
                for i in range(NPIECE):
                    act.wait_ge(stage_in[i % 2], 16 * (NPIECE // 2 * ly + i // 2 + 1))
                    act.activation(piece(i, w_hi), staged(i), ACT.Copy).then_inc(w_hi_out, 1)
                transposed_norm(G * ly)
                split_hi(ly, 0)

            def step(ly, g, h, first, last):
                n = G * ly + g
                if h == 0 and not first:
                    act.wait_ge(proj_done, JOBS * n)
                    split_hi(ly, g)
                if found := unit(ly, g, h, 1, first):
                    u, head = found
                    par = head % 2
                    act.wait_ge(max_done, u + 1)
                    if not (first and h < 3):
                        act.wait_ge(t_done, u - 1)
                    for b in range(2):
                        ins = act.activation(probs[par][:, b, :], SB[par][:, 256 * b:256 * b + P + 1], ACT.Exp,
                                             bias=nmax[:, par, b:b + 1], accum_out=sums[:, par, b:b + 1])
                    ins.then_inc(exp_done, 1)
                for i, (kind, which) in step_jobs(h):
                    if kind == "qk":
                        u, _ = unit(ly, g, h, 0, first)
                        act.wait_ge(proj_done, JOBS * n + i + 1)
                        if not (first and h < 2):
                            act.wait_ge(s_done, u - 1)
                        act.activation(q_sb[h % 2][:], PJ[i % 2][:, 0:256].rearrange("p (b t) -> p b t", b=2), ACT.Identity,
                                       bias=bqs[:, h:h + 1], scale=SCALE).then_inc(qk_ready, 1)
                        act.activation(k_sb[h % 2][:, :, 0:P], PJ[i % 2][:, 256:512].rearrange("p (b t) -> p b t", b=2),
                                       ACT.Identity, bias=bk[:, h:h + 1]).then_inc(qk_ready, 1)
                if found := unit(ly, g, h, 2, first):
                    u, _ = found
                    act.wait_ge(av_done, u + 1)
                    if not (first and h < 3):
                        act.wait_ge(o_done, u)
                    act.activation(av_hi[:], AVB[:, 0:256].rearrange("p (b t) -> p b t", b=2), ACT.Copy).then_inc(avhi_ready, 1)
                if h == 9 and not last:
                    transposed_norm(n + 1)

            layers(act, begin, step, lambda ly: None)

        @block.vector
        def _(dve):
            def split_lo(ly, g):
                n = G * ly + g
                dve.wait_ge(in_hi_ready, 2 * n + 1)
                dve.tensor_tensor(ctx_lo[:], ctx_raw[:], ctx_hi[:].bitcast(F32), ALU.subtract).then_inc(in_lo_ready, 1)
                dve.wait_ge(in_hi_ready, 2 * n + 2)
                dve.tensor_tensor(hT_lo[:], hT[:], hT_hi[:].bitcast(F32), ALU.subtract).then_inc(in_lo_ready, 1)

            def flat(g):
                return X[:, bass.ds(2 * g, 2), :].rearrange("p b l -> p (b l)")

            def normalize(n, g):
                norm(dve, X[:, bass.ds(2 * g, 2), :], xn, TokenNorm.STEPS * n, xn_ready)

            def begin(ly):
                dve.memset(norm.waited[:], 0.0).then_inc(layer_open, 1)
                normalize(G * ly, 0)
                dve.wait_ge(small_in, 16 * 7 * (ly + 1))
                dve.wait_ge(cleared, 4)
                dve.tensor_copy(diag[:, :, 0:16:5], bias_v[:].rearrange("p (j c) -> p c j", c=4)).then_inc(diag_ready, 1)
                for i in range(NPIECE):
                    dve.wait_ge(w_hi_out, NPIECE * ly + i + 1)
                    dve.tensor_tensor(piece(i, w_lo), staged(i), piece(i, w_hi).bitcast(F32), ALU.subtract).then_inc(w_lo_out, 1)
                split_lo(ly, 0)
                dve.wait_ge(tail_w_done, ly + 1)
                for c in range(4):
                    ins = dve.tensor_copy(tail_w[32 * c:32 * c + 4, :], AUX[32 * c:32 * c + 4, 0:256])
                ins.then_inc(tail_w_ready, 1)

            def step(ly, g, h, first, last):
                n = G * ly + g
                if h == 0 and not first:
                    split_lo(ly, g)
                if (ended := ends_group(g, h, 3, first, last)) is not None:
                    dve.wait_ge(o_done, H * (G * ly + ended + 1))
                    dve.tensor_tensor(flat(ended), flat(ended), OUT[:], ALU.add).then_inc(out_added, 1)
                if found := unit(ly, g, h, 1, first):
                    u, head = found
                    par = head % 2
                    dve.wait_ge(s_done, u + 1)
                    dve.tensor_reduce(nmax[:, par, :], SB[par][:].rearrange("p (b t) -> p b t", b=2)[:, :, 0:P + 1], AX_X,
                                      ALU.max, negate=True).then_inc(max_done, 1)
                if found := unit(ly, g, h, 2, first):
                    u, head = found
                    dve.wait_ge(t_done, u + 1)
                    if not (first and h < 3):
                        dve.wait_ge(av_done, u)
                    dve.tensor_copy(probsT[:], TB[:, 0:256].rearrange("p (b t) -> p b t", b=2)).then_inc(pT_ready, 1)
                    if head == H - 1:
                        dve.tensor_copy(wbT[:], TB[:, 256:512].rearrange("p (b t) -> p b t", b=2)).then_inc(wbT_ready, 1)
                if found := unit(ly, g, h, 1, first):
                    u, head = found
                    par = head % 2
                    dve.wait_ge(exp_done, u + 1)
                    dve.reciprocal(rsum[:, par, :], sums[:, par, :]).then_inc(rec_done, 1)
                    dve.wait_ge(rec_done, u + 1)
                    if head == 0 and not first:
                        dve.wait_ge(t_done, u)
                    for b in range(2):
                        dve.tensor_scalar(probs[par][:, b, 0:P], probs[par][:, b, 0:P], rsum[:, par, b:b + 1], None, ALU.mult)
                    col = bias_row(head)
                    dve.tensor_tensor(wb[:, :, col:col + 1], probs[par][:, :, P:P + 1], rsum[:, par, :].rearrange("p (b o) -> p b o", o=1),
                                      ALU.mult).then_inc(norm_done, 1)
                for i, (kind, c) in step_jobs(h):
                    if kind == "v":
                        dve.wait_ge(proj_done, JOBS * n + i + 1)
                        if not first:
                            dve.wait_ge(av_done, H * (n - 1) + 4 * (c // 2) + 4)
                        cut = slice(512 * (c // 2), 512 * (c // 2) + 512)
                        dve.tensor_tensor(v_sb[:, c % 2, cut], PJ[i % 2][:], bv[:, cut], ALU.add).then_inc(v_ready, 1)
                if found := unit(ly, g, h, 2, first):
                    u, _ = found
                    dve.wait_ge(avhi_ready, u + 1)
                    dve.tensor_tensor(av_lo[:], AVB[:, 0:256].rearrange("p (b t) -> p b t", b=2), av_hi[:].bitcast(F32),
                                      ALU.subtract).then_inc(avlo_ready, 1)
                if (ended := ends_group(g, h, 3, first, last)) is not None:
                    dve.wait_ge(tail_done, G * ly + ended + 1)
                    dve.wait_ge(out_added, G * ly + ended + 1)
                    dve.tensor_tensor(flat(ended), flat(ended), AUX[:], ALU.add).then_inc(tail_added, 1)
                if h == 5 and not last:
                    normalize(n + 1, g + 1)

            def finish(ly):
                dve.wait_ge(tail_added, G * (ly + 1))

            layers(dve, begin, step, finish)

        @block.tensor
        def _(pe):
            def transposed_norm(n, before):
                pe.wait_ge(xn_ready, 2 * (n + 1))
                if before:
                    pe.wait_ge(*before)
                for b in range(2):
                    for kt in range(KT):
                        col = 256 * kt + P * b
                        ins = pe.transpose(AUX[:, col:col + P], xn[:, b, P * kt:P * kt + P], ident[:])
                ins.then_inc(hT_done, 1)

            def project(n, i, kind, which, first):
                if (kind, which) == ("qk", 0):
                    pe.wait_ge(in_lo_ready, 2 * (n + 1))
                wait_emptied(pe, n, i - 2, first)
                bank = PJ[i % 2]
                if kind == "qk":
                    cut = slice(P * which, P * which + P)
                    for j, (w, hi, lo) in enumerate((("wq", hT_hi, hT_lo), ("wk", ctx_hi, ctx_lo))):
                        out = bank[:, 256 * j:256 * j + 256]
                        for kt in range(KT):
                            ins = three_pass(pe, out, w_hi[w][:, kt, cut], w_lo[w][:, kt, cut],
                                             hi[:, kt], lo[:, kt], kt == 0, kt == KT - 1)
                else:
                    b = which % 2
                    cut = slice(512 * (which // 2), 512 * (which // 2) + 512)
                    for kt in range(KT):
                        ins = three_pass(pe, bank[:], ctx_hi[:, kt, b, :], ctx_lo[:, kt, b, :],
                                         w_hi["wv"][:, kt, cut], w_lo["wv"][:, kt, cut], kt == 0, kt == KT - 1)
                ins.then_inc(proj_done, 1)

            def begin(ly):
                transposed_norm(G * ly, None)
                pe.wait_ge(w_lo_out, NPIECE * (ly + 1))
                pe.wait_ge(diag_ready, ly + 1)
                pe.wait_ge(hT_ready, KT * (G * ly + 1))
                for j in range(4):
                    for c in range(4):
                        for w in (w_hi, w_lo):
                            ins = pe.matmul(AUX[32 * c:32 * c + 4, 0:256], diag[:, c, 4 * j:4 * j + 4],
                                            w["wo"][:, 4 * j + c, :].bitcast(F32), start=(j == 0 and w is w_hi),
                                            stop=(j == 3 and w is w_lo))
                ins.then_inc(tail_w_done, 1)

            def step(ly, g, h, first, last):
                n = G * ly + g
                if found := unit(ly, g, h, 1, first):
                    u, head = found
                    par = head % 2
                    pe.wait_ge(qk_ready, 2 * u + 2)
                    pe.wait_ge(bias_k_ready, u + 1)
                    if not (first and h < 3):
                        pe.wait_ge(exp_done, u - 1)
                    for b in range(2):
                        ins = pe.matmul(SB[par][:, 256 * b:256 * b + P + 1], q_sb[par][:, b, :], k_sb[par][:, b, :],
                                        start=True, stop=True)
                    ins.then_inc(s_done, 1)
                if found := unit(ly, g, h, 2, first):
                    u, head = found
                    par = head % 2
                    pe.wait_ge(norm_done, u + 1)
                    if not (first and h < 3):
                        pe.wait_ge(pT_ready, u)
                    if head == 0 and not first:
                        pe.wait_ge(wbT_ready, n)
                    for b in range(2):
                        ins = pe.transpose(TB[:, P * b:P * b + P], probs[par][:, b, 0:P], ident[:])
                    if head == H - 1:
                        for b in range(2):
                            ins = pe.transpose(TB[:, 256 + P * b:256 + P * b + P], wb[:, b, :], ident[:])
                    ins.then_inc(t_done, 1)
                if (ended := ends_group(g, h, 3, first, last)) is not None:
                    e = G * ly + ended
                    pe.wait_ge(wbT_ready, e + 1)
                    if h < H:
                        pe.wait_ge(hT_ready, KT * (e + 2))
                    else:
                        pe.wait_ge(tail_added, e)
                    for b in range(2):
                        ins = pe.matmul(AUX[:, 256 * b:256 * b + 256], wbT[:, b, :], tail_w[:], start=True, stop=True)
                    ins.then_inc(tail_done, 1)

                def projections():
                    for i, (kind, which) in step_jobs(h):
                        project(n, i, kind, which, first)

                if h > 0:
                    projections()
                if found := unit(ly, g, h, 2, first):
                    u, head = found
                    pe.wait_ge(pT_ready, u + 1)
                    pe.wait_ge(v_ready, 8 * (n - (1 if h < 2 else 0)) + 2 * (head // 4) + 2)
                    if not (first and h < 3):
                        pe.wait_ge(avlo_ready, u)
                    for b in range(2):
                        ins = pe.matmul(AVB[:, P * b:P * b + P], v_sb[:, b, P * head:P * head + P], probsT[:, b, :],
                                        start=True, stop=True)
                    ins.then_inc(av_done, 1)
                if found := unit(ly, g, h, 3, first):
                    u, head = found
                    pe.wait_ge(avlo_ready, u + 1)
                    if head == 0 and not first:
                        pe.wait_ge(out_added, n)
                    for b in range(2):
                        ins = three_pass(pe, OUT[:, 256 * b:256 * b + 256], av_hi[:, b, :], av_lo[:, b, :],
                                         w_hi["wo"][:, head, :], w_lo["wo"][:, head, :],
                                         head == 0 and b == 0, head == H - 1 and b == 1, skip=True)
                    ins.then_inc(o_done, 1)
                if h == 0:
                    projections()
                if h == 8 and not last:
                    transposed_norm(n + 1, (tail_w_ready, ly + 1) if first else (tail_added, n))

            layers(pe, begin, step, lambda ly: None)



def mlp(nc, X, ident, banks, d, out, G):
    KT, F, J = 2, 1024, 4
    with ExitStack() as local:
        m = Mem(nc, local)
        w1_raw, w2_raw = m.sb("w1_raw", [P, KT, F]), m.sb("w2_raw", [P, 8, 256])
        w1_hi, w1_lo = m.sb("w1_hi", [P, KT, F], F32R), m.sb("w1_lo", [P, KT, F], F32R)
        w2_hi, w2_lo = m.sb("w2_hi", [P, 8, 256], F32R), m.sb("w2_lo", [P, 8, 256], F32R)
        ln, b1, b2 = m.sb("mln", [P, 2, KT]), m.sb("b1", [P, 8]), m.sb("b2", [P, 2, 256])
        xn, hT = m.sb("mxn", [P, 2, 256]), m.sb("mhT", [P, KT, 256])
        hT_hi, hT_lo = m.sb("mhT_hi", [P, KT, 256], F32R), m.sb("mhT_lo", [P, KT, 256], F32R)
        act_f = [m.sb(f"gelu{i}", [P, 2, 256]) for i in range(2)]
        act_hi = [m.sb(f"gelu_hi{i}", [P, 2, 256], F32R) for i in range(2)]
        act_lo = [m.sb(f"gelu_lo{i}", [P, 2, 256], F32R) for i in range(2)]
        norm = TokenNorm(m, "mn")
        FC1, AUX, OUT = banks[0:2], banks[2], banks[3]
        (small_in, w1_in, w2_in, w_hi_out, w_lo_out, xn_ready, hT_done, hT_ready, hT_hi_ready, hT_lo_ready, fc1_done,
         gelu_ready, act_hi_ready, act_lo_ready, b2_added, fc2_done, y_ready, stored) = m.sems(*(f"m_{n}" for n in (
             "small_in", "w1_in", "w2_in", "w_hi_out", "w_lo_out", "xn_ready", "hT_done", "hT_ready", "hT_hi_ready",
             "hT_lo_ready", "fc1_done", "gelu_ready", "act_hi_ready", "act_lo_ready", "b2_added", "fc2_done",
             "y_ready", "stored")))

        def groups(eng, step):
            for j in range(J):
                step(0, j, True, False)
            with eng.Fori(1, G - 1) as g:
                for j in range(J):
                    step(g, j, False, False)
            for j in range(J + 1):
                step(G - 1, j, False, True)

        def flat(t):
            return t.rearrange("p b l -> p (b l)")

        def Xg(g):
            return X[:, bass.ds(2 * g, 2), :]

        block = local.enter_context(nc.Block())

        @block.sync
        def _(sp):
            sp.dma_start(w1_raw[:], d["w1"].rearrange("(t p) f -> p t f", p=P)).then_inc(w1_in, 16)
            sp.dma_start(ln[:], d["mln"]).then_inc(small_in, 16)
            sp.dma_start(b1[:], d["b1"]).then_inc(small_in, 16)
            sp.dma_start(w2_raw[:], d["w2"].rearrange("(t p) o -> p t o", p=P)).then_inc(w2_in, 16)
            for b in range(2):
                sp.dma_start(b2[:, b, :], d["b2"].to_broadcast([P, 256])).then_inc(small_in, 16)
            with sp.Fori(0, G) as g:
                sp.wait_ge(y_ready, g + 1)
                sp.dma_start(out[bass.ds(2 * g, 2)].rearrange("b q f -> q b f"), Xg(g)).then_inc(stored, 16)
            sp.wait_ge(stored, 16 * G)

        @block.gpsimd
        def _(pool):
            pool.wait_ge(small_in, 64)
            with pool.Fori(0, G) as g:
                pool.wait_ge(xn_ready, 2 * (g + 1))
                pool.tensor_tensor(Xg(g), Xg(g), b2[:], ALU.add).then_inc(b2_added, 1)

        @block.scalar
        def _(act):
            def transposed_norm(g):
                act.wait_ge(hT_done, g + 1)
                for kt in range(KT):
                    act.activation(hT[:, kt, :], AUX[:, 256 * kt:256 * kt + 256], ACT.Identity,
                                   bias=ln[:, 1, kt:kt + 1], scale=ln[:, 0, kt:kt + 1]).then_inc(hT_ready, 1)

            act.wait_ge(small_in, 64)
            act.wait_ge(w1_in, 16)
            act.activation(w1_hi[:], w1_raw[:], ACT.Copy).then_inc(w_hi_out, 1)
            transposed_norm(0)
            act.wait_ge(w2_in, 16)
            act.activation(w2_hi[:], w2_raw[:], ACT.Copy).then_inc(w_hi_out, 1)

            def step(g, j, first, last):
                if j == J:
                    return
                u = J * g + j
                act.wait_ge(fc1_done, u + 1)
                if not (first and j < 2):
                    act.wait_ge(act_lo_ready, u - 1)
                for i in range(2):
                    ins = act.activation(act_f[j % 2][:, i, :], FC1[j % 2][:, 256 * i:256 * i + 256], ACT.Gelu,
                                         bias=b1[:, 2 * j + i:2 * j + i + 1])
                ins.then_inc(gelu_ready, 1)
                if j == 2 and not last:
                    transposed_norm(g + 1)

            groups(act, step)

        @block.vector
        def _(dve):
            def normalize(g):
                norm(dve, Xg(g), xn, TokenNorm.STEPS * g, xn_ready)

            def split(g):
                dve.wait_ge(hT_ready, KT * (g + 1))
                if not (isinstance(g, int) and g == 0):
                    dve.wait_ge(fc1_done, J * g)
                dve.tensor_copy(hT_hi[:], hT[:]).then_inc(hT_hi_ready, 1)
                dve.wait_ge(hT_hi_ready, g + 1)
                dve.tensor_tensor(hT_lo[:], hT[:], hT_hi[:].bitcast(F32), ALU.subtract).then_inc(hT_lo_ready, 1)

            normalize(0)
            for i, (raw, hi, lo) in enumerate(((w1_raw, w1_hi, w1_lo), (w2_raw, w2_hi, w2_lo))):
                dve.wait_ge(w_hi_out, i + 1)
                dve.tensor_tensor(lo[:], raw[:], hi[:].bitcast(F32), ALU.subtract).then_inc(w_lo_out, 1)
                if i == 0:
                    split(0)

            def step(g, j, first, last):
                u = J * g + j
                if j == 0 and not first:
                    split(g)
                if j < J:
                    dve.wait_ge(gelu_ready, u + 1)
                    if not (first and j < 2):
                        dve.wait_ge(fc2_done, u - 1)
                    dve.tensor_copy(act_hi[j % 2][:], act_f[j % 2][:]).then_inc(act_hi_ready, 1)
                    dve.wait_ge(act_hi_ready, u + 1)
                    dve.tensor_tensor(act_lo[j % 2][:], act_f[j % 2][:], act_hi[j % 2][:].bitcast(F32), ALU.subtract).then_inc(act_lo_ready, 1)
                if (j == 0 and not first) or j == J:
                    ended = g if j == J else g - 1
                    dve.wait_ge(fc2_done, J * (ended + 1))
                    dve.wait_ge(b2_added, ended + 1)
                    dve.tensor_tensor(flat(Xg(ended)), flat(Xg(ended)), OUT[:], ALU.add).then_inc(y_ready, 1)
                if j == 1 and not last:
                    normalize(g + 1)

            groups(dve, step)

        @block.tensor
        def _(pe):
            def transposed_norm(g):
                pe.wait_ge(xn_ready, 2 * (g + 1))
                if not (isinstance(g, int) and g == 0):
                    pe.wait_ge(hT_ready, KT * g)
                for b in range(2):
                    for kt in range(KT):
                        col = 256 * kt + P * b
                        ins = pe.transpose(AUX[:, col:col + P], xn[:, b, P * kt:P * kt + P], ident[:])
                ins.then_inc(hT_done, 1)

            def second(u, g, j):
                if j == 0 and not (isinstance(g, int) and g == 0):
                    pe.wait_ge(y_ready, g)
                pe.wait_ge(act_lo_ready, u + 1)
                for b in range(2):
                    for i in range(2):
                        cut = slice(P * b, P * b + P)
                        ins = three_pass(pe, OUT[:, 256 * b:256 * b + 256], act_hi[j % 2][:, i, cut], act_lo[j % 2][:, i, cut],
                                         w2_hi[:, 2 * j + i, :], w2_lo[:, 2 * j + i, :],
                                         j == 0 and b == 0 and i == 0, j == J - 1 and b == 1 and i == 1, skip=True)
                ins.then_inc(fc2_done, 1)

            transposed_norm(0)
            pe.wait_ge(w_lo_out, 2)

            def step(g, j, first, last):
                u = J * g + j
                if j == 0 and not first:
                    second(u - 1, g - 1, J - 1)
                if j < J:
                    if j == 0:
                        pe.wait_ge(hT_lo_ready, g + 1)
                    if not (first and j < 2):
                        pe.wait_ge(gelu_ready, u - 1)
                    for i in range(2):
                        cut = slice(P * (2 * j + i), P * (2 * j + i) + P)
                        for kt in range(KT):
                            ins = three_pass(pe, FC1[j % 2][:, 256 * i:256 * i + 256], w1_hi[:, kt, cut], w1_lo[:, kt, cut],
                                             hT_hi[:, kt], hT_lo[:, kt], kt == 0, kt == KT - 1)
                    ins.then_inc(fc1_done, 1)
                if j > 0:
                    second(u - 1, g, j - 1)
                if j == 2 and not last:
                    transposed_norm(g + 1)

            groups(pe, step)


def sequence(nc, d, out):
    G = 8
    with ExitStack() as ctx:
        m = Mem(nc, ctx)
        X = m.sb("X", [P, 2 * G, 256])
        ident = m.sb("ident", [P, P])
        banks = [m.psum(f"bank{i}") for i in range(8)]
        attention0(nc, X, ident, banks, d, G)
        norm0(nc, X, banks, G)
        cross_layers(nc, X, ident, banks, d, G)
        mlp(nc, X, ident, banks, d, out, G)



def _layout(inputs):
    import numpy as np

    a = {k: np.asarray(v) for k, v in inputs.items()}
    l0, l1 = (lambda n: a[f"L0_xattn_{n}"]), (lambda n: a[f"L1_xattn_{n}"])
    both = lambda n: np.stack([l1(f"{n}1"), l1(f"{n}2")])
    heads = lambda t: t.reshape(2, 16, P).transpose(0, 2, 1)
    ln = np.stack([np.stack([l1(f"{n}_scale"), l1(f"{n}_offset")]) for n in ("ln1", "ln2", "ln_mlp")])
    ln = ln.reshape(3, 2, 2, P).transpose(0, 3, 1, 2)
    ctx = a["ctx_2048"]
    arrays = {
        "x": a["x"], "u": ctx, "ctxT": ctx.transpose(2, 0, 1).reshape(2, P, 16, P).transpose(1, 0, 2, 3),
        "wz0": l0("Wqkv0").T, "wz1": l0("Wqkv1").T, "wu0": l0("Winj0").T, "wu1": l0("Winj1").T, "wo0": l0("Wo").T,
        "rwb": l0("r_w_bias").reshape(8, P).T, "bo0": l0("bo").reshape(P, 1), "ident": np.eye(P, dtype=np.float32),
        "wq": both("wq"), "wk": both("wk"), "wv": both("wv"), "wo": both("wo"),
        "bq": heads(both("bq")), "bk": heads(both("bk")), "bias_k": heads(both("bias_k")), "bias_v": heads(both("bias_v")),
        "bv": both("bv"), "bo": both("bo"), "ln": ln[:2], "mln": ln[2],
        "w1": l1("w_fc1"), "b1": l1("b_fc1").reshape(8, P).T, "w2": l1("w_fc2"), "b2": l1("b_fc2").reshape(1, 256),
    }
    return {k: np.ascontiguousarray(v) for k, v in arrays.items()}


def kernel(**inputs):
    import concourse.bacc as bacc
    from concourse.bass_utils import run_bass_kernel_spmd

    nc = bacc.Bacc("TRN2", target_bir_lowering=False, num_devices=1)
    arrays = {f"in_{name}": a for name, a in _layout(inputs).items()}
    d = {name[3:]: nc.dram_tensor(name, a.shape, mybir.dt.from_np(a.dtype), kind="ExternalInput").ap()
         for name, a in arrays.items()}
    out = nc.dram_tensor("out", (16, P, 256), F32, kind="ExternalOutput").ap()
    sequence(nc, d, out)
    return run_bass_kernel_spmd(nc, [arrays], core_ids=[0]).results[0]["out"]
```

```python
from contextlib import ExitStack

import concourse.bass as bass
from concourse import mybir

F32 = mybir.dt.float32
F32R = mybir.dt.float32r
I32 = mybir.dt.int32
ALU = mybir.AluOpType
ACT = mybir.ActivationFunctionType
AX_X = mybir.AxisListType.X
EPS = 1e-5
P = 128


class Mem:

    def __init__(self, nc, stack):
        self.nc, self.stack = nc, stack

    def sb(self, name, shape, dt=F32):
        return self.stack.enter_context(self.nc.sbuf_tensor(name, shape, dt))

    def psum(self, name):
        return self.stack.enter_context(self.nc.psum_tensor(name, [P, 512], F32))

    def sem(self, name):
        return self.stack.enter_context(self.nc.semaphore(name))

    def sems(self, *names):
        return [self.sem(n) for n in names]


def wait(eng, sem, value):
    if isinstance(value, int) and value <= 0:
        return
    eng.wait_ge(sem, value)


def three_pass(eng, out, w_hi, w_lo, m_hi, m_lo, start, stop, skip=False):
    eng.matmul(out, w_hi, m_lo, start=start, stop=False, skip_group_check=skip)
    eng.matmul(out, w_lo, m_hi, start=False, stop=False, skip_group_check=skip)
    return eng.matmul(out, w_hi, m_hi, start=False, stop=stop, skip_group_check=skip)



def attention0(nc, X, ident, banks, d, G):
    PAIRS, L, C = 8, 256, 2
    NB = 2 * PAIRS
    with ExitStack() as local:
        m = Mem(nc, local)
        names = ("wz0", "wz1", "wu0", "wu1")
        w_hi = {n: m.sb(f"{n}_hi", [P, 3, 1024], F32R) for n in names}
        w_lo = {n: m.sb(f"{n}_lo", [P, 3, 1024], F32R) for n in names}
        wo_hi = m.sb("wo0_hi", [P, PAIRS, P], F32R)
        wo_lo = m.sb("wo0_lo", [P, PAIRS, P], F32R)
        stage = [m.sb(f"stage0_{i}", [P, 1024]) for i in range(2)]
        u_raw = m.sb("u_raw", [P, 2, L])
        z_hi, z_lo = m.sb("z_hi", [P, 2, L], F32R), m.sb("z_lo", [P, 2, L], F32R)
        u_hi, u_lo = m.sb("u_hi", [P, 2, L], F32R), m.sb("u_lo", [P, 2, L], F32R)
        q_sb = [[m.sb(f"q{x}{i}", [P, C, 2, P], F32R) for i in range(2)] for x in "AB"]
        k_hi = [[m.sb(f"kh{x}{i}", [P, C, 2, P], F32R) for i in range(2)] for x in "AB"]
        k_lo = [[m.sb(f"kl{x}{i}", [P, C, 2, P], F32R) for i in range(2)] for x in "AB"]
        v_sb = m.sb("v0", [P, 2, C, 1024])
        probs = [[m.sb(f"p{x}{i}", [P, 2, L]) for i in range(2)] for x in "AB"]
        probsT = [[m.sb(f"pT{x}{i}", [P, 2, L]) for i in range(2)] for x in "AB"]
        nmax = [m.sb(f"nmax{x}", [P, 2, 2]) for x in "AB"]
        sums = [m.sb(f"sums{x}", [P, 2, 2]) for x in "AB"]
        rsum = [m.sb(f"rsum{x}", [P, 2, 2]) for x in "AB"]
        av_f = m.sb("av0", [P, 2, L])
        av_hi, av_lo = m.sb("av0_hi", [P, 2, L], F32R), m.sb("av0_lo", [P, 2, L], F32R)
        rwb, bo = m.sb("rwb", [P, PAIRS]), m.sb("bo0", [P, 1])
        mean_w, eps = m.sb("mean_w", [P, P]), m.sb("eps0", [P, 1])
        sq, std, rstd = (m.sb(n, [P, 512]) for n in ("sq", "std", "rstd"))

        PJ, SB, TB, AVB, OUT = banks[0:2], banks[2:4], banks[4:6], banks[6], banks[7]

        (x_in, small_in, stage_in0, stage_in1, w_split_hi, w_split_lo, const,
         u_in, zu_hi, zu_lo, proj_done, q_hi_ready, q_ready, k_hi_ready, k_lo_ready, k_dup_in0, k_dup_in1, v_ready, s_done,
         max_done, exp_done, rec_done, normA_done, normB_done, t_done, ptA_ready, ptB_ready, av_done, avhi_ready,
         avlo_ready, w_done, out_done, mean_done, centred, squared, var_done, std_ready, rstd_ready,
         normed) = m.sems(*(f"a0_{n}" for n in (
             "x_in", "small_in", "stage_in0", "stage_in1", "w_split_hi", "w_split_lo", "const",
             "u_in", "zu_hi", "zu_lo", "proj_done", "q_hi_ready", "q_ready", "k_hi_ready", "k_lo_ready", "k_dup_in0", "k_dup_in1",
             "v_ready", "s_done", "max_done", "exp_done", "rec_done", "normA_done", "normB_done", "t_done", "ptA_ready",
             "ptB_ready", "av_done", "avhi_ready", "avlo_ready", "w_done", "out_done", "mean_done", "centred",
             "squared", "var_done", "std_ready", "rstd_ready", "normed")))
        stage_in, k_dup_in = [stage_in0, stage_in1], [k_dup_in0, k_dup_in1]

        pieces = [("qk", 0, "z"), ("qk", 0, "u"), ("v", 0, "z"), ("v", 0, "u"), ("qk", 1, "z"), ("qk", 1, "u"), ("wo", 0, ""),
                  ("v", 1, "z"), ("v", 1, "u"), ("qk", 2, "z"), ("qk", 2, "u"), ("qk", 3, "z"), ("qk", 3, "u")]
        AHEAD_PIECES = 4
        STEP_PIECES = {0: [4, 5], 1: [6], 2: [7, 8], 3: [9], 4: [10], 5: [11], 6: [12]}
        POOL_FROM = 6

        def piece(i, tables, wo):
            kind, c, src = pieces[i]
            st = stage[i % 2]
            if kind == "wo":
                return [("wo0", wo[:], st[:].rearrange("k (p o) -> k p o", o=P))]
            found = []
            for j in range(2):
                n = f"w{src}{j}"
                half = st[:, 512 * j:512 * j + 512]
                if kind == "qk":
                    found.append((n, tables[n][:, 0:2, 256 * c:256 * c + 256], half.rearrange("p (s n) -> p s n", s=2)))
                else:
                    found.append((n, tables[n][:, 2, 512 * c:512 * c + 512], half))
            return found

        def hi_piece(i):
            return piece(i, w_hi, wo_hi)

        def lo_piece(i):
            return piece(i, w_lo, wo_lo)

        ahead = [("k", 0, 0), ("q", 0, 0), ("k", 1, 0)] + [("v", c, 0) for c in range(3)]
        AHEAD = len(ahead)
        STAT = ("mean", "var")

        FURTHER = {(0, 0): ("v", 3, 0), (2, 0): ("mean", 0, 0), (2, 1): ("v", 4, 0), (3, 0): ("v", 5, 0), (3, 1): ("var", 0, 0),
                   (4, 0): ("v", 6, 0), (4, 1): ("v", 7, 0), (6, 1): ("v", 0, 1), (7, 0): ("v", 1, 1), (7, 1): ("v", 2, 1)}

        def jobs(p, b):
            kind, pair = ("q", p + 1) if b == 0 else ("k", p + 2)
            return [FURTHER[at] for at in ((p, b),) if at in FURTHER] + [(kind, pair % PAIRS, pair // PAIRS)]

        in_order = [job for i in range(NB) for job in jobs(*divmod(i, 2))]
        projections = [job for job in in_order if job[0] not in STAT]
        JOBS = len(projections)
        SPLIT_NEXT = (PAIRS - 2, 0)
        AFTER_SPLIT = (PAIRS - 2, 1)
        BEFORE_NEXT = sum(job[2] == 0 for job in projections)

        def step_jobs(g, p, b, first, last):
            start = sum(len(jobs(*divmod(i, 2))) for i in range(2 * p + b))
            for i, job in enumerate(jobs(p, b), start):
                if (last and job[2]) or (first and job[0] in STAT):
                    continue
                before = sum(j[0] not in STAT for j in in_order[:i])
                yield AHEAD + JOBS * g + before, (AHEAD + i) % 2, job, i

        def wait_emptied(eng, i, g, first):
            i -= 2
            if first and i >= 0 and in_order[i][0] in STAT:
                i -= 2
            if first and i < 0:
                if i < -AHEAD:
                    return
                (kind, which, _), further = ahead[AHEAD + i], 0
            else:
                kind, which, further = in_order[i]
                if i < 0:
                    further -= 1
            if kind == "v":
                eng.wait_ge(v_ready, 8 * (g + further) + which + 1)
            elif kind in STAT:
                eng.wait_ge(centred if kind == "mean" else std_ready, g)
            else:
                eng.wait_ge(q_ready if kind == "q" else k_lo_ready, PAIRS * (g + further) + which + 1)

        def groups(eng, step):
            for i in range(NB):
                step(0, *divmod(i, 2), True, False)
            with eng.Fori(1, G - 1) as g:
                for i in range(NB):
                    step(g, *divmod(i, 2), False, False)
            for i in range(NB):
                step(G - 1, *divmod(i, 2), False, True)

        def back(g, p, n):
            return (g, p - n) if p >= n else (g - 1, p - n + PAIRS)

        def qk_before(g, p, b, first, last):
            if p or b:
                found = [(g, *job[:3]) for job in step_jobs(g, *divmod(2 * p + b - 1, 2), first, last)]
            else:
                found = [] if first else [(g - 1, *job[:3]) for job in step_jobs(g - 1, PAIRS - 1, 1, False, False)]
            return [job for job in found if job[3][0] in "qk"]

        def further_jobs(g, p, b, first, last):
            return [job[:3] for job in step_jobs(g, p, b, first, last) if job[2][0] not in "qk"]

        def flat(t):
            return t.rearrange("p b l -> p (b l)")

        def chunks(t):
            return t[:].rearrange("p c b l -> p (c b l)")

        def Xg(g):
            return flat(X[:, bass.ds(2 * g, 2), :])

        block = local.enter_context(nc.Block())

        @block.sync
        def _(sp):
            def load_piece(i):
                kind, c, _ = pieces[i]
                for n, _, st in hi_piece(i):
                    if kind == "wo":
                        src = d["wo0"].rearrange("(p k) o -> k p o", k=P)
                    elif kind == "qk":
                        src = d[n].rearrange("p (s n) -> p s n", s=3)[:, 0:2, 256 * c:256 * c + 256]
                    else:
                        src = d[n][:, 2048 + 512 * c:2048 + 512 * c + 512]
                    sp.dma_start(st, src).then_inc(stage_in[i % 2], 16)

            load_piece(0)
            sp.dma_start(X[:, 0:2, :], d["x"][0:2].rearrange("b d l -> d b l")).then_inc(x_in, 16)
            load_piece(1)
            sp.dma_start(u_raw[:], d["u"][0:2].rearrange("b d l -> d b l")).then_inc(u_in, 16)
            sp.dma_start(rwb[:], d["rwb"]).then_inc(small_in, 16)
            sp.dma_start(bo[:], d["bo0"]).then_inc(small_in, 16)
            sp.dma_start(ident[:], d["ident"]).then_inc(small_in, 16)

            def stage_piece(i):
                sp.wait_ge(w_split_lo, i - 1)
                load_piece(i)

            def double_k(pair, p):
                par = p % 2
                for part, ready in ((k_hi, k_hi_ready), (k_lo, k_lo_ready)):
                    sp.wait_ge(ready, pair + 1)
                    for x in range(2):
                        own, other = slice(64 * x, 64 * x + 64), slice(64 * (1 - x), 64 * (1 - x) + 64)
                        sp.dma_start(part[x][par][other].bitcast(F32), part[x][par][own].bitcast(F32)).then_inc(k_dup_in[par], 16)

            for i in range(2, AHEAD_PIECES):
                stage_piece(i)
            double_k(0, 0)
            for i in (4, 5):
                stage_piece(i)
            double_k(1, 1)
            sp.dma_start(X[:, 2:, :], d["x"][2:].rearrange("b d l -> d b l")).then_inc(x_in, 16)

            def load_u(g):
                sp.wait_ge(zu_lo, 2 * g)
                sp.dma_start(u_raw[:], d["u"][bass.ds(2 * g, 2)].rearrange("b d l -> d b l")).then_inc(u_in, 16)

            def step(g, p, b, first, last):
                if (p, b) == (0, 0) and not last:
                    load_u(g + 1)
                if first:
                    for i in STEP_PIECES.get(2 * p + b, []):
                        if i + 2 < len(pieces):
                            stage_piece(i + 2)
                if b == 1 and not (last and p + 2 >= PAIRS):
                    double_k(PAIRS * g + p + 2, p + 2)

            groups(sp, step)

        @block.gpsimd
        def _(pool):
            pool.memset(mean_w[:], 1.0 / P).then_inc(const, 1)
            pool.memset(eps[:], EPS).then_inc(const, 1)

            def av_low(pair):
                pool.wait_ge(avhi_ready, pair + 1)
                pool.tensor_tensor(flat(av_lo[:]), flat(av_f[:]), flat(av_hi[:]).bitcast(F32), ALU.subtract).then_inc(avlo_ready, 1)

            def scale(g):
                pool.wait_ge(rstd_ready, 4 * (g + 1))
                pool.tensor_tensor(Xg(g), Xg(g), rstd[:], ALU.mult).then_inc(normed, 1)

            def step(g, p, b, first, last):
                u = NB * g + 2 * p + b
                if b == 0 and not (first and p < 2):
                    ag, ap = back(g, p, 2)
                    av_low(PAIRS * ag + ap)
                if first:
                    for i in STEP_PIECES.get(2 * p + b, []):
                        if i < POOL_FROM:
                            continue
                        pool.wait_ge(w_split_lo, i)
                        pool.wait_ge(w_split_hi, i + 1)
                        for (_, hi, st), (_, lo, _) in zip(hi_piece(i), lo_piece(i)):
                            ins = pool.tensor_tensor(lo, st, hi.bitcast(F32), ALU.subtract)
                        ins.then_inc(w_split_lo, 1)
                pool.wait_ge(rec_done, 2 * u + 2)
                factor = rsum[1][:, b, :].rearrange("p (i o) -> p i o", o=1).to_broadcast([P, 2, L])
                pool.tensor_tensor(probs[1][b][:], probs[1][b][:], factor, ALU.mult).then_inc(normB_done, 1)

                if not first and (p, b) == (5, 1):
                    scale(g - 1)

            groups(pool, step)
            av_low(PAIRS * G - 2)
            av_low(PAIRS * G - 1)
            scale(G - 1)

        @block.scalar
        def _(act):
            def split_hi(g):
                act.wait_ge(u_in, 16 * (g + 1))
                act.activation(z_hi[:], X[:, bass.ds(2 * g, 2), :], ACT.Copy).then_inc(zu_hi, 1)
                act.activation(u_hi[:], u_raw[:], ACT.Copy).then_inc(zu_hi, 1)

            def split_piece(i):
                dmas = sum(1 if pieces[j][0] == "wo" else 2 for j in range(i % 2, i + 1, 2))
                act.wait_ge(stage_in[i % 2], 16 * dmas)
                for _, hi, st in hi_piece(i):
                    ins = act.activation(hi, st, ACT.Copy)
                ins.then_inc(w_split_hi, 1)

            def evac(n, bank, job, g):
                kind, which, further = job
                if kind in STAT:
                    return
                if kind == "v":
                    gg = g + further
                    act.wait_ge(proj_done, n + 1)
                    wait(act, av_done, NB * gg - (NB // 2 if which < 4 else 0) if not (isinstance(gg, int) and gg == 0) else 0)
                    half_, rest = divmod(which, 4)
                    dst = v_sb[:, rest // 2, rest % 2, 512 * half_:512 * half_ + 512]
                    act.activation(dst, PJ[bank][:], ACT.Copy).then_inc(v_ready, 1)
                    return
                pair = PAIRS * (g + further) + which
                par = which % 2
                act.wait_ge(proj_done, n + 1)
                wait(act, s_done, 4 * (pair - 1))
                for x in range(2):
                    rows = slice(64 * x, 64 * x + 64)
                    if kind == "q":
                        ins = act.activation(chunks(q_sb[x][par])[rows], PJ[bank][rows], ACT.Identity,
                                             bias=rwb[rows, which:which + 1])
                    else:
                        ins = act.activation(chunks(k_hi[x][par])[rows], PJ[bank][rows], ACT.Copy, scale=0.125)
                ins.then_inc(q_hi_ready if kind == "q" else k_hi_ready, 1)

            def std_dev(g, bank):
                act.wait_ge(var_done, g + 1)
                wait(act, rstd_ready, 4 * g)
                act.activation(std[:], PJ[bank][:], ACT.Sqrt, bias=eps[:, 0:1]).then_inc(std_ready, 1)

            def square(g):
                act.wait_ge(centred, g + 1)
                wait(act, var_done, g)
                act.activation(sq[:], Xg(g), ACT.Square).then_inc(squared, 1)

            def pt_b(u, b):
                act.wait_ge(t_done, 2 * u + 2)
                wait(act, av_done, u - 1)
                act.activation(flat(probsT[1][b][:]), TB[1][:], ACT.Copy).then_inc(ptB_ready, 1)

            def av_high(pair):
                act.wait_ge(av_done, 2 * pair + 2)
                wait(act, w_done, pair)
                act.activation(flat(av_f[:]), AVB[:], ACT.Copy)
                act.activation(flat(av_hi[:]), AVB[:], ACT.Copy).then_inc(avhi_ready, 1)

            act.wait_ge(small_in, 48)
            act.wait_ge(const, 2)
            split_piece(0)
            act.wait_ge(x_in, 16)
            split_hi(0)
            split_piece(1)
            for n, job in enumerate(ahead):
                if n == 3:
                    split_piece(2)
                    split_piece(3)
                evac(n, n % 2, job, 0)

            def step(g, p, b, first, last):
                u = NB * g + 2 * p + b
                start = first and p == 0 and b == 0
                if not (first and p == 0):
                    pt_b(u - 2, b)
                if b == 0 and not (first and p < 2):
                    ag, ap = back(g, p, 2)
                    av_high(PAIRS * ag + ap)
                for jg, n, bank, job in qk_before(g, p, b, first, last):
                    evac(n, bank, job, jg)
                for x in range(2):
                    act.wait_ge(max_done, 2 * u + x + 1)
                    if not (first and p == 0):
                        act.wait_ge(t_done, 2 * (u - 2) + x + 1)
                    for it in range(2):
                        ins = act.activation(probs[x][b][:, it, :], SB[x][:, L * it:L * it + L], ACT.Exp,
                                             bias=nmax[x][:, b, it:it + 1], accum_out=sums[x][:, b, it:it + 1])
                    ins.then_inc(exp_done, 1)
                for n, bank, job in further_jobs(g, p, b, first, last):
                    if job[0] == "var":
                        std_dev(g - 1, bank)
                    evac(n, bank, job, g)
                if (p, b) == (2, 1) and not first:
                    square(g - 1)
                if (p, b) == SPLIT_NEXT and not last:
                    act.wait_ge(proj_done, AHEAD + JOBS * g + BEFORE_NEXT)
                    if first:
                        act.wait_ge(x_in, 32)
                    split_hi(g + 1)
                if first:
                    for i in STEP_PIECES.get(2 * p + b, []):
                        split_piece(i)

            groups(act, step)
            av_high(PAIRS * G - 2)
            pt_b(NB * G - 2, 0)
            pt_b(NB * G - 1, 1)
            av_high(PAIRS * G - 1)
            square(G - 1)
            std_dev(G - 1, 1)

        @block.vector
        def _(dve):
            def split_lo(g):
                dve.wait_ge(zu_hi, 2 * g + 2)
                dve.tensor_tensor(z_lo[:], X[:, bass.ds(2 * g, 2), :], z_hi[:].bitcast(F32), ALU.subtract).then_inc(zu_lo, 1)
                dve.tensor_tensor(u_lo[:], u_raw[:], u_hi[:].bitcast(F32), ALU.subtract).then_inc(zu_lo, 1)

            def split_piece(i):
                dve.wait_ge(w_split_hi, i + 1)
                for (_, hi, st), (_, lo, _) in zip(hi_piece(i), lo_piece(i)):
                    ins = dve.tensor_tensor(lo, st, hi.bitcast(F32), ALU.subtract)
                ins.then_inc(w_split_lo, 1)

            def evac(n, bank, job, g):
                kind, which, further = job
                if kind not in ("q", "k"):
                    return
                pair, par = PAIRS * (g + further) + which, which % 2
                dve.wait_ge(q_hi_ready if kind == "q" else k_hi_ready, pair + 1)
                for x in range(2):
                    rows = slice(64 * x, 64 * x + 64)
                    if kind == "q":
                        other = slice(64 * (1 - x), 64 * (1 - x) + 64)
                        q = chunks(q_sb[x][par])
                        ins = dve.scalar_tensor_tensor(q[other], PJ[bank][rows], rwb[rows, which:which + 1],
                                                       q[rows].bitcast(F32), ALU.add, ALU.subtract)
                    else:
                        ins = dve.scalar_tensor_tensor(chunks(k_lo[x][par])[rows], PJ[bank][rows], 0.125,
                                                       chunks(k_hi[x][par])[rows].bitcast(F32), ALU.mult, ALU.subtract)
                ins.then_inc(q_ready if kind == "q" else k_lo_ready, 1)

            def pt_a(u, b):
                dve.wait_ge(t_done, 2 * u + 1)
                wait(dve, av_done, u - 1)
                dve.tensor_copy(flat(probsT[0][b][:]), TB[0][:]).then_inc(ptA_ready, 1)

            def output(g):
                dve.wait_ge(w_done, PAIRS * (g + 1))
                dve.scalar_tensor_tensor(Xg(g), OUT[:], bo[:, 0:1], Xg(g), ALU.add, ALU.add).then_inc(out_done, 1)

            def centre(g, bank):
                dve.wait_ge(mean_done, g + 1)
                dve.tensor_tensor(Xg(g), Xg(g), PJ[bank][:], ALU.subtract).then_inc(centred, 1)

            def normalize(u, b):
                for x in range(2):
                    dve.wait_ge(exp_done, 2 * u + x + 1)
                    dve.reciprocal(rsum[x][:, b, :], sums[x][:, b, :]).then_inc(rec_done, 1)
                dve.wait_ge(rec_done, 2 * u + 1)
                for it in range(2):
                    row = probs[0][b][:, it, :]
                    ins = dve.tensor_scalar(row, row, rsum[0][:, b, it:it + 1], None, ALU.mult)
                ins.then_inc(normA_done, 1)

            def reciprocal_std(g, quarter):
                if quarter == 0:
                    dve.wait_ge(std_ready, g + 1)
                    wait(dve, normed, g)
                cut = slice(P * quarter, P * quarter + P)
                dve.reciprocal(rstd[:, cut], std[:, cut]).then_inc(rstd_ready, 1)

            def step(g, p, b, first, last):
                u = NB * g + 2 * p + b
                if not (first and p == 0):
                    pt_a(u - 2, b)
                for x in range(2):
                    dve.wait_ge(s_done, 2 * u + x + 1)
                    dve.tensor_reduce(nmax[x][:, b, :], SB[x][:].rearrange("p (i j) -> p i j", i=2), AX_X, ALU.max,
                                      negate=True).then_inc(max_done, 1)
                for jg, n, bank, job in qk_before(g, p, b, first, last):
                    evac(n, bank, job, jg)
                for n, bank, job in further_jobs(g, p, b, first, last):
                    if job[0] == "mean":
                        centre(g - 1, bank)
                normalize(u, b)
                if first:
                    for i in STEP_PIECES.get(2 * p + b, []):
                        if i < POOL_FROM:
                            split_piece(i)
                if (p, b) == SPLIT_NEXT and not last:
                    split_lo(g + 1)
                if not first:
                    if (p, b) == (1, 1):
                        output(g - 1)
                    if (4, 0) <= (p, b) <= (5, 1):
                        reciprocal_std(g - 1, 2 * p + b - 8)

            split_piece(0)
            dve.wait_ge(x_in, 16)
            split_lo(0)
            split_piece(1)
            for n, job in enumerate(ahead):
                if n == 3:
                    split_piece(2)
                    split_piece(3)
                evac(n, n % 2, job, 0)
            groups(dve, step)
            pt_a(NB * G - 2, 0)
            pt_a(NB * G - 1, 1)
            output(G - 1)
            centre(G - 1, 0)
            for quarter in range(4):
                reciprocal_std(G - 1, quarter)

        @block.tensor
        def _(pe):
            pe.wait_ge(small_in, 48)
            pe.wait_ge(const, 2)

            def mean(out, src, done):
                pe.matmul(out[:], mean_w[:], src, start=True, stop=True).then_inc(done, 1)

            def project(n, bank, job, i, g, first):
                kind, which, further = job
                if further or (isinstance(n, int) and n == 0):
                    pe.wait_ge(zu_lo, 2 * (g + further) + 2)
                if first and not further:
                    need = ("v", which // 4, "u") if kind == "v" else ("qk", which // 2, "u")
                    pe.wait_ge(w_split_lo, pieces.index(need) + 1)
                wait_emptied(pe, i, g, first)
                if kind == "mean":
                    pe.wait_ge(out_done, g)
                    mean(PJ[bank], Xg(g - 1), mean_done)
                    return
                if kind == "var":
                    pe.wait_ge(squared, g)
                    mean(PJ[bank], sq[:], var_done)
                    return
                if kind in "qk":
                    part, cut = (0 if kind == "q" else 1), slice(P * which, P * which + P)
                    for c in range(C):
                        out = PJ[bank][:, 256 * c:256 * c + 256]
                        pos = slice(P * c, P * c + P)
                        three_pass(pe, out, w_hi[f"wz{c}"][:, part, cut], w_lo[f"wz{c}"][:, part, cut],
                                   z_hi[:, :, pos], z_lo[:, :, pos], True, False)
                        ins = three_pass(pe, out, w_hi[f"wu{c}"][:, part, cut], w_lo[f"wu{c}"][:, part, cut],
                                         u_hi[:, :, pos], u_lo[:, :, pos], False, True)
                else:
                    half_, rest = divmod(which, 4)
                    b, c = divmod(rest, 2)
                    pos = slice(P * c, P * c + P)
                    cut = slice(512 * half_, 512 * half_ + 512)
                    three_pass(pe, PJ[bank][:], z_hi[:, b, pos], z_lo[:, b, pos],
                               w_hi[f"wz{c}"][:, 2, cut], w_lo[f"wz{c}"][:, 2, cut], True, False)
                    ins = three_pass(pe, PJ[bank][:], u_hi[:, b, pos], u_lo[:, b, pos],
                                     w_hi[f"wu{c}"][:, 2, cut], w_lo[f"wu{c}"][:, 2, cut], False, True)
                ins.then_inc(proj_done, 1)

            def scores(g, p, b, first):
                u = NB * g + 2 * p + b
                pair, par = PAIRS * g + p, p % 2
                pe.wait_ge(q_ready, pair + 1)
                pe.wait_ge(k_dup_in[par], 64 * (PAIRS // 2 * g + p // 2 + 1))
                for x in range(2):
                    if not (first and p == 0 and b == 0):
                        pe.wait_ge(exp_done, 2 * (u - 1) + x + 1)
                    for it in range(2):
                        out, q = SB[x][:, L * it:L * it + L], q_sb[x][par][:, it, b, :]
                        pe.matmul(out, q, k_lo[x][par][:, :, b, :], start=True, stop=False)
                        ins = pe.matmul(out, q, k_hi[x][par][:, :, b, :], start=False, stop=True)
                    ins.then_inc(s_done, 1)

            def transposes(u, b):
                for x in range(2):
                    pe.wait_ge((normA_done, normB_done)[x], u + 1)
                    wait(pe, (ptA_ready, ptB_ready)[x], u)
                    for jt in range(2):
                        for it in range(2):
                            ins = pe.transpose(TB[x][:, L * jt + P * it:L * jt + P * it + P],
                                               probs[x][b][:, it, P * jt:P * jt + P], ident[:])
                    ins.then_inc(t_done, 1)

            def weighted(g, p, b):
                u = NB * g + 2 * p + b
                pe.wait_ge(v_ready, 8 * g + (8 if p >= 4 else 4))
                pe.wait_ge(ptA_ready, u + 1)
                pe.wait_ge(ptB_ready, u + 1)
                if b == 0:
                    wait(pe, avhi_ready, PAIRS * g + p)
                for jt in range(2):
                    for x in range(2):
                        col = P * p + 64 * x
                        ins = pe.matmul(AVB[64 * x:64 * x + 64, L * b:L * b + L], v_sb[:, b, jt, col:col + 64],
                                        probsT[x][b][:, jt, :], start=(jt == 0), stop=(jt == 1))
                ins.then_inc(av_done, 1)

            def out_product(g, p, first):
                pe.wait_ge(avlo_ready, PAIRS * g + p + 1)
                if first:
                    pe.wait_ge(w_split_lo, pieces.index(("wo", 0, "")) + 1)
                if p == 0:
                    wait(pe, out_done, g)
                three_pass(pe, OUT[:], wo_hi[:, p, :], wo_lo[:, p, :], flat(av_hi[:]), flat(av_lo[:]),
                           p == 0, p == PAIRS - 1).then_inc(w_done, 1)

            def step(g, p, b, first, last):
                u = NB * g + 2 * p + b
                scores(g, p, b, first)
                found = list(step_jobs(g, p, b, first, last))
                early = 0 if (p, b) == AFTER_SPLIT else 1
                for n, bank, job, i in found[:early]:
                    project(n, bank, job, i, g, first)
                if not (first and p == 0 and b == 0):
                    transposes(u - 1, 1 - b)
                if not (first and p == 0):
                    weighted(*back(g, p, 1), b)
                for n, bank, job, i in found[early:]:
                    project(n, bank, job, i, g, first)
                if b == 0 and not (first and p < 2):
                    out_product(*back(g, p, 2), first)

            for n, job in enumerate(ahead):
                project(n, n % 2, job, n - AHEAD, 0, True)
            groups(pe, step)
            transposes(NB * G - 1, 1)
            weighted(G - 1, PAIRS - 1, 0)
            out_product(G - 1, PAIRS - 2, False)
            weighted(G - 1, PAIRS - 1, 1)
            out_product(G - 1, PAIRS - 1, False)
            pe.wait_ge(out_done, G)
            mean(PJ[0], Xg(G - 1), mean_done)
            pe.wait_ge(squared, G)
            mean(PJ[1], sq[:], var_done)



class NormedInput:

    BEFORE = (0, 2, 4, 5, 6) + tuple(range(7, 17))
    STAGES, CHAIN, KT = len(BEFORE), 16, 2

    def __init__(self, m, X, d):
        self.X, self.d = X, d
        self.stats, self.mv = m.sb("n_stats", [P, 2, 6]), m.sb("n_mv", [P, 2, 2])
        self.var, self.y, self.t = (m.sb(f"n_{n}", [P, 2]) for n in ("var", "y", "t"))
        self.waited = m.sb("n_waited", [P, 1])
        self.half = m.sb("n_half", [P, 2], I32)
        self.xn, self.hT = m.sb("xn", [P, 2, 256]), m.sb("hT", [P, 2, 256])
        self.hT_hi = [m.sb(f"hT_hi{i}", [P, 2, 256], F32R) for i in range(2)]
        self.hT_lo = [m.sb(f"hT_lo{i}", [P, 2, 256], F32R) for i in range(2)]
        self.ln_all = m.sb("ln_all", [P, 3, 4])
        self.ln = m.sb("ln", [P, 1, 4])
        (self.ln_in, self.ln_ready, self.chain, self.xn_ready, self.hT_done, self.hT_ready, self.hi_ready,
         self.lo_ready) = m.sems(*(f"n_{n}" for n in (
             "ln_in", "ln_ready", "chain", "xn_ready", "hT_done", "hT_ready", "hi_ready", "lo_ready")))

    def set_layer(self, dve, layer):
        dve.tensor_copy(self.ln[:], self.ln_all[:, bass.ds(layer, 1), :]).then_inc(self.ln_ready, 1)

    def stage(self, dve, k, n, g):
        Xg, base = self.X[:, bass.ds(2 * g, 2), :], self.CHAIN * n
        if k > 0:
            dve.wait_ge(self.chain, base + self.BEFORE[k])
        if k == 0:
            for b in range(2):
                dve.bn_stats(self.stats[:, b, :], Xg[:, b, :]).then_inc(self.chain, 1)
        elif k == 1:
            dve.memset(self.waited[:], 0.0)
            for b in range(2):
                dve.bn_aggr(self.mv[:, b, :], self.stats[:, b, :]).then_inc(self.chain, 1)
        elif k == 2:
            dve.tensor_scalar(self.var[:], self.mv[:, :, 1], EPS, None, ALU.add).then_inc(self.chain, 1)
        elif k == 3:
            dve.tensor_scalar(self.half[:], self.var[:].bitcast(I32), 1, None, ALU.logical_shift_right).then_inc(self.chain, 1)
        elif k == 4:
            dve.tensor_scalar(self.y[:].bitcast(I32), self.half[:], -1.0, float(0x5F3759DF), ALU.mult, ALU.add).then_inc(self.chain, 1)
        elif k == self.STAGES - 1:
            for b in range(2):
                dve.tensor_scalar(self.xn[:, b, :], Xg[:, b, :], self.mv[:, b, 0:1], self.y[:, b:b + 1],
                                  ALU.subtract, ALU.mult).then_inc(self.xn_ready, 1)
        elif k % 3 == 2:
            dve.tensor_tensor(self.t[:], self.y[:], self.y[:], ALU.mult).then_inc(self.chain, 1)
        elif k % 3 == 0:
            dve.scalar_tensor_tensor(self.t[:], self.t[:], -0.5, self.var[:], ALU.mult, ALU.mult).then_inc(self.chain, 1)
        else:
            dve.scalar_tensor_tensor(self.y[:], self.t[:], 1.5, self.y[:], ALU.add, ALU.mult).then_inc(self.chain, 1)

    def transpose(self, pe, n, bank, ident):
        pe.wait_ge(self.xn_ready, 2 * (n + 1))
        for b in range(2):
            for kt in range(self.KT):
                col = 256 * kt + P * b
                ins = pe.transpose(bank[:, col:col + P], self.xn[:, b, P * kt:P * kt + P], ident[:])
        ins.then_inc(self.hT_done, 1)

    def scale_offset(self, act, n, layer, bank):
        act.wait_ge(self.ln_ready, layer + 1)
        act.wait_ge(self.hT_done, n + 1)
        for kt in range(self.KT):
            act.activation(self.hT[:, kt, :], bank[:, 256 * kt:256 * kt + 256], ACT.Identity,
                           bias=self.ln[:, 0, 2 + kt:3 + kt], scale=self.ln[:, 0, kt:kt + 1]).then_inc(self.hT_ready, 1)

    def split_hi(self, act, n, par):
        act.wait_ge(self.hT_ready, self.KT * (n + 1))
        act.activation(self.hT_hi[par][:], self.hT[:], ACT.Copy).then_inc(self.hi_ready, 1)

    def split_lo(self, dve, n, par):
        dve.wait_ge(self.hi_ready, n + 1)
        dve.tensor_tensor(self.hT_lo[par][:], self.hT[:], self.hT_hi[par][:].bitcast(F32), ALU.subtract).then_inc(self.lo_ready, 1)



def cross_layers(nc, X, ident, banks, d, G, norm):
    H, KT, LAYERS = 16, 2, 2
    SCALE = P ** -0.5
    BO_ROW, PER = 16, 5
    BQ, BK, BIAS_K, BIAS_V, BV = range(5)
    QK_HEADS, V_HEADS, O_HEADS = 2, 4, 4

    def bias_row(h):
        return 32 * (h % 4) + h // 4

    with ExitStack() as local:
        m = Mem(nc, local)
        w_hi = {n: m.sb(f"{n}_hi", [P, KT, 2048], F32R) for n in ("wq", "wk", "wv")}
        w_lo = {n: m.sb(f"{n}_lo", [P, KT, 2048], F32R) for n in ("wq", "wk", "wv")}
        w_hi["wo"], w_lo["wo"] = m.sb("wo_hi", [P, H, 256], F32R), m.sb("wo_lo", [P, H, 256], F32R)
        stage = [m.sb(f"stage1_{i}", [P, 1024]) for i in range(2)]
        params_all = m.sb("params_all", [P, LAYERS, 5 * H])
        params = m.sb("params", [P, 1, 5 * H])
        diag = m.sb("diag", [P, 4, 4 * PER])
        tail_w = m.sb("tail_w", [P, 256])
        ctx_raw = m.sb("ctx_raw", [P, KT, 2, P])
        ctx_hi = [m.sb(f"ctx_hi{i}", [P, KT, 2, P], F32R) for i in range(2)]
        ctx_lo = [m.sb(f"ctx_lo{i}", [P, KT, 2, P], F32R) for i in range(2)]
        q_sb = [m.sb(f"cq{i}", [P, 2, P]) for i in range(2)]
        k_sb = [m.sb(f"ck{i}", [P, 2, P + 1]) for i in range(2)]
        v_sb = m.sb("cv", [P, 2, 2048])
        probs = [m.sb(f"cp{i}", [P, 2, P + 1]) for i in range(2)]
        nmax, sums, rsum = (m.sb(f"c_{n}", [P, 2, 2]) for n in ("nmax", "sums", "rsum"))
        probsT = m.sb("cpT", [P, 2, P])
        wb, wbT = m.sb("wb", [P, 2, P]), m.sb("wbT", [P, 2, P])
        av_hi, av_lo = m.sb("cav_hi", [P, 2, P], F32R), m.sb("cav_lo", [P, 2, P], F32R)
        one = m.sb("one", [P, 1])

        PJ, SB, TB, AVB, AUX, OUT = banks[0:2], banks[2:4], banks[4], banks[5], banks[6], banks[7]
        (cleared, small_in, bo_in, stage_in0, stage_in1, w_hi_out, w_lo_out, bqs_ready, diag_ready, tail_w_done,
         tail_w_ready, ctx_in, ctx_hi_ready, ctx_lo_ready, proj_done, qk_ready, bias_k_ready,
         v_ready, s_done, max_done, exp_done, rec_done, norm_done, t_done, pT_ready, wbT_ready, av_done,
         avhi_ready, avlo_ready, o_done, out_added, tail_done, tail_added, layer_open) = m.sems(*(f"c_{n}" for n in (
             "cleared", "small_in", "bo_in", "stage_in0", "stage_in1", "w_hi_out", "w_lo_out", "bqs_ready", "diag_ready",
             "tail_w_done", "tail_w_ready", "ctx_in", "ctx_hi_ready", "ctx_lo_ready", "proj_done", "qk_ready",
             "bias_k_ready", "v_ready", "s_done", "max_done", "exp_done", "rec_done", "norm_done", "t_done",
             "pT_ready", "wbT_ready", "av_done", "avhi_ready", "avlo_ready", "o_done", "out_added", "tail_done",
             "tail_added", "layer_open")))
        stage_in = [stage_in0, stage_in1]

        pieces = [("qk", 0), ("v", 0), ("qk", 1), ("o", 0), ("v", 1), ("qk", 2), ("qk", 3), ("o", 1), ("qk", 4), ("v", 2),
                  ("qk", 5), ("o", 2), ("qk", 6), ("v", 3), ("qk", 7), ("o", 3)]
        NPIECE = len(pieces)

        def piece(i, tables):
            kind, c = pieces[i % NPIECE]
            st = stage[i % 2]
            if kind == "qk":
                cut = slice(256 * c, 256 * c + 256)
                return [(tables["wq"][:, :, cut], st[:, 0:512].rearrange("p (t n) -> p t n", t=KT)),
                        (tables["wk"][:, :, cut], st[:, 512:1024].rearrange("p (t n) -> p t n", t=KT))]
            if kind == "v":
                return [(tables["wv"][:, :, 512 * c:512 * c + 512], st[:].rearrange("p (t n) -> p t n", t=KT))]
            return [(tables["wo"][:, 4 * c:4 * c + 4, :], st[:].rearrange("p (h n) -> p h n", h=O_HEADS))]

        def piece_count(ly, i):
            return NPIECE * ly + i + 1

        V_CHUNK = {0: 0, 1: 1, 4: 2, 5: 3, 8: 4, 9: 5, 12: 6, 13: 7}

        def jobs(h):
            return [("qk", h)] * (h < H) + [("v", V_CHUNK[i]) for i in (h,) if i in V_CHUNK]

        in_order = [job for h in range(H) for job in jobs(h)]
        JOBS = len(in_order)

        def step_jobs(h):
            return enumerate(jobs(h), sum(len(jobs(i)) for i in range(h)))

        def wait_emptied(eng, gg, i, first):
            if i < 0 and first:
                return
            kind, which = in_order[i]
            n = gg - 1 if i < 0 else gg
            if kind == "qk":
                eng.wait_ge(qk_ready, 2 * (H * n + which) + 2)
            else:
                eng.wait_ge(v_ready, 8 * n + which + 1)

        def layers(eng, begin, step, finish):
            with eng.Fori(0, LAYERS) as ly:
                begin(ly)
                for h in range(H):
                    step(ly, 0, 0, h, True, False)
                with eng.Fori(0, (G - 2) // 2) as t:
                    for i in range(2):
                        for h in range(H):
                            step(ly, 2 * t + (1 + i), (1 + i) % 2, h, False, False)
                for h in range(H + 4):
                    step(ly, G - 1, 1, h, False, True)
                finish(ly)

        def unit(ly, g, h, lag, first):
            h -= lag
            if (h < 0 and first) or h >= H:
                return None
            return H * (G * ly + g) + h, h % H

        def ends_group(g, h, at, first, last):
            if h == at and not first:
                return g - 1
            if h == H + at:
                return g
            return None

        NORM_TRANSPOSE, NORM_SCALE, SPLIT_HI, SPLIT_LO = 8, 9, 10, 11

        block = local.enter_context(nc.Block())

        @block.sync
        def _(sp):
            def load_ctx(g):
                sp.dma_start(ctx_raw[:], d["ctxT"][:, :, bass.ds(2 * g, 2), :]).then_inc(ctx_in, 16)

            def load_piece(i, layer):
                kind, c = pieces[i % NPIECE]
                at = bass.ds(layer, 1)
                ready = stage_in[i % 2]
                if kind == "o":
                    src = d["wo"][at].rearrange("a (h k) o -> k (a h) o", k=P)[:, 4 * c:4 * c + 4, :]
                    sp.dma_start(piece(i, w_hi)[0][1], src).then_inc(ready, 16)
                    return
                width, names = (512, ("wv",)) if kind == "v" else (256, ("wq", "wk"))
                for n, (_, st) in zip(names, piece(i, w_hi)):
                    src = d[n][at].rearrange("a (t p) n -> p (a t) n", p=P)[:, :, width * c:width * c + width]
                    sp.dma_start(st, src).then_inc(ready, 16)

            load_piece(0, 0)
            load_piece(1, 0)
            sp.dma_start(norm.ln_all[:], d["ln"].rearrange("p l i k -> p l (i k)")).then_inc(norm.ln_in, 16)
            load_ctx(0)
            sp.dma_start(params_all[:], d["params"].rearrange("p l n h -> p l (n h)")).then_inc(small_in, 16)
            sp.wait_ge(cleared, 2)
            with sp.Fori(0, LAYERS) as ly:
                other = ly * -1 + 1
                sp.wait_ge(ctx_lo_ready, G * ly + 1)
                for i in range(2, NPIECE + 2):
                    sp.wait_ge(w_lo_out, piece_count(ly, i - 2))
                    if i == 3:
                        load_ctx(1)
                    load_piece(i, ly if i < NPIECE else other)
                    if i == 2:
                        sp.wait_ge(layer_open, ly + 1)
                        sp.dma_start(tail_w[BO_ROW:BO_ROW + 1, :], d["bo"][bass.ds(ly, 1)]).then_inc(bo_in, 16)
                with sp.Fori(2, G) as g:
                    sp.wait_ge(ctx_lo_ready, G * ly + g)
                    load_ctx(g)
                sp.wait_ge(ctx_lo_ready, G * ly + G)
                load_ctx(0)

        @block.gpsimd
        def _(pool):
            pool.memset(tail_w[:], 0.0).then_inc(cleared, 1)
            pool.memset(diag[:], 0.0).then_inc(cleared, 1)
            pool.memset(wb[:], 0.0).then_inc(cleared, 1)
            pool.wait_ge(cleared, 3)
            for row in [BO_ROW] + [32 * c + 4 for c in range(4)]:
                pool.memset(wb[:, :, row:row + 1], 1.0).then_inc(cleared, 1)
            pool.memset(one[:], 1.0).then_inc(cleared, 1)
            pool.wait_ge(cleared, 9)

            def begin(ly):
                pool.wait_ge(layer_open, ly + 1)

            def step(ly, g, par, h, first, last):
                if h >= H:
                    return
                n, _ = unit(ly, g, h, 0, first)
                if not (first and h < 2):
                    pool.wait_ge(s_done, n - 1)
                for b in range(2):
                    ins = pool.tensor_tensor(k_sb[h % 2][:, b, P:P + 1], params[:, 0, H * BIAS_K + h:H * BIAS_K + h + 1], one[:], ALU.mult)
                ins.then_inc(bias_k_ready, 1)

            layers(pool, begin, step, lambda ly: None)

        @block.scalar
        def _(act):
            def split_ctx(n, par):
                act.wait_ge(ctx_in, 16 * (n + 1))
                act.activation(ctx_hi[par][:], ctx_raw[:], ACT.Copy).then_inc(ctx_hi_ready, 1)

            def split_piece(ly, i):
                dmas = 2 if pieces[i % NPIECE][0] == "qk" else 1
                per_layer = sum(2 if k == "qk" else 1 for k, _ in pieces[i % 2::2])
                before = sum(2 if pieces[j % NPIECE][0] == "qk" else 1 for j in range(i % 2, i, 2))
                act.wait_ge(stage_in[i % 2], 16 * (per_layer * ly + before + dmas))
                for dst, st in piece(i, w_hi):
                    ins = act.activation(dst, st, ACT.Copy)
                ins.then_inc(w_hi_out, 1)

            act.wait_ge(small_in, 16)
            q_bias = params_all[:, :, 0:H]
            act.mul(q_bias, q_bias, SCALE).then_inc(bqs_ready, 1)
            split_piece(0, 0)
            norm.scale_offset(act, 0, 0, AUX)
            norm.split_hi(act, 0, 0)
            split_ctx(0, 0)
            split_piece(0, 1)

            def begin(ly):
                act.wait_ge(layer_open, ly + 1)

            def step(ly, g, par, h, first, last):
                n = G * ly + g
                if first and h + 2 < NPIECE:
                    split_piece(ly, h + 2)
                if last and h in (H, H + 1):
                    split_piece(ly, h)
                if found := unit(ly, g, h, 1, first):
                    u, head = found
                    s = head % 2
                    act.wait_ge(max_done, u + 1)
                    if not (first and h < 3):
                        act.wait_ge(t_done, u - 1)
                    for b in range(2):
                        ins = act.activation(probs[s][:, b, :], SB[s][:, 256 * b:256 * b + P + 1], ACT.Exp,
                                             bias=nmax[:, s, b:b + 1], accum_out=sums[:, s, b:b + 1])
                    ins.then_inc(exp_done, 1)
                for i, (kind, which) in step_jobs(h):
                    if kind == "qk":
                        u, _ = unit(ly, g, h, 0, first)
                        act.wait_ge(proj_done, JOBS * n + i + 1)
                        if not (first and h < 2):
                            act.wait_ge(s_done, u - 1)
                        act.activation(q_sb[h % 2][:], PJ[i % 2][:, 0:256].rearrange("p (b t) -> p b t", b=2), ACT.Identity,
                                       bias=params[:, 0, H * BQ + h:H * BQ + h + 1], scale=SCALE).then_inc(qk_ready, 1)
                        act.activation(k_sb[h % 2][:, :, 0:P], PJ[i % 2][:, 256:512].rearrange("p (b t) -> p b t", b=2),
                                       ACT.Identity, bias=params[:, 0, H * BK + h:H * BK + h + 1]).then_inc(qk_ready, 1)
                if found := unit(ly, g, h, 2, first):
                    u, _ = found
                    act.wait_ge(av_done, u + 1)
                    if not (first and h < 3):
                        act.wait_ge(o_done, u)
                    act.activation(av_hi[:], AVB[:, 0:256].rearrange("p (b t) -> p b t", b=2), ACT.Copy).then_inc(avhi_ready, 1)
                if h == NORM_SCALE:
                    norm.scale_offset(act, n + 1, ly + int(last), AUX)
                if h == SPLIT_HI:
                    norm.split_hi(act, n + 1, 1 - par)
                    split_ctx(n + 1, 1 - par)

            layers(act, begin, step, lambda ly: None)

        @block.vector
        def _(dve):
            def split_ctx(n, par):
                dve.wait_ge(ctx_hi_ready, n + 1)
                dve.tensor_tensor(ctx_lo[par][:], ctx_raw[:], ctx_hi[par][:].bitcast(F32), ALU.subtract).then_inc(ctx_lo_ready, 1)

            def split_piece(ly, i):
                dve.wait_ge(w_hi_out, piece_count(ly, i))
                for (hi, st), (lo, _) in zip(piece(i, w_hi), piece(i, w_lo)):
                    ins = dve.tensor_tensor(lo, st, hi.bitcast(F32), ALU.subtract)
                ins.then_inc(w_lo_out, 1)

            def flat(g):
                return X[:, bass.ds(2 * g, 2), :].rearrange("p b l -> p (b l)")

            for k in range(norm.STAGES):
                norm.stage(dve, k, 0, 0)
            dve.wait_ge(norm.ln_in, 16)
            norm.set_layer(dve, 0)
            split_piece(0, 0)
            norm.split_lo(dve, 0, 0)
            split_ctx(0, 0)
            split_piece(0, 1)
            dve.wait_ge(small_in, 16)
            dve.wait_ge(bqs_ready, 1)
            dve.wait_ge(cleared, 2)

            def begin(ly):
                dve.tensor_copy(params[:], params_all[:, bass.ds(ly, 1), :]).then_inc(layer_open, 1)
                dve.wait_ge(layer_open, ly + 1)
                by_head = lambda n: params[:, 0, H * n:H * n + H].rearrange("p (j c) -> p c j", c=4)
                dve.tensor_tensor(diag[:, :, 0:(PER + 1) * 3 + 1:PER + 1], by_head(BIAS_V), by_head(BV), ALU.subtract).then_inc(diag_ready, 1)
                dve.tensor_copy(diag[:, :, PER - 1:4 * PER:PER], by_head(BV)).then_inc(diag_ready, 1)

            def step(ly, g, par, h, first, last):
                n = G * ly + g
                if last and h == 0:
                    norm.set_layer(dve, ly + 1)
                if 2 * h < norm.STAGES:
                    norm.stage(dve, 2 * h, n + 1, 0 if last else g + 1)
                if (ended := ends_group(g, h, 3, first, last)) is not None:
                    dve.wait_ge(o_done, H * (G * ly + ended + 1))
                    dve.tensor_tensor(flat(ended), flat(ended), OUT[:], ALU.add).then_inc(out_added, 1)
                if found := unit(ly, g, h, 1, first):
                    u, head = found
                    s = head % 2
                    dve.wait_ge(s_done, u + 1)
                    dve.tensor_reduce(nmax[:, s, :], SB[s][:].rearrange("p (b t) -> p b t", b=2)[:, :, 0:P + 1], AX_X,
                                      ALU.max, negate=True).then_inc(max_done, 1)
                if found := unit(ly, g, h, 2, first):
                    u, head = found
                    dve.wait_ge(t_done, u + 1)
                    if not (first and h < 3):
                        dve.wait_ge(av_done, u)
                    dve.tensor_copy(probsT[:], TB[:, 0:256].rearrange("p (b t) -> p b t", b=2)).then_inc(pT_ready, 1)
                    if head == H - 1:
                        dve.tensor_copy(wbT[:], TB[:, 256:512].rearrange("p (b t) -> p b t", b=2)).then_inc(wbT_ready, 1)
                if found := unit(ly, g, h, 1, first):
                    u, head = found
                    s = head % 2
                    dve.wait_ge(exp_done, u + 1)
                    dve.reciprocal(rsum[:, s, :], sums[:, s, :]).then_inc(rec_done, 1)
                    if 2 * h + 1 < norm.STAGES:
                        norm.stage(dve, 2 * h + 1, n + 1, 0 if last else g + 1)
                    dve.wait_ge(rec_done, u + 1)
                    if head == 0 and not first:
                        dve.wait_ge(t_done, u)
                    for b in range(2):
                        dve.tensor_scalar(probs[s][:, b, 0:P], probs[s][:, b, 0:P], rsum[:, s, b:b + 1], None, ALU.mult)
                    col = bias_row(head)
                    dve.tensor_tensor(wb[:, :, col:col + 1], probs[s][:, :, P:P + 1], rsum[:, s, :].rearrange("p (b o) -> p b o", o=1),
                                      ALU.mult).then_inc(norm_done, 1)
                elif 2 * h + 1 < norm.STAGES:
                    norm.stage(dve, 2 * h + 1, n + 1, 0 if last else g + 1)
                if first and h + 2 < NPIECE:
                    split_piece(ly, h + 2)
                if last and h in (H, H + 1):
                    split_piece(ly, h)
                for i, (kind, c) in step_jobs(h):
                    if kind == "v":
                        dve.wait_ge(proj_done, JOBS * n + i + 1)
                        if not first:
                            dve.wait_ge(av_done, H * (n - 1) + 4 * (c // 2) + 4)
                        cut = slice(512 * (c // 2), 512 * (c // 2) + 512)
                        dve.tensor_copy(v_sb[:, c % 2, cut], PJ[i % 2][:]).then_inc(v_ready, 1)
                if found := unit(ly, g, h, 2, first):
                    u, _ = found
                    dve.wait_ge(avhi_ready, u + 1)
                    dve.tensor_tensor(av_lo[:], AVB[:, 0:256].rearrange("p (b t) -> p b t", b=2), av_hi[:].bitcast(F32),
                                      ALU.subtract).then_inc(avlo_ready, 1)
                if (ended := ends_group(g, h, 3, first, last)) is not None:
                    dve.wait_ge(tail_done, G * ly + ended + 1)
                    dve.wait_ge(out_added, G * ly + ended + 1)
                    dve.tensor_tensor(flat(ended), flat(ended), AUX[:], ALU.add).then_inc(tail_added, 1)
                if h == SPLIT_LO:
                    norm.split_lo(dve, n + 1, 1 - par)
                    split_ctx(n + 1, 1 - par)
                if first and h == H - 1:
                    dve.wait_ge(tail_w_done, ly + 1)
                    for c in range(4):
                        ins = dve.tensor_copy(tail_w[32 * c:32 * c + PER, :], AUX[32 * c:32 * c + PER, 0:256])
                    ins.then_inc(tail_w_ready, 1)

            def finish(ly):
                dve.wait_ge(tail_added, G * (ly + 1))

            layers(dve, begin, step, finish)

        @block.tensor
        def _(pe):
            def project(ly, n, par, i, kind, which, first):
                if (kind, which) == ("qk", 0):
                    pe.wait_ge(norm.lo_ready, n + 1)
                    pe.wait_ge(ctx_lo_ready, n + 1)
                if first:
                    used = ("qk", which // QK_HEADS) if kind == "qk" else ("v", which // 2)
                    pe.wait_ge(w_lo_out, piece_count(ly, pieces.index(used)))
                wait_emptied(pe, n, i - 2, first)
                bank = PJ[i % 2]
                if kind == "qk":
                    cut = slice(P * which, P * which + P)
                    for j, (w, hi, lo) in enumerate((("wq", norm.hT_hi[par], norm.hT_lo[par]), ("wk", ctx_hi[par], ctx_lo[par]))):
                        out = bank[:, 256 * j:256 * j + 256]
                        for kt in range(KT):
                            ins = three_pass(pe, out, w_hi[w][:, kt, cut], w_lo[w][:, kt, cut],
                                             hi[:, kt], lo[:, kt], kt == 0, kt == KT - 1)
                else:
                    b = which % 2
                    cut = slice(512 * (which // 2), 512 * (which // 2) + 512)
                    for kt in range(KT):
                        ins = three_pass(pe, bank[:], ctx_hi[par][:, kt, b, :], ctx_lo[par][:, kt, b, :],
                                         w_hi["wv"][:, kt, cut], w_lo["wv"][:, kt, cut], kt == 0, kt == KT - 1)
                ins.then_inc(proj_done, 1)

            def tail_weights(ly):
                pe.wait_ge(diag_ready, 2 * (ly + 1))
                pe.wait_ge(norm.hT_ready, KT * (G * ly + 2))
                for j in range(4):
                    for c in range(4):
                        for w in (w_hi, w_lo):
                            ins = pe.matmul(AUX[32 * c:32 * c + PER, 0:256], diag[:, c, PER * j:PER * j + PER],
                                            w["wo"][:, 4 * j + c, :].bitcast(F32), start=(j == 0 and w is w_hi),
                                            stop=(j == 3 and w is w_lo))
                ins.then_inc(tail_w_done, 1)

            norm.transpose(pe, 0, AUX, ident)

            def step(ly, g, par, h, first, last):
                n = G * ly + g
                if found := unit(ly, g, h, 1, first):
                    u, head = found
                    s = head % 2
                    pe.wait_ge(qk_ready, 2 * u + 2)
                    pe.wait_ge(bias_k_ready, u + 1)
                    if not (first and h < 3):
                        pe.wait_ge(exp_done, u - 1)
                    for b in range(2):
                        ins = pe.matmul(SB[s][:, 256 * b:256 * b + P + 1], q_sb[s][:, b, :], k_sb[s][:, b, :],
                                        start=True, stop=True)
                    ins.then_inc(s_done, 1)
                if found := unit(ly, g, h, 2, first):
                    u, head = found
                    s = head % 2
                    pe.wait_ge(norm_done, u + 1)
                    if not (first and h < 3):
                        pe.wait_ge(pT_ready, u)
                    if head == 0 and not first:
                        pe.wait_ge(wbT_ready, n)
                    for b in range(2):
                        ins = pe.transpose(TB[:, P * b:P * b + P], probs[s][:, b, 0:P], ident[:])
                    if head == H - 1:
                        for b in range(2):
                            ins = pe.transpose(TB[:, 256 + P * b:256 + P * b + P], wb[:, b, :], ident[:])
                    ins.then_inc(t_done, 1)
                if (ended := ends_group(g, h, 3, first, last)) is not None:
                    e = G * ly + ended
                    pe.wait_ge(wbT_ready, e + 1)
                    pe.wait_ge(tail_w_ready, ly + 1)
                    pe.wait_ge(bo_in, 16 * (ly + 1))
                    pe.wait_ge(norm.hT_ready, KT * (e + 2))
                    for b in range(2):
                        ins = pe.matmul(AUX[:, 256 * b:256 * b + 256], wbT[:, b, :], tail_w[:], start=True, stop=True)
                    ins.then_inc(tail_done, 1)
                for i, (kind, which) in step_jobs(h):
                    project(ly, n, par, i, kind, which, first)
                if found := unit(ly, g, h, 2, first):
                    u, head = found
                    pe.wait_ge(pT_ready, u + 1)
                    pe.wait_ge(v_ready, 8 * (n - (1 if h < 2 else 0)) + 2 * (head // 4) + 2)
                    if not (first and h < 3):
                        pe.wait_ge(avlo_ready, u)
                    for b in range(2):
                        ins = pe.matmul(AVB[:, P * b:P * b + P], v_sb[:, b, P * head:P * head + P], probsT[:, b, :],
                                        start=True, stop=True)
                    ins.then_inc(av_done, 1)
                if found := unit(ly, g, h, 3, first):
                    u, head = found
                    pe.wait_ge(avlo_ready, u + 1)
                    if first:
                        pe.wait_ge(w_lo_out, piece_count(ly, pieces.index(("o", head // O_HEADS))))
                    if head == 0 and first:
                        pe.wait_ge(layer_open, ly + 1)
                    elif head == 0:
                        pe.wait_ge(out_added, n)
                    for b in range(2):
                        ins = three_pass(pe, OUT[:, 256 * b:256 * b + 256], av_hi[:, b, :], av_lo[:, b, :],
                                         w_hi["wo"][:, head, :], w_lo["wo"][:, head, :],
                                         head == 0 and b == 0, head == H - 1 and b == 1, skip=True)
                    ins.then_inc(o_done, 1)
                if h == NORM_TRANSPOSE:
                    if not first:
                        pe.wait_ge(tail_added, n)
                    norm.transpose(pe, n + 1, AUX, ident)
                if first and h == H - 1:
                    tail_weights(ly)

            layers(pe, lambda ly: None, step, lambda ly: None)



def mlp(nc, X, ident, banks, d, out, G, norm):
    KT, F, J = 2, 1024, 4
    N0 = 2 * G
    LAG = 2
    with ExitStack() as local:
        m = Mem(nc, local)
        w1_raw, w2_raw = m.sb("w1_raw", [P, KT, F]), m.sb("w2_raw", [P, 8, 256])
        w1_hi, w1_lo = m.sb("w1_hi", [P, KT, F], F32R), m.sb("w1_lo", [P, KT, F], F32R)
        w2_hi, w2_lo = m.sb("w2_hi", [P, 8, 256], F32R), m.sb("w2_lo", [P, 8, 256], F32R)
        b1, b2 = m.sb("b1", [P, 8]), m.sb("b2", [P, 2, 256])
        act_f = [m.sb(f"gelu{i}", [P, 2, 256]) for i in range(J)]
        act_hi = [m.sb(f"gelu_hi{i}", [P, 2, 256], F32R) for i in range(J)]
        act_lo = [m.sb(f"gelu_lo{i}", [P, 2, 256], F32R) for i in range(J)]
        FC1, AUX, OUT = banks[0:2], banks[2], banks[3]
        (small_in, w_hi_out, w_lo_out, fc1_done, gelu_ready, act_hi_ready, act_lo_ready, b2_added, fc2_done, y_ready,
         stored) = m.sems(*(f"m_{n}" for n in (
             "small_in", "w_hi_out", "w_lo_out", "fc1_done", "gelu_ready", "act_hi_ready", "act_lo_ready", "b2_added",
             "fc2_done", "y_ready", "stored")))
        w1_in, w2_in = ([m.sem(f"m_{w}_in{j}") for j in range(J)] for w in ("w1", "w2"))

        pieces = []
        for j in range(J):
            cut, rows = slice(256 * j, 256 * j + 256), slice(2 * j, 2 * j + 2)
            pieces.append((w1_in[j], w1_raw[:, :, cut], w1_hi[:, :, cut], w1_lo[:, :, cut]))
            pieces.append((w2_in[j], w2_raw[:, rows], w2_hi[:, rows], w2_lo[:, rows]))
        AHEAD = 3

        def step_pieces(j):
            return range(AHEAD + 2 * j, min(AHEAD + 2 * j + 2, 2 * J))

        def groups(eng, step):
            for j in range(J):
                step(0, 0, j, True, False)
            with eng.Fori(0, (G - 2) // 2) as t:
                for i in range(2):
                    for j in range(J):
                        step(2 * t + (1 + i), (1 + i) % 2, j, False, False)
            for j in range(J + LAG):
                step(G - 1, 1, j, False, True)

        def flat(t):
            return t.rearrange("p b l -> p (b l)")

        def Xg(g):
            return X[:, bass.ds(2 * g, 2), :]

        block = local.enter_context(nc.Block())

        @block.sync
        def _(sp):
            w1, w2 = d["w1"].rearrange("(t p) f -> p t f", p=P), d["w2"].rearrange("(t p) o -> p t o", p=P)
            sp.dma_start(w1_raw[:, :, 0:256], w1[:, :, 0:256]).then_inc(w1_in[0], 16)
            sp.dma_start(b1[:], d["b1"]).then_inc(small_in, 16)
            sp.dma_start(w2_raw[:, 0:2], w2[:, 0:2]).then_inc(w2_in[0], 16)
            for b in range(2):
                sp.dma_start(b2[:, b, :], d["b2"].to_broadcast([P, 256])).then_inc(small_in, 16)
            for j in range(1, J):
                sp.dma_start(w1_raw[:, :, 256 * j:256 * j + 256], w1[:, :, 256 * j:256 * j + 256]).then_inc(w1_in[j], 16)
                sp.dma_start(w2_raw[:, 2 * j:2 * j + 2], w2[:, 2 * j:2 * j + 2]).then_inc(w2_in[j], 16)
            with sp.Fori(0, G) as g:
                sp.wait_ge(y_ready, g + 1)
                sp.dma_start(out[bass.ds(2 * g, 2)].rearrange("b q f -> q b f"), Xg(g)).then_inc(stored, 16)
            sp.wait_ge(stored, 16 * G)

        @block.gpsimd
        def _(pool):
            pool.wait_ge(small_in, 48)
            with pool.Fori(0, G) as g:
                pool.wait_ge(norm.xn_ready, 2 * (N0 + g + 1))
                pool.tensor_tensor(Xg(g), Xg(g), b2[:], ALU.add).then_inc(b2_added, 1)

        @block.scalar
        def _(act):
            def split_piece(i):
                loaded, raw, hi, _ = pieces[i]
                act.wait_ge(loaded, 16)
                act.activation(hi, raw, ACT.Copy).then_inc(w_hi_out, 1)

            act.wait_ge(small_in, 48)
            for i in range(AHEAD):
                split_piece(i)

            def step(g, par, j, first, last):
                if j >= J:
                    return
                u = J * g + j
                act.wait_ge(fc1_done, u + 1)
                if not first:
                    act.wait_ge(act_lo_ready, u - J + 1)
                for i in range(2):
                    ins = act.activation(act_f[j][:, i, :], FC1[j % 2][:, 256 * i:256 * i + 256], ACT.Gelu,
                                         bias=b1[:, 2 * j + i:2 * j + i + 1])
                ins.then_inc(gelu_ready, 1)
                act.wait_ge(gelu_ready, u + 1)
                if not first:
                    act.wait_ge(fc2_done, u - J + 1)
                act.activation(act_hi[j][:], act_f[j][:], ACT.Copy).then_inc(act_hi_ready, 1)
                if first:
                    for i in step_pieces(j):
                        split_piece(i)
                if j == 3 and not last:
                    norm.scale_offset(act, N0 + g + 1, 2, AUX)
                    norm.split_hi(act, N0 + g + 1, 1 - par)

            groups(act, step)

        @block.vector
        def _(dve):
            def split_piece(i):
                _, raw, hi, lo = pieces[i]
                dve.wait_ge(w_hi_out, i + 1)
                dve.tensor_tensor(lo, raw, hi.bitcast(F32), ALU.subtract).then_inc(w_lo_out, 1)

            for i in range(AHEAD):
                split_piece(i)

            norm_at = [((0, 1), (2, 3), (4, 5, 6, 7)), ((8,), (9, 10, 11), (12, 13, 14)), ((), (), ()), ((), (), ())]

            def add_output(g):
                dve.wait_ge(fc2_done, J * (g + 1))
                dve.wait_ge(b2_added, g + 1)
                dve.tensor_tensor(flat(Xg(g)), flat(Xg(g)), OUT[:], ALU.add).then_inc(y_ready, 1)

            def step(g, par, j, first, last):
                u = J * g + j

                def norm_stage(place):
                    if j < J and not last:
                        for k in norm_at[j][place]:
                            norm.stage(dve, k, N0 + g + 1, g + 1)

                if j == LAG - 1 and not first:
                    add_output(g - 1)
                norm_stage(0)
                if j < J:
                    dve.wait_ge(act_hi_ready, u + 1)
                    dve.tensor_tensor(act_lo[j][:], act_f[j][:], act_hi[j][:].bitcast(F32), ALU.subtract).then_inc(act_lo_ready, 1)
                    norm_stage(1)
                if first and j < J:
                    for i in step_pieces(j):
                        split_piece(i)
                norm_stage(2)
                if j == 3 and not last:
                    norm.split_lo(dve, N0 + g + 1, 1 - par)

            groups(dve, step)
            add_output(G - 1)

        @block.tensor
        def _(pe):
            def second(u, g, j, first):
                if j == 0 and not first:
                    pe.wait_ge(y_ready, g)
                if first:
                    pe.wait_ge(w_lo_out, 2 * j + 2)
                pe.wait_ge(act_lo_ready, u + 1)
                for b in range(2):
                    for i in range(2):
                        cut = slice(P * b, P * b + P)
                        ins = three_pass(pe, OUT[:, 256 * b:256 * b + 256], act_hi[j][:, i, cut], act_lo[j][:, i, cut],
                                         w2_hi[:, 2 * j + i, :], w2_lo[:, 2 * j + i, :],
                                         j == 0 and b == 0 and i == 0, j == J - 1 and b == 1 and i == 1, skip=True)
                ins.then_inc(fc2_done, 1)

            def step(g, par, j, first, last):
                u = J * g + j
                if j == 0 and not first:
                    second(u - LAG, g - 1, J - LAG, False)
                if j < J:
                    if j == 0:
                        pe.wait_ge(norm.lo_ready, N0 + g + 1)
                    if not (first and j < 2):
                        pe.wait_ge(gelu_ready, u - 1)
                    if first:
                        pe.wait_ge(w_lo_out, 2 * j + 1)
                    for i in range(2):
                        cut = slice(P * (2 * j + i), P * (2 * j + i) + P)
                        for kt in range(KT):
                            ins = three_pass(pe, FC1[j % 2][:, 256 * i:256 * i + 256], w1_hi[:, kt, cut], w1_lo[:, kt, cut],
                                             norm.hT_hi[par][:, kt], norm.hT_lo[par][:, kt], kt == 0, kt == KT - 1)
                    ins.then_inc(fc1_done, 1)
                if j == 3 and not last:
                    norm.transpose(pe, N0 + g + 1, AUX, ident)
                if j >= LAG:
                    second(u - LAG, g, j - LAG, first)
                elif j > 0 and not first:
                    second(u - LAG, g - 1, J + j - LAG, False)

            groups(pe, step)


def sequence(nc, d, out):
    G = 8
    with ExitStack() as ctx:
        m = Mem(nc, ctx)
        X = m.sb("X", [P, 2 * G, 256])
        ident = m.sb("ident", [P, P])
        banks = [m.psum(f"bank{i}") for i in range(8)]
        attention0(nc, X, ident, banks, d, G)
        with ExitStack() as local:
            shared = NormedInput(Mem(nc, local), X, d)
            cross_layers(nc, X, ident, banks, d, G, shared)
            mlp(nc, X, ident, banks, d, out, G, shared)



def _layout(inputs):
    import numpy as np

    a = {k: np.asarray(v) for k, v in inputs.items()}
    l0, l1 = (lambda n: a[f"L0_xattn_{n}"]), (lambda n: a[f"L1_xattn_{n}"])
    both = lambda n: np.stack([l1(f"{n}1"), l1(f"{n}2")])
    heads = lambda t: t.reshape(2, 16, P).transpose(0, 2, 1)
    ln = np.stack([np.stack([l1(f"{n}_scale"), l1(f"{n}_offset")]) for n in ("ln1", "ln2", "ln_mlp")])
    ln = ln.reshape(3, 2, 2, P).transpose(3, 0, 1, 2)
    params = np.stack([heads(both(n)) for n in ("bq", "bk", "bias_k", "bias_v", "bv")], axis=2).transpose(1, 0, 2, 3)
    ctx = a["ctx_2048"]
    arrays = {
        "x": a["x"], "u": ctx, "ctxT": ctx.transpose(2, 0, 1).reshape(2, P, 16, P).transpose(1, 0, 2, 3),
        "wz0": l0("Wqkv0").T, "wz1": l0("Wqkv1").T, "wu0": l0("Winj0").T, "wu1": l0("Winj1").T, "wo0": l0("Wo").T,
        "rwb": l0("r_w_bias").reshape(8, P).T, "bo0": l0("bo").reshape(P, 1), "ident": np.eye(P, dtype=np.float32),
        "wq": both("wq"), "wk": both("wk"), "wv": both("wv"), "wo": both("wo"),
        "params": params, "bo": both("bo"), "ln": ln,
        "w1": l1("w_fc1"), "b1": l1("b_fc1").reshape(8, P).T, "w2": l1("w_fc2"), "b2": l1("b_fc2").reshape(1, 256),
    }
    return {k: np.ascontiguousarray(v) for k, v in arrays.items()}


def kernel(**inputs):
    import concourse.bacc as bacc
    from concourse.bass_utils import run_bass_kernel_spmd

    nc = bacc.Bacc("TRN2", target_bir_lowering=False, num_devices=1)
    arrays = {f"in_{name}": a for name, a in _layout(inputs).items()}
    d = {name[3:]: nc.dram_tensor(name, a.shape, mybir.dt.from_np(a.dtype), kind="ExternalInput").ap()
         for name, a in arrays.items()}
    out = nc.dram_tensor("out", (16, P, 256), F32, kind="ExternalOutput").ap()
    sequence(nc, d, out)
    return run_bass_kernel_spmd(nc, [arrays], core_ids=[0]).results[0]["out"]
```

```python
from contextlib import ExitStack

import concourse.bass as bass
from concourse import mybir

F32 = mybir.dt.float32
F32R = mybir.dt.float32r
I32 = mybir.dt.int32
ALU = mybir.AluOpType
ACT = mybir.ActivationFunctionType
AX_X = mybir.AxisListType.X
EPS = 1e-5
P = 128


class Mem:

    def __init__(self, nc, stack):
        self.nc, self.stack = nc, stack

    def sb(self, name, shape, dt=F32):
        return self.stack.enter_context(self.nc.sbuf_tensor(name, shape, dt))

    def psum(self, name):
        return self.stack.enter_context(self.nc.psum_tensor(name, [P, 512], F32))

    def sem(self, name):
        return self.stack.enter_context(self.nc.semaphore(name))

    def sems(self, *names):
        return [self.sem(n) for n in names]


def wait(eng, sem, value):
    if isinstance(value, int) and value <= 0:
        return
    eng.wait_ge(sem, value)


def three_pass(eng, out, w_hi, w_lo, m_hi, m_lo, start, stop, skip=False):
    eng.matmul(out, w_hi, m_lo, start=start, stop=False, skip_group_check=skip)
    eng.matmul(out, w_lo, m_hi, start=False, stop=False, skip_group_check=skip)
    return eng.matmul(out, w_hi, m_hi, start=False, stop=stop, skip_group_check=skip)



def flat_of(t):
    return t[:].rearrange("p b l -> p (b l)")


def attention0(nc, X, ident, banks, d, G, normed_input, cross_start):
    PAIRS, L, C = 8, 256, 2
    NB = 2 * PAIRS
    with ExitStack() as local:
        m = Mem(nc, local)
        names = ("wz0", "wz1", "wu0", "wu1")
        w_hi = {n: m.sb(f"{n}_hi", [P, 3, 1024], F32R) for n in names}
        w_lo = {n: m.sb(f"{n}_lo", [P, 3, 1024], F32R) for n in names}
        wo_hi = m.sb("wo0_hi", [P, PAIRS, P], F32R)
        wo_lo = m.sb("wo0_lo", [P, PAIRS, P], F32R)
        ni = normed_input
        u_raw = cross_start.ctx_raw[:].rearrange("p (b l) -> p b l", b=2)
        v_sb = cross_start.wide
        sq, std = m.sb("sq", [P, 512]), m.sb("std", [P, 512])
        stage = [[flat_of(ni.xn), flat_of(ni.hT)], [sq[:], std[:]]]
        z_hi, z_lo = m.sb("z_hi", [P, 2, L], F32R), m.sb("z_lo", [P, 2, L], F32R)
        u_hi, u_lo = m.sb("u_hi", [P, 2, L], F32R), m.sb("u_lo", [P, 2, L], F32R)
        q_sb = [[m.sb(f"q{x}{i}", [P, C, 2, P], F32R) for i in range(2)] for x in "AB"]
        k_hi = [[m.sb(f"kh{x}{i}", [P, C, 2, P], F32R) for i in range(2)] for x in "AB"]
        k_lo = [[m.sb(f"kl{x}{i}", [P, C, 2, P], F32R) for i in range(2)] for x in "AB"]
        probs = [[m.sb(f"p{x}{i}", [P, 2, L]) for i in range(2)] for x in "AB"]
        probsT = [[m.sb(f"pT{x}{i}", [P, 2, L]) for i in range(2)] for x in "AB"]
        stage += [[flat_of(probs[0][0]), flat_of(probs[0][1])], [flat_of(probsT[0][0]), flat_of(probsT[0][1])]]
        nmax = [m.sb(f"nmax{x}", [P, 2, 2]) for x in "AB"]
        sums = [m.sb(f"sums{x}", [P, 2, 2]) for x in "AB"]
        rsum = [m.sb(f"rsum{x}", [P, 2, 2]) for x in "AB"]
        av_f = m.sb("av0", [P, 2, L])
        av_hi, av_lo = m.sb("av0_hi", [P, 2, L], F32R), m.sb("av0_lo", [P, 2, L], F32R)
        rwb, bo = m.sb("rwb", [P, PAIRS]), m.sb("bo0", [P, 1])
        mean_w, eps, warm = m.sb("mean_w", [P, P]), m.sb("eps0", [P, 1]), m.sb("warm", [P, 1])
        rstd = m.sb("rstd", [P, 512])

        PJ, SB, TB, AVB, OUT = banks[0:2], banks[2:4], banks[4:6], banks[6], banks[7]

        (x_in, small_in, stage_in0, stage_in1, stage_in2, stage_in3, w_split_hi, w_split_lo, const,
         u_in, zu_hi, zu_lo, proj_done, q_hi_ready, q_ready, k_hi_ready, k_lo_ready, k_dup_in0, k_dup_in1, v_ready, s_done,
         max_done, exp_done, rec_done, normA_done, normB_done, t_done, ptA_ready, ptB_ready, av_done, avhi_ready,
         avlo_ready, w_done, out_done, mean_done, centred, squared, var_done, std_ready, rstd_ready,
         normed) = m.sems(*(f"a0_{n}" for n in (
             "x_in", "small_in", "stage_in0", "stage_in1", "stage_in2", "stage_in3", "w_split_hi", "w_split_lo", "const",
             "u_in", "zu_hi", "zu_lo", "proj_done", "q_hi_ready", "q_ready", "k_hi_ready", "k_lo_ready", "k_dup_in0", "k_dup_in1",
             "v_ready", "s_done", "max_done", "exp_done", "rec_done", "normA_done", "normB_done", "t_done", "ptA_ready",
             "ptB_ready", "av_done", "avhi_ready", "avlo_ready", "w_done", "out_done", "mean_done", "centred",
             "squared", "var_done", "std_ready", "rstd_ready", "normed")))
        stage_in, k_dup_in = [stage_in0, stage_in1, stage_in2, stage_in3], [k_dup_in0, k_dup_in1]

        pieces = [("qk", 0, "z"), ("qk", 0, "u"), ("v", 0, "z"), ("v", 0, "u"), ("qk", 1, "z"), ("qk", 1, "u"), ("wo", 0, ""),
                  ("v", 1, "z"), ("v", 1, "u"), ("qk", 2, "z"), ("qk", 2, "u"), ("qk", 3, "z"), ("qk", 3, "u")]
        AHEAD_PIECES = 4
        STEP_PIECES = {0: [4, 5], 1: [6], 2: [7], 3: [8, 9], 4: [10], 5: [11], 6: [12]}
        POOL_FROM = 9

        def stage_of(i):
            return i if i in (2, 3) else i % 2

        def piece(i, tables, wo):
            kind, c, src = pieces[i]
            found = []
            for j in range(2):
                n, half = f"w{src}{j}", stage[stage_of(i)][j]
                if kind == "wo":
                    found.append(("wo0", wo[:, 4 * j:4 * j + 4], half.rearrange("k (p o) -> k p o", o=P)))
                elif kind == "qk":
                    found.append((n, tables[n][:, 0:2, 256 * c:256 * c + 256], half.rearrange("p (s n) -> p s n", s=2)))
                else:
                    found.append((n, tables[n][:, 2, 512 * c:512 * c + 512], half))
            return found

        def hi_piece(i):
            return piece(i, w_hi, wo_hi)

        def lo_piece(i):
            return piece(i, w_lo, wo_lo)

        ahead = [("k", 0, 0), ("q", 0, 0), ("k", 1, 0)] + [("v", c, 0) for c in range(3)]
        AHEAD = len(ahead)
        STAT = ("mean", "var")

        FURTHER = {(0, 0): ("v", 3, 0), (2, 0): ("mean", 0, 0), (2, 1): ("v", 4, 0), (3, 0): ("v", 5, 0), (3, 1): ("var", 0, 0),
                   (4, 0): ("v", 6, 0), (4, 1): ("v", 7, 0), (6, 1): ("v", 0, 1), (7, 0): ("v", 1, 1), (7, 1): ("v", 2, 1)}

        def jobs(p, b):
            kind, pair = ("q", p + 1) if b == 0 else ("k", p + 2)
            return [FURTHER[at] for at in ((p, b),) if at in FURTHER] + [(kind, pair % PAIRS, pair // PAIRS)]

        in_order = [job for i in range(NB) for job in jobs(*divmod(i, 2))]
        projections = [job for job in in_order if job[0] not in STAT]
        JOBS = len(projections)
        SPLIT_NEXT = (PAIRS - 2, 0)
        AFTER_SPLIT = (PAIRS - 2, 1)
        BEFORE_NEXT = sum(job[2] == 0 for job in projections)

        def step_jobs(g, p, b, first, last):
            start = sum(len(jobs(*divmod(i, 2))) for i in range(2 * p + b))
            for i, job in enumerate(jobs(p, b), start):
                if (last and job[2]) or (first and job[0] in STAT):
                    continue
                before = sum(j[0] not in STAT for j in in_order[:i])
                yield AHEAD + JOBS * g + before, (AHEAD + i) % 2, job, i

        def wait_emptied(eng, i, g, first):
            i -= 2
            if first and i >= 0 and in_order[i][0] in STAT:
                i -= 2
            if first and i < 0:
                if i < -AHEAD:
                    return
                (kind, which, _), further = ahead[AHEAD + i], 0
            else:
                kind, which, further = in_order[i]
                if i < 0:
                    further -= 1
            if kind == "v":
                eng.wait_ge(v_ready, 8 * (g + further) + which + 1)
            elif kind in STAT:
                eng.wait_ge(centred if kind == "mean" else std_ready, g)
            else:
                eng.wait_ge(q_ready if kind == "q" else k_lo_ready, PAIRS * (g + further) + which + 1)

        def groups(eng, step):
            for i in range(NB):
                step(0, *divmod(i, 2), True, False)
            with eng.Fori(1, G - 1) as g:
                for i in range(NB):
                    step(g, *divmod(i, 2), False, False)
            for i in range(NB):
                step(G - 1, *divmod(i, 2), False, True)

        def back(g, p, n):
            return (g, p - n) if p >= n else (g - 1, p - n + PAIRS)

        def qk_before(g, p, b, first, last):
            if p or b:
                found = [(g, *job[:3]) for job in step_jobs(g, *divmod(2 * p + b - 1, 2), first, last)]
            else:
                found = [] if first else [(g - 1, *job[:3]) for job in step_jobs(g - 1, PAIRS - 1, 1, False, False)]
            return [job for job in found if job[3][0] in "qk"]

        def further_jobs(g, p, b, first, last):
            return [job[:3] for job in step_jobs(g, p, b, first, last) if job[2][0] not in "qk"]

        def flat(t):
            return t.rearrange("p b l -> p (b l)")

        def chunks(t):
            return t[:].rearrange("p c b l -> p (c b l)")

        def Xg(g):
            return flat(X[:, bass.ds(2 * g, 2), :])

        block = local.enter_context(nc.Block())

        @block.sync
        def _(sp):
            def load_piece(i):
                kind, c, _ = pieces[i]
                for j, (n, _, st) in enumerate(hi_piece(i)):
                    if kind == "wo":
                        src = d["wo0"].rearrange("(p k) o -> k p o", k=P)[:, 4 * j:4 * j + 4]
                    elif kind == "qk":
                        src = d[n].rearrange("p (s n) -> p s n", s=3)[:, 0:2, 256 * c:256 * c + 256]
                    else:
                        src = d[n][:, 2048 + 512 * c:2048 + 512 * c + 512]
                    sp.dma_start(st, src).then_inc(stage_in[stage_of(i)], 16)

            load_piece(0)
            sp.dma_start(X[:, 0:2, :], d["x"][0:2].rearrange("b d l -> d b l")).then_inc(x_in, 16)
            load_piece(1)
            sp.dma_start(u_raw, d["u"][0:2].rearrange("b d l -> d b l")).then_inc(u_in, 16)
            load_piece(2)
            load_piece(3)
            sp.dma_start(rwb[:], d["rwb"]).then_inc(small_in, 16)
            sp.dma_start(bo[:], d["bo0"]).then_inc(small_in, 16)
            sp.dma_start(ident[:], d["ident"]).then_inc(small_in, 16)
            sp.dma_start(ni.ln_all[:], d["ln"].rearrange("p l i k -> p l (i k)")).then_inc(ni.ln_in, 16)

            def stage_piece(i):
                sp.wait_ge(w_split_lo, i - 3 if i < 6 else i - 1)
                load_piece(i)

            def double_k(pair, p):
                par = p % 2
                for part, ready in ((k_hi, k_hi_ready), (k_lo, k_lo_ready)):
                    sp.wait_ge(ready, pair + 1)
                    for x in range(2):
                        own, other = slice(64 * x, 64 * x + 64), slice(64 * (1 - x), 64 * (1 - x) + 64)
                        sp.dma_start(part[x][par][other].bitcast(F32), part[x][par][own].bitcast(F32)).then_inc(k_dup_in[par], 16)

            for i in (4, 5):
                stage_piece(i)
            double_k(0, 0)
            double_k(1, 1)
            sp.dma_start(X[:, 2:, :], d["x"][2:].rearrange("b d l -> d b l")).then_inc(x_in, 16)

            def load_u(g):
                sp.wait_ge(zu_lo, 2 * g)
                sp.dma_start(u_raw, d["u"][bass.ds(2 * g, 2)].rearrange("b d l -> d b l")).then_inc(u_in, 16)

            def step(g, p, b, first, last):
                if (p, b) == (0, 0) and not last:
                    load_u(g + 1)
                if first:
                    for i in STEP_PIECES.get(2 * p + b, []):
                        if i + 2 < len(pieces):
                            stage_piece(i + 2)
                if b == 1 and not (last and p + 2 >= PAIRS):
                    double_k(PAIRS * g + p + 2, p + 2)

            groups(sp, step)
            sp.wait_ge(zu_lo, 2 * G)
            sp.wait_ge(av_done, NB * (G - 1) + NB // 2)
            cross_start.load(sp)

        @block.gpsimd
        def _(pool):
            pool.memset(mean_w[:], 1.0 / P).then_inc(const, 1)
            pool.memset(eps[:], EPS).then_inc(const, 1)

            def av_low(pair):
                pool.wait_ge(avhi_ready, pair + 1)
                pool.tensor_tensor(flat(av_lo[:]), flat(av_f[:]), flat(av_hi[:]).bitcast(F32), ALU.subtract).then_inc(avlo_ready, 1)

            def scale(g):
                pool.wait_ge(rstd_ready, 4 * (g + 1))
                pool.tensor_tensor(Xg(g), Xg(g), rstd[:], ALU.mult).then_inc(normed, 1)

            def step(g, p, b, first, last):
                u = NB * g + 2 * p + b
                if b == 0 and not (first and p < 2):
                    ag, ap = back(g, p, 2)
                    av_low(PAIRS * ag + ap)
                if first:
                    for i in STEP_PIECES.get(2 * p + b, []):
                        if i < POOL_FROM:
                            continue
                        pool.wait_ge(w_split_lo, i)
                        pool.wait_ge(w_split_hi, i + 1)
                        for (_, hi, st), (_, lo, _) in zip(hi_piece(i), lo_piece(i)):
                            ins = pool.tensor_tensor(lo, st, hi.bitcast(F32), ALU.subtract)
                        ins.then_inc(w_split_lo, 1)
                pool.wait_ge(rec_done, 2 * u + 2)
                factor = rsum[1][:, b, :].rearrange("p (i o) -> p i o", o=1).to_broadcast([P, 2, L])
                pool.tensor_tensor(probs[1][b][:], probs[1][b][:], factor, ALU.mult).then_inc(normB_done, 1)

                if not first and (p, b) == (5, 1):
                    scale(g - 1)

            groups(pool, step)
            av_low(PAIRS * G - 2)
            av_low(PAIRS * G - 1)

        @block.scalar
        def _(act):
            def split_hi(g):
                act.wait_ge(u_in, 16 * (g + 1))
                act.activation(z_hi[:], X[:, bass.ds(2 * g, 2), :], ACT.Copy).then_inc(zu_hi, 1)
                act.activation(u_hi[:], u_raw, ACT.Copy).then_inc(zu_hi, 1)

            def split_piece(i):
                act.wait_ge(stage_in[stage_of(i)], 32 * (i // 2 if i >= 4 else 1))
                for _, hi, st in hi_piece(i):
                    ins = act.activation(hi, st, ACT.Copy)
                ins.then_inc(w_split_hi, 1)

            def evac(n, bank, job, g):
                kind, which, further = job
                if kind in STAT:
                    return
                if kind == "v":
                    gg = g + further
                    act.wait_ge(proj_done, n + 1)
                    wait(act, av_done, NB * gg - (NB // 2 if which < 4 else 0) if not (isinstance(gg, int) and gg == 0) else 0)
                    half_, rest = divmod(which, 4)
                    dst = v_sb[:, rest // 2, rest % 2, 512 * half_:512 * half_ + 512]
                    act.activation(dst, PJ[bank][:], ACT.Copy).then_inc(v_ready, 1)
                    return
                pair = PAIRS * (g + further) + which
                par = which % 2
                act.wait_ge(proj_done, n + 1)
                wait(act, s_done, 4 * (pair - 1))
                for x in range(2):
                    rows = slice(64 * x, 64 * x + 64)
                    if kind == "q":
                        ins = act.activation(chunks(q_sb[x][par])[rows], PJ[bank][rows], ACT.Identity,
                                             bias=rwb[rows, which:which + 1])
                    else:
                        ins = act.activation(chunks(k_hi[x][par])[rows], PJ[bank][rows], ACT.Copy, scale=0.125)
                ins.then_inc(q_hi_ready if kind == "q" else k_hi_ready, 1)

            def std_dev(g, bank, out):
                act.wait_ge(var_done, g + 1)
                wait(act, rstd_ready, 4 * g)
                act.activation(out, PJ[bank][:], ACT.Sqrt, bias=eps[:, 0:1]).then_inc(std_ready, 1)

            def square(g):
                act.wait_ge(centred, g + 1)
                wait(act, var_done, g)
                act.activation(sq[:], Xg(g), ACT.Square).then_inc(squared, 1)

            def pt_b(u, b):
                act.wait_ge(t_done, 2 * u + 2)
                wait(act, av_done, u - 1)
                act.activation(flat(probsT[1][b][:]), TB[1][:], ACT.Copy).then_inc(ptB_ready, 1)

            def av_high(pair):
                act.wait_ge(av_done, 2 * pair + 2)
                wait(act, w_done, pair)
                act.activation(flat(av_f[:]), AVB[:], ACT.Copy)
                act.activation(flat(av_hi[:]), AVB[:], ACT.Copy).then_inc(avhi_ready, 1)

            act.wait_ge(const, 2)
            act.activation(warm[:], eps[:], ACT.Exp)
            split_piece(0)
            act.wait_ge(x_in, 16)
            split_hi(0)
            split_piece(1)
            act.wait_ge(small_in, 48)
            for n, job in enumerate(ahead):
                if n < 2:
                    split_piece(2 + n)
                evac(n, n % 2, job, 0)

            def step(g, p, b, first, last):
                u = NB * g + 2 * p + b
                start = first and p == 0 and b == 0
                if not (first and p == 0):
                    pt_b(u - 2, b)
                if b == 0 and not (first and p < 2):
                    ag, ap = back(g, p, 2)
                    av_high(PAIRS * ag + ap)
                for jg, n, bank, job in qk_before(g, p, b, first, last):
                    evac(n, bank, job, jg)
                if first:
                    for i in STEP_PIECES.get(2 * p + b, []):
                        split_piece(i)
                for x in range(2):
                    act.wait_ge(max_done, 2 * u + x + 1)
                    if not (first and p == 0):
                        act.wait_ge(t_done, 2 * (u - 2) + x + 1)
                    for it in range(2):
                        ins = act.activation(probs[x][b][:, it, :], SB[x][:, L * it:L * it + L], ACT.Exp,
                                             bias=nmax[x][:, b, it:it + 1], accum_out=sums[x][:, b, it:it + 1])
                    ins.then_inc(exp_done, 1)
                for n, bank, job in further_jobs(g, p, b, first, last):
                    if job[0] == "var":
                        std_dev(g - 1, bank, std[:])
                    evac(n, bank, job, g)
                if (p, b) == (2, 1) and not first:
                    square(g - 1)
                if last and (p, b) == (7, 1):
                    ni.scale_offset(act, 0, 0, PJ[0])
                    ni.split_hi(act, 0, 0)
                if (p, b) == SPLIT_NEXT and not last:
                    act.wait_ge(proj_done, AHEAD + JOBS * g + BEFORE_NEXT)
                    if first:
                        act.wait_ge(x_in, 32)
                    split_hi(g + 1)

            groups(act, step)
            av_high(PAIRS * G - 2)
            pt_b(NB * G - 2, 0)
            pt_b(NB * G - 1, 1)
            av_high(PAIRS * G - 1)
            square(G - 1)
            std_dev(G - 1, 1, flat_of(ni.xn))

        @block.vector
        def _(dve):
            def split_lo(g):
                dve.wait_ge(zu_hi, 2 * g + 2)
                dve.tensor_tensor(z_lo[:], X[:, bass.ds(2 * g, 2), :], z_hi[:].bitcast(F32), ALU.subtract).then_inc(zu_lo, 1)
                dve.tensor_tensor(u_lo[:], u_raw, u_hi[:].bitcast(F32), ALU.subtract).then_inc(zu_lo, 1)

            def split_piece(i):
                dve.wait_ge(w_split_hi, i + 1)
                for (_, hi, st), (_, lo, _) in zip(hi_piece(i), lo_piece(i)):
                    ins = dve.tensor_tensor(lo, st, hi.bitcast(F32), ALU.subtract)
                ins.then_inc(w_split_lo, 1)

            def evac(n, bank, job, g):
                kind, which, further = job
                if kind not in ("q", "k"):
                    return
                pair, par = PAIRS * (g + further) + which, which % 2
                dve.wait_ge(q_hi_ready if kind == "q" else k_hi_ready, pair + 1)
                for x in range(2):
                    rows = slice(64 * x, 64 * x + 64)
                    if kind == "q":
                        other = slice(64 * (1 - x), 64 * (1 - x) + 64)
                        q = chunks(q_sb[x][par])
                        ins = dve.scalar_tensor_tensor(q[other], PJ[bank][rows], rwb[rows, which:which + 1],
                                                       q[rows].bitcast(F32), ALU.add, ALU.subtract)
                    else:
                        ins = dve.scalar_tensor_tensor(chunks(k_lo[x][par])[rows], PJ[bank][rows], 0.125,
                                                       chunks(k_hi[x][par])[rows].bitcast(F32), ALU.mult, ALU.subtract)
                ins.then_inc(q_ready if kind == "q" else k_lo_ready, 1)

            def pt_a(u, b):
                dve.wait_ge(t_done, 2 * u + 1)
                wait(dve, av_done, u - 1)
                dve.tensor_copy(flat(probsT[0][b][:]), TB[0][:]).then_inc(ptA_ready, 1)

            def output(g):
                dve.wait_ge(w_done, PAIRS * (g + 1))
                dve.scalar_tensor_tensor(Xg(g), OUT[:], bo[:, 0:1], Xg(g), ALU.add, ALU.add).then_inc(out_done, 1)

            def centre(g, bank):
                dve.wait_ge(mean_done, g + 1)
                dve.tensor_tensor(Xg(g), Xg(g), PJ[bank][:], ALU.subtract).then_inc(centred, 1)

            def normalize(u, b):
                for x in range(2):
                    dve.wait_ge(exp_done, 2 * u + x + 1)
                    dve.reciprocal(rsum[x][:, b, :], sums[x][:, b, :]).then_inc(rec_done, 1)
                dve.wait_ge(rec_done, 2 * u + 1)
                for it in range(2):
                    row = probs[0][b][:, it, :]
                    ins = dve.tensor_scalar(row, row, rsum[0][:, b, it:it + 1], None, ALU.mult)
                ins.then_inc(normA_done, 1)

            def reciprocal_std(g, quarter):
                if quarter == 0:
                    dve.wait_ge(std_ready, g + 1)
                    wait(dve, normed, g)
                cut = slice(P * quarter, P * quarter + P)
                dve.reciprocal(rstd[:, cut], std[:, cut]).then_inc(rstd_ready, 1)

            def step(g, p, b, first, last):
                u = NB * g + 2 * p + b
                if not (first and p == 0):
                    pt_a(u - 2, b)
                for x in range(2):
                    dve.wait_ge(s_done, 2 * u + x + 1)
                    dve.tensor_reduce(nmax[x][:, b, :], SB[x][:].rearrange("p (i j) -> p i j", i=2), AX_X, ALU.max,
                                      negate=True).then_inc(max_done, 1)
                for jg, n, bank, job in qk_before(g, p, b, first, last):
                    evac(n, bank, job, jg)
                for n, bank, job in further_jobs(g, p, b, first, last):
                    if job[0] == "mean":
                        centre(g - 1, bank)
                if first:
                    for i in STEP_PIECES.get(2 * p + b, []):
                        if i < POOL_FROM:
                            split_piece(i)
                normalize(u, b)
                if (p, b) == SPLIT_NEXT and not last:
                    split_lo(g + 1)
                if last and 2 * p + b == 0:
                    dve.wait_ge(ni.ln_in, 16)
                    ni.set_layer(dve, 0)
                    ni.stage(dve, 0, 0, 0)
                if last and 2 * p + b + 1 < ni.STAGES:
                    ni.stage(dve, 2 * p + b + 1, 0, 0)
                if last and (p, b) == (7, 1):
                    ni.split_lo(dve, 0, 0)
                if not first:
                    if (p, b) == (1, 1):
                        output(g - 1)
                    if (4, 0) <= (p, b) <= (5, 1):
                        reciprocal_std(g - 1, 2 * p + b - 8)

            split_piece(0)
            dve.wait_ge(x_in, 16)
            split_lo(0)
            split_piece(1)
            for n, job in enumerate(ahead):
                if n < 2:
                    split_piece(2 + n)
                evac(n, n % 2, job, 0)
            groups(dve, step)
            pt_a(NB * G - 2, 0)
            pt_a(NB * G - 1, 1)
            output(G - 1)
            centre(G - 1, 0)

        @block.tensor
        def _(pe):
            pe.wait_ge(small_in, 48)
            pe.wait_ge(const, 2)

            def mean(out, src, done):
                pe.matmul(out[:], mean_w[:], src, start=True, stop=True).then_inc(done, 1)

            def project(n, bank, job, i, g, first):
                kind, which, further = job
                if further or (isinstance(n, int) and n == 0):
                    pe.wait_ge(zu_lo, 2 * (g + further) + 2)
                if first and not further:
                    need = ("v", which // 4, "u") if kind == "v" else ("qk", which // 2, "u")
                    pe.wait_ge(w_split_lo, pieces.index(need) + 1)
                wait_emptied(pe, i, g, first)
                if kind == "mean":
                    pe.wait_ge(out_done, g)
                    mean(PJ[bank], Xg(g - 1), mean_done)
                    return
                if kind == "var":
                    pe.wait_ge(squared, g)
                    mean(PJ[bank], sq[:], var_done)
                    return
                if kind in "qk":
                    part, cut = (0 if kind == "q" else 1), slice(P * which, P * which + P)
                    for c in range(C):
                        out = PJ[bank][:, 256 * c:256 * c + 256]
                        pos = slice(P * c, P * c + P)
                        three_pass(pe, out, w_hi[f"wz{c}"][:, part, cut], w_lo[f"wz{c}"][:, part, cut],
                                   z_hi[:, :, pos], z_lo[:, :, pos], True, False)
                        ins = three_pass(pe, out, w_hi[f"wu{c}"][:, part, cut], w_lo[f"wu{c}"][:, part, cut],
                                         u_hi[:, :, pos], u_lo[:, :, pos], False, True)
                else:
                    half_, rest = divmod(which, 4)
                    b, c = divmod(rest, 2)
                    pos = slice(P * c, P * c + P)
                    cut = slice(512 * half_, 512 * half_ + 512)
                    three_pass(pe, PJ[bank][:], z_hi[:, b, pos], z_lo[:, b, pos],
                               w_hi[f"wz{c}"][:, 2, cut], w_lo[f"wz{c}"][:, 2, cut], True, False)
                    ins = three_pass(pe, PJ[bank][:], u_hi[:, b, pos], u_lo[:, b, pos],
                                     w_hi[f"wu{c}"][:, 2, cut], w_lo[f"wu{c}"][:, 2, cut], False, True)
                ins.then_inc(proj_done, 1)

            def scores(g, p, b, first):
                u = NB * g + 2 * p + b
                pair, par = PAIRS * g + p, p % 2
                pe.wait_ge(q_ready, pair + 1)
                pe.wait_ge(k_dup_in[par], 64 * (PAIRS // 2 * g + p // 2 + 1))
                for x in range(2):
                    if not (first and p == 0 and b == 0):
                        pe.wait_ge(exp_done, 2 * (u - 1) + x + 1)
                    for it in range(2):
                        out, q = SB[x][:, L * it:L * it + L], q_sb[x][par][:, it, b, :]
                        pe.matmul(out, q, k_lo[x][par][:, :, b, :], start=True, stop=False)
                        ins = pe.matmul(out, q, k_hi[x][par][:, :, b, :], start=False, stop=True)
                    ins.then_inc(s_done, 1)

            def transposes(u, b):
                for x in range(2):
                    pe.wait_ge((normA_done, normB_done)[x], u + 1)
                    wait(pe, (ptA_ready, ptB_ready)[x], u)
                    for jt in range(2):
                        for it in range(2):
                            ins = pe.transpose(TB[x][:, L * jt + P * it:L * jt + P * it + P],
                                               probs[x][b][:, it, P * jt:P * jt + P], ident[:])
                    ins.then_inc(t_done, 1)

            def weighted(g, p, b):
                u = NB * g + 2 * p + b
                pe.wait_ge(v_ready, 8 * g + (8 if p >= 4 else 4))
                pe.wait_ge(ptA_ready, u + 1)
                pe.wait_ge(ptB_ready, u + 1)
                if b == 0:
                    wait(pe, avhi_ready, PAIRS * g + p)
                for jt in range(2):
                    for x in range(2):
                        col = P * p + 64 * x
                        ins = pe.matmul(AVB[64 * x:64 * x + 64, L * b:L * b + L], v_sb[:, b, jt, col:col + 64],
                                        probsT[x][b][:, jt, :], start=(jt == 0), stop=(jt == 1))
                ins.then_inc(av_done, 1)

            def out_product(g, p, first):
                pe.wait_ge(avlo_ready, PAIRS * g + p + 1)
                if first:
                    pe.wait_ge(w_split_lo, pieces.index(("wo", 0, "")) + 1)
                if p == 0:
                    wait(pe, out_done, g)
                three_pass(pe, OUT[:], wo_hi[:, p, :], wo_lo[:, p, :], flat(av_hi[:]), flat(av_lo[:]),
                           p == 0, p == PAIRS - 1).then_inc(w_done, 1)

            def step(g, p, b, first, last):
                u = NB * g + 2 * p + b
                scores(g, p, b, first)
                found = list(step_jobs(g, p, b, first, last))
                early = 0 if (p, b) == AFTER_SPLIT else 1
                for n, bank, job, i in found[:early]:
                    project(n, bank, job, i, g, first)
                if not (first and p == 0 and b == 0):
                    transposes(u - 1, 1 - b)
                if not (first and p == 0):
                    weighted(*back(g, p, 1), b)
                for n, bank, job, i in found[early:]:
                    project(n, bank, job, i, g, first)
                if b == 0 and not (first and p < 2):
                    out_product(*back(g, p, 2), first)
                if last and (p, b) == (7, 0):
                    ni.transpose(pe, 0, PJ[0], ident)

            for n, job in enumerate(ahead):
                project(n, n % 2, job, n - AHEAD, 0, True)
            groups(pe, step)
            transposes(NB * G - 1, 1)
            weighted(G - 1, PAIRS - 1, 0)
            out_product(G - 1, PAIRS - 2, False)
            weighted(G - 1, PAIRS - 1, 1)
            out_product(G - 1, PAIRS - 1, False)
            pe.wait_ge(out_done, G)
            pe.wait_ge(ni.hT_ready, 2)
            mean(PJ[0], Xg(G - 1), mean_done)
            pe.wait_ge(squared, G)
            mean(PJ[1], sq[:], var_done)



class NormedInput:

    BEFORE = (0, 2, 4, 5, 6) + tuple(range(7, 17))
    STAGES, CHAIN, KT = len(BEFORE), 16, 2

    def __init__(self, m, X, d):
        self.X, self.d = X, d
        self.stats, self.mv = m.sb("n_stats", [P, 2, 6]), m.sb("n_mv", [P, 2, 2])
        self.var, self.y, self.t = (m.sb(f"n_{n}", [P, 2]) for n in ("var", "y", "t"))
        self.waited = m.sb("n_waited", [P, 1])
        self.half = m.sb("n_half", [P, 2], I32)
        self.xn, self.hT = m.sb("xn", [P, 2, 256]), m.sb("hT", [P, 2, 256])
        self.hT_hi, self.hT_lo = [m.sb("hT_hi0", [P, 2, 256], F32R)], [m.sb("hT_lo0", [P, 2, 256], F32R)]
        self.ln_all = m.sb("ln_all", [P, 3, 4])
        self.ln = m.sb("ln", [P, 1, 4])
        (self.ln_in, self.ln_ready, self.chain, self.xn_ready, self.hT_done, self.hT_ready, self.hi_ready,
         self.lo_ready) = m.sems(*(f"n_{n}" for n in (
             "ln_in", "ln_ready", "chain", "xn_ready", "hT_done", "hT_ready", "hi_ready", "lo_ready")))

    def add_second(self, m):
        self.hT_hi.append(m.sb("hT_hi1", [P, 2, 256], F32R))
        self.hT_lo.append(m.sb("hT_lo1", [P, 2, 256], F32R))

    def set_layer(self, dve, layer):
        dve.tensor_copy(self.ln[:], self.ln_all[:, bass.ds(layer, 1), :]).then_inc(self.ln_ready, 1)

    def stage(self, dve, k, n, g):
        Xg, base = self.X[:, bass.ds(2 * g, 2), :], self.CHAIN * n
        if k > 0:
            dve.wait_ge(self.chain, base + self.BEFORE[k])
        if k == 0:
            for b in range(2):
                dve.bn_stats(self.stats[:, b, :], Xg[:, b, :]).then_inc(self.chain, 1)
        elif k == 1:
            dve.memset(self.waited[:], 0.0)
            for b in range(2):
                dve.bn_aggr(self.mv[:, b, :], self.stats[:, b, :]).then_inc(self.chain, 1)
        elif k == 2:
            dve.tensor_scalar(self.var[:], self.mv[:, :, 1], EPS, None, ALU.add).then_inc(self.chain, 1)
        elif k == 3:
            dve.tensor_scalar(self.half[:], self.var[:].bitcast(I32), 1, None, ALU.logical_shift_right).then_inc(self.chain, 1)
        elif k == 4:
            dve.tensor_scalar(self.y[:].bitcast(I32), self.half[:], -1.0, float(0x5F3759DF), ALU.mult, ALU.add).then_inc(self.chain, 1)
        elif k == self.STAGES - 1:
            for b in range(2):
                dve.tensor_scalar(self.xn[:, b, :], Xg[:, b, :], self.mv[:, b, 0:1], self.y[:, b:b + 1],
                                  ALU.subtract, ALU.mult).then_inc(self.xn_ready, 1)
        elif k % 3 == 2:
            dve.tensor_tensor(self.t[:], self.y[:], self.y[:], ALU.mult).then_inc(self.chain, 1)
        elif k % 3 == 0:
            dve.scalar_tensor_tensor(self.t[:], self.t[:], -0.5, self.var[:], ALU.mult, ALU.mult).then_inc(self.chain, 1)
        else:
            dve.scalar_tensor_tensor(self.y[:], self.t[:], 1.5, self.y[:], ALU.add, ALU.mult).then_inc(self.chain, 1)

    def transpose(self, pe, n, bank, ident):
        pe.wait_ge(self.xn_ready, 2 * (n + 1))
        for b in range(2):
            for kt in range(self.KT):
                col = 256 * kt + P * b
                ins = pe.transpose(bank[:, col:col + P], self.xn[:, b, P * kt:P * kt + P], ident[:])
        ins.then_inc(self.hT_done, 1)

    def scale_offset(self, act, n, layer, bank):
        act.wait_ge(self.ln_ready, layer + 1)
        act.wait_ge(self.hT_done, n + 1)
        for kt in range(self.KT):
            act.activation(self.hT[:, kt, :], bank[:, 256 * kt:256 * kt + 256], ACT.Identity,
                           bias=self.ln[:, 0, 2 + kt:3 + kt], scale=self.ln[:, 0, kt:kt + 1]).then_inc(self.hT_ready, 1)

    def split_hi(self, act, n, par):
        act.wait_ge(self.hT_ready, self.KT * (n + 1))
        act.activation(self.hT_hi[par][:], self.hT[:], ACT.Copy).then_inc(self.hi_ready, 1)

    def split_lo(self, dve, n, par):
        dve.wait_ge(self.hi_ready, n + 1)
        dve.tensor_tensor(self.hT_lo[par][:], self.hT[:], self.hT_hi[par][:].bitcast(F32), ALU.subtract).then_inc(self.lo_ready, 1)



class CrossStart:

    KT, MLP_UNITS = 2, 2
    pieces = [("qk", 0), ("v", 0), ("qk", 1), ("o", 0), ("v", 1), ("qk", 2), ("qk", 3), ("o", 1), ("qk", 4), ("v", 2),
              ("qk", 5), ("o", 2), ("qk", 6), ("v", 3), ("qk", 7), ("o", 3)]

    def __init__(self, m, d):
        self.d = d
        self.wide = m.sb("wide", [P, 2, 2, 1024])
        self.ctx_raw = m.sb("ctx_raw", [P, 512])
        self.mlp_raw = [[self.wide[:, i, j, 0:512].rearrange("p (t n) -> p t n", t=2) for j in range(self.MLP_UNITS)] for i in range(2)]
        self.mlp_in = [m.sems(*(f"m_{w}_in{j}" for j in range(self.MLP_UNITS))) for w in ("w1", "w2")]
        self.stage_in, self.ctx_in = m.sems("c_stage_in0", "c_stage_in1"), m.sem("c_ctx_in")

    def in_stage(self, i):
        kind = self.pieces[i % len(self.pieces)][0]
        if kind == "qk":
            return [self.wide[:, i % 2, j, 0:512].rearrange("p (t n) -> p t n", t=self.KT) for j in range(2)]
        return [self.wide[:, i % 2, :, 0:512]]

    def other(self, i, j):
        return self.wide[:, i, j, 512:1024]

    def load_ctx(self, sp, g):
        dst = self.ctx_raw[:].rearrange("p (t b l) -> p t b l", t=self.KT, b=2)
        sp.dma_start(dst, self.d["ctxT"][:, :, bass.ds(2 * g, 2), :]).then_inc(self.ctx_in, 16)

    def load_piece(self, sp, i, layer):
        kind, c = self.pieces[i % len(self.pieces)]
        at, ready = bass.ds(layer, 1), self.stage_in[i % 2]
        if kind == "o":
            for j in range(2):
                src = self.d["wo"][at].rearrange("a (h k) o -> k (a h) o", k=P)[:, 4 * c + 2 * j:4 * c + 2 * j + 2, :]
                dst = self.wide[:, i % 2, j, 0:512].rearrange("p (h o) -> p h o", h=2)
                sp.dma_start(dst, src).then_inc(ready, 16)
            return
        width, names = (512, ("wv",)) if kind == "v" else (256, ("wq", "wk"))
        for n, st in zip(names, self.in_stage(i)):
            src = self.d[n][at].rearrange("a (t p) n -> p (a t) n", p=P)[:, :, width * c:width * c + width]
            sp.dma_start(st, src).then_inc(ready, 16)

    def load_mlp(self, sp):
        w1, w2 = self.d["w1"].rearrange("(t p) f -> p t f", p=P), self.d["w2"].rearrange("(t p) o -> p t o", p=P)
        for j in range(self.MLP_UNITS):
            sp.dma_start(self.mlp_raw[0][j], w1[:, :, 256 * j:256 * j + 256]).then_inc(self.mlp_in[0][j], 16)
            sp.dma_start(self.mlp_raw[1][j], w2[:, 2 * j:2 * j + 2]).then_inc(self.mlp_in[1][j], 16)

    def load(self, sp):
        self.load_piece(sp, 0, 0)
        self.load_ctx(sp, 0)
        self.load_piece(sp, 1, 0)


def cross_layers(nc, X, ident, banks, d, G, norm, start):
    H, KT, LAYERS = 16, 2, 2
    SCALE = P ** -0.5
    BO_ROW, PER = 16, 5
    BQ, BK, BIAS_K, BIAS_V, BV = range(5)
    QK_HEADS, V_HEADS, O_HEADS = 2, 4, 4

    def bias_row(h):
        return 32 * (h % 4) + h // 4

    with ExitStack() as local:
        m = Mem(nc, local)
        w_hi = {n: m.sb(f"{n}_hi", [P, KT, 2048], F32R) for n in ("wq", "wk", "wv")}
        w_lo = {n: m.sb(f"{n}_lo", [P, KT, 2048], F32R) for n in ("wq", "wk", "wv")}
        w_hi["wo"], w_lo["wo"] = m.sb("wo_hi", [P, H, 256], F32R), m.sb("wo_lo", [P, H, 256], F32R)
        params_all = m.sb("params_all", [P, LAYERS, 5 * H])
        params = m.sb("params", [P, 1, 5 * H])
        diag = m.sb("diag", [P, 4, 4 * PER])
        tail_w = m.sb("tail_w", [P, 256])
        ctx_raw, ctx_in, stage_in = start.ctx_raw[:].rearrange("p (t b l) -> p t b l", t=KT, b=2), start.ctx_in, start.stage_in
        ctx_hi = [m.sb(f"ctx_hi{i}", [P, KT, 2, P], F32R) for i in range(2)]
        ctx_lo = [m.sb(f"ctx_lo{i}", [P, KT, 2, P], F32R) for i in range(2)]
        q_sb = [start.other(0, 0)[:, 256 * i:256 * i + 256].rearrange("p (b t) -> p b t", b=2) for i in range(2)]
        k_sb = [m.sb(f"ck{i}", [P, 2, P + 1]) for i in range(2)]
        v_sb = m.sb("cv", [P, 2, 2048])
        probs = [m.sb(f"cp{i}", [P, 2, P + 1]) for i in range(2)]
        nmax, sums, rsum = (m.sb(f"c_{n}", [P, 2, 2]) for n in ("nmax", "sums", "rsum"))
        probsT, wb, wbT = (start.other(*at)[:, 0:256].rearrange("p (b t) -> p b t", b=2) for at in ((0, 1), (1, 0), (1, 1)))
        av_hi, av_lo = m.sb("cav_hi", [P, 2, P], F32R), m.sb("cav_lo", [P, 2, P], F32R)
        one = m.sb("one", [P, 1])

        PJ, SB, TB, AVB, AUX, OUT = banks[0:2], banks[2:4], banks[4], banks[5], banks[6], banks[7]
        (cleared, small_in, bo_in, w_hi_out, w_lo_out, bqs_ready, diag_ready, tail_w_done,
         tail_w_ready, ctx_hi_ready, ctx_lo_ready, proj_done, qk_ready, bias_k_ready,
         v_ready, s_done, max_done, exp_done, rec_done, norm_done, t_done, pT_ready, wbT_ready, av_done,
         avhi_ready, avlo_ready, o_done, out_added, tail_done, tail_added, layer_open, rstd_ready) = m.sems(*(f"c_{n}" for n in (
             "cleared", "small_in", "bo_in", "w_hi_out", "w_lo_out", "bqs_ready", "diag_ready",
             "tail_w_done", "tail_w_ready", "ctx_hi_ready", "ctx_lo_ready", "proj_done", "qk_ready",
             "bias_k_ready", "v_ready", "s_done", "max_done", "exp_done", "rec_done", "norm_done", "t_done",
             "pT_ready", "wbT_ready", "av_done", "avhi_ready", "avlo_ready", "o_done", "out_added", "tail_done",
             "tail_added", "layer_open", "rstd_ready")))
        pieces = start.pieces
        NPIECE = len(pieces)

        def piece(i, tables):
            kind, c = pieces[i % NPIECE]
            if kind == "qk":
                found = [tables[n][:, :, 256 * c:256 * c + 256] for n in ("wq", "wk")]
            elif kind == "v":
                found = [tables["wv"][:, :, 512 * c:512 * c + 512]]
            else:
                found = [tables["wo"][:, 4 * c:4 * c + 4, :].rearrange("p (x h) o -> p x (h o)", x=2)]
            return list(zip(found, start.in_stage(i)))

        def piece_count(ly, i):
            return NPIECE * ly + i + 1

        V_CHUNK = {0: 0, 1: 1, 4: 2, 5: 3, 8: 4, 9: 5, 12: 6, 13: 7}

        def jobs(h):
            return [("qk", h)] * (h < H) + [("v", V_CHUNK[i]) for i in (h,) if i in V_CHUNK]

        in_order = [job for h in range(H) for job in jobs(h)]
        JOBS = len(in_order)

        def step_jobs(h):
            return enumerate(jobs(h), sum(len(jobs(i)) for i in range(h)))

        def wait_emptied(eng, gg, i, first):
            if i < 0 and first:
                return
            kind, which = in_order[i]
            n = gg - 1 if i < 0 else gg
            if kind == "qk":
                eng.wait_ge(qk_ready, 2 * (H * n + which) + 2)
            else:
                eng.wait_ge(v_ready, 8 * n + which + 1)

        def layers(eng, begin, step, finish):
            with eng.Fori(0, LAYERS) as ly:
                begin(ly)
                for h in range(H):
                    step(ly, 0, 0, h, True, False)
                with eng.Fori(0, (G - 2) // 2) as t:
                    for i in range(2):
                        for h in range(H):
                            step(ly, 2 * t + (1 + i), (1 + i) % 2, h, False, False)
                for h in range(H + 4):
                    step(ly, G - 1, 1, h, False, True)
                finish(ly)

        def unit(ly, g, h, lag, first):
            h -= lag
            if (h < 0 and first) or h >= H:
                return None
            return H * (G * ly + g) + h, h % H

        def ends_group(g, h, at, first, last):
            if h == at and not first:
                return g - 1
            if h == H + at:
                return g
            return None

        NORM_TRANSPOSE, NORM_SCALE, SPLIT_HI, SPLIT_LO = 8, 9, 10, 11

        block = local.enter_context(nc.Block())

        @block.sync
        def _(sp):
            sp.dma_start(params_all[:], d["params"].rearrange("p l n h -> p l (n h)")).then_inc(small_in, 16)
            sp.wait_ge(cleared, 2)
            with sp.Fori(0, LAYERS) as ly:
                other = ly * -1 + 1
                sp.wait_ge(ctx_lo_ready, G * ly + 1)
                for i in range(2, NPIECE + 2):
                    sp.wait_ge(w_lo_out, piece_count(ly, i - 2))
                    if i == 3:
                        start.load_ctx(sp, 1)
                    start.load_piece(sp, i, ly if i < NPIECE else other)
                    if i == 2:
                        sp.wait_ge(layer_open, ly + 1)
                        sp.dma_start(tail_w[BO_ROW:BO_ROW + 1, :], d["bo"][bass.ds(ly, 1)]).then_inc(bo_in, 16)
                with sp.Fori(2, G) as g:
                    sp.wait_ge(ctx_lo_ready, G * ly + g)
                    start.load_ctx(sp, g)
                sp.wait_ge(ctx_lo_ready, G * ly + G)
                start.load_ctx(sp, 0)
            sp.wait_ge(w_lo_out, piece_count(LAYERS - 1, NPIECE + 1))
            start.load_mlp(sp)

        @block.gpsimd
        def _(pool):
            pool.memset(tail_w[:], 0.0).then_inc(cleared, 1)
            pool.memset(diag[:], 0.0).then_inc(cleared, 1)
            pool.memset(wb, 0.0).then_inc(cleared, 1)
            pool.wait_ge(cleared, 3)
            for row in [BO_ROW] + [32 * c + 4 for c in range(4)]:
                pool.memset(wb[:, :, row:row + 1], 1.0).then_inc(cleared, 1)
            pool.memset(one[:], 1.0).then_inc(cleared, 1)
            pool.wait_ge(cleared, 9)

            def begin(ly):
                pool.wait_ge(layer_open, ly + 1)

            def step(ly, g, par, h, first, last):
                if h >= H:
                    return
                n, _ = unit(ly, g, h, 0, first)
                if not (first and h < 2):
                    pool.wait_ge(s_done, n - 1)
                for b in range(2):
                    ins = pool.tensor_tensor(k_sb[h % 2][:, b, P:P + 1], params[:, 0, H * BIAS_K + h:H * BIAS_K + h + 1], one[:], ALU.mult)
                ins.then_inc(bias_k_ready, 1)

            layers(pool, begin, step, lambda ly: None)

        @block.scalar
        def _(act):
            def split_ctx(n, par):
                act.wait_ge(ctx_in, 16 * (n + 1))
                act.activation(ctx_hi[par][:], ctx_raw, ACT.Copy).then_inc(ctx_hi_ready, 1)

            def split_piece(ly, i):
                per_layer = sum(1 if k == "v" else 2 for k, _ in pieces[i % 2::2])
                so_far = sum(1 if pieces[j % NPIECE][0] == "v" else 2 for j in range(i % 2, i + 1, 2))
                act.wait_ge(stage_in[i % 2], 16 * (per_layer * ly + so_far))
                for dst, st in piece(i, w_hi):
                    ins = act.activation(dst, st, ACT.Copy)
                ins.then_inc(w_hi_out, 1)

            split_piece(0, 0)
            split_ctx(0, 0)
            split_piece(0, 1)
            act.wait_ge(small_in, 16)
            q_bias = params_all[:, :, 0:H]
            act.mul(q_bias, q_bias, SCALE).then_inc(bqs_ready, 1)

            def begin(ly):
                act.wait_ge(layer_open, ly + 1)

            def step(ly, g, par, h, first, last):
                n = G * ly + g
                if first and h + 2 < NPIECE:
                    split_piece(ly, h + 2)
                if last and h in (H, H + 1):
                    split_piece(ly, h)
                if found := unit(ly, g, h, 1, first):
                    u, head = found
                    s = head % 2
                    act.wait_ge(max_done, u + 1)
                    if not (first and h < 3):
                        act.wait_ge(t_done, u - 1)
                    for b in range(2):
                        ins = act.activation(probs[s][:, b, :], SB[s][:, 256 * b:256 * b + P + 1], ACT.Exp,
                                             bias=nmax[:, s, b:b + 1], accum_out=sums[:, s, b:b + 1])
                    ins.then_inc(exp_done, 1)
                for i, (kind, which) in step_jobs(h):
                    if kind == "qk":
                        u, _ = unit(ly, g, h, 0, first)
                        act.wait_ge(proj_done, JOBS * n + i + 1)
                        if not (first and h < 2):
                            act.wait_ge(s_done, u - 1)
                        act.activation(q_sb[h % 2], PJ[i % 2][:, 0:256].rearrange("p (b t) -> p b t", b=2), ACT.Identity,
                                       bias=params[:, 0, H * BQ + h:H * BQ + h + 1], scale=SCALE).then_inc(qk_ready, 1)
                        act.activation(k_sb[h % 2][:, :, 0:P], PJ[i % 2][:, 256:512].rearrange("p (b t) -> p b t", b=2),
                                       ACT.Identity, bias=params[:, 0, H * BK + h:H * BK + h + 1]).then_inc(qk_ready, 1)
                if found := unit(ly, g, h, 2, first):
                    u, _ = found
                    act.wait_ge(av_done, u + 1)
                    if not (first and h < 3):
                        act.wait_ge(o_done, u)
                    act.activation(av_hi[:], AVB[:, 0:256].rearrange("p (b t) -> p b t", b=2), ACT.Copy).then_inc(avhi_ready, 1)
                if h == NORM_SCALE:
                    norm.scale_offset(act, n + 1, ly + int(last), AUX)
                if h == SPLIT_HI:
                    norm.split_hi(act, n + 1, 1 - par)
                    split_ctx(n + 1, 1 - par)

            layers(act, begin, step, lambda ly: None)

        @block.vector
        def _(dve):
            def split_ctx(n, par):
                dve.wait_ge(ctx_hi_ready, n + 1)
                dve.tensor_tensor(ctx_lo[par][:], ctx_raw, ctx_hi[par][:].bitcast(F32), ALU.subtract).then_inc(ctx_lo_ready, 1)

            def split_piece(ly, i):
                dve.wait_ge(w_hi_out, piece_count(ly, i))
                for (hi, st), (lo, _) in zip(piece(i, w_hi), piece(i, w_lo)):
                    ins = dve.tensor_tensor(lo, st, hi.bitcast(F32), ALU.subtract)
                ins.then_inc(w_lo_out, 1)

            def flat(g):
                return X[:, bass.ds(2 * g, 2), :].rearrange("p b l -> p (b l)")

            split_piece(0, 0)
            split_ctx(0, 0)
            split_piece(0, 1)
            xn = flat_of(norm.xn)
            dve.reciprocal(xn, xn).then_inc(rstd_ready, 1)
            dve.wait_ge(rstd_ready, 1)
            dve.tensor_tensor(flat(G - 1), flat(G - 1), xn, ALU.mult)
            dve.wait_ge(small_in, 16)
            dve.wait_ge(bqs_ready, 1)
            dve.wait_ge(cleared, 2)

            def begin(ly):
                dve.tensor_copy(params[:], params_all[:, bass.ds(ly, 1), :]).then_inc(layer_open, 1)
                dve.wait_ge(layer_open, ly + 1)
                by_head = lambda n: params[:, 0, H * n:H * n + H].rearrange("p (j c) -> p c j", c=4)
                dve.tensor_tensor(diag[:, :, 0:(PER + 1) * 3 + 1:PER + 1], by_head(BIAS_V), by_head(BV), ALU.subtract).then_inc(diag_ready, 1)
                dve.tensor_copy(diag[:, :, PER - 1:4 * PER:PER], by_head(BV)).then_inc(diag_ready, 1)

            def step(ly, g, par, h, first, last):
                n = G * ly + g
                if last and h == 0:
                    norm.set_layer(dve, ly + 1)
                if 2 * h < norm.STAGES:
                    norm.stage(dve, 2 * h, n + 1, 0 if last else g + 1)
                if (ended := ends_group(g, h, 3, first, last)) is not None:
                    dve.wait_ge(o_done, H * (G * ly + ended + 1))
                    dve.tensor_tensor(flat(ended), flat(ended), OUT[:], ALU.add).then_inc(out_added, 1)
                if found := unit(ly, g, h, 1, first):
                    u, head = found
                    s = head % 2
                    dve.wait_ge(s_done, u + 1)
                    dve.tensor_reduce(nmax[:, s, :], SB[s][:].rearrange("p (b t) -> p b t", b=2)[:, :, 0:P + 1], AX_X,
                                      ALU.max, negate=True).then_inc(max_done, 1)
                if found := unit(ly, g, h, 2, first):
                    u, head = found
                    dve.wait_ge(t_done, u + 1)
                    if not (first and h < 3):
                        dve.wait_ge(av_done, u)
                    dve.tensor_copy(probsT, TB[:, 0:256].rearrange("p (b t) -> p b t", b=2)).then_inc(pT_ready, 1)
                    if head == H - 1:
                        dve.tensor_copy(wbT, TB[:, 256:512].rearrange("p (b t) -> p b t", b=2)).then_inc(wbT_ready, 1)
                if found := unit(ly, g, h, 1, first):
                    u, head = found
                    s = head % 2
                    dve.wait_ge(exp_done, u + 1)
                    dve.reciprocal(rsum[:, s, :], sums[:, s, :]).then_inc(rec_done, 1)
                    if 2 * h + 1 < norm.STAGES:
                        norm.stage(dve, 2 * h + 1, n + 1, 0 if last else g + 1)
                    dve.wait_ge(rec_done, u + 1)
                    if head == 0 and not first:
                        dve.wait_ge(t_done, u)
                    for b in range(2):
                        dve.tensor_scalar(probs[s][:, b, 0:P], probs[s][:, b, 0:P], rsum[:, s, b:b + 1], None, ALU.mult)
                    col = bias_row(head)
                    dve.tensor_tensor(wb[:, :, col:col + 1], probs[s][:, :, P:P + 1], rsum[:, s, :].rearrange("p (b o) -> p b o", o=1),
                                      ALU.mult).then_inc(norm_done, 1)
                elif 2 * h + 1 < norm.STAGES:
                    norm.stage(dve, 2 * h + 1, n + 1, 0 if last else g + 1)
                if first and h + 2 < NPIECE:
                    split_piece(ly, h + 2)
                if last and h in (H, H + 1):
                    split_piece(ly, h)
                for i, (kind, c) in step_jobs(h):
                    if kind == "v":
                        dve.wait_ge(proj_done, JOBS * n + i + 1)
                        if not first:
                            dve.wait_ge(av_done, H * (n - 1) + 4 * (c // 2) + 4)
                        cut = slice(512 * (c // 2), 512 * (c // 2) + 512)
                        dve.tensor_copy(v_sb[:, c % 2, cut], PJ[i % 2][:]).then_inc(v_ready, 1)
                if found := unit(ly, g, h, 2, first):
                    u, _ = found
                    dve.wait_ge(avhi_ready, u + 1)
                    dve.tensor_tensor(av_lo[:], AVB[:, 0:256].rearrange("p (b t) -> p b t", b=2), av_hi[:].bitcast(F32),
                                      ALU.subtract).then_inc(avlo_ready, 1)
                if (ended := ends_group(g, h, 3, first, last)) is not None:
                    dve.wait_ge(tail_done, G * ly + ended + 1)
                    dve.wait_ge(out_added, G * ly + ended + 1)
                    dve.tensor_tensor(flat(ended), flat(ended), AUX[:], ALU.add).then_inc(tail_added, 1)
                if h == SPLIT_LO:
                    norm.split_lo(dve, n + 1, 1 - par)
                    split_ctx(n + 1, 1 - par)
                if first and h == H - 1:
                    dve.wait_ge(tail_w_done, ly + 1)
                    for c in range(4):
                        ins = dve.tensor_copy(tail_w[32 * c:32 * c + PER, :], AUX[32 * c:32 * c + PER, 0:256])
                    ins.then_inc(tail_w_ready, 1)

            def finish(ly):
                dve.wait_ge(tail_added, G * (ly + 1))

            layers(dve, begin, step, finish)

        @block.tensor
        def _(pe):
            def project(ly, n, par, i, kind, which, first):
                if (kind, which) == ("qk", 0):
                    pe.wait_ge(norm.lo_ready, n + 1)
                    pe.wait_ge(ctx_lo_ready, n + 1)
                if first:
                    used = ("qk", which // QK_HEADS) if kind == "qk" else ("v", which // 2)
                    pe.wait_ge(w_lo_out, piece_count(ly, pieces.index(used)))
                wait_emptied(pe, n, i - 2, first)
                bank = PJ[i % 2]
                if kind == "qk":
                    cut = slice(P * which, P * which + P)
                    for j, (w, hi, lo) in enumerate((("wq", norm.hT_hi[par], norm.hT_lo[par]), ("wk", ctx_hi[par], ctx_lo[par]))):
                        out = bank[:, 256 * j:256 * j + 256]
                        for kt in range(KT):
                            ins = three_pass(pe, out, w_hi[w][:, kt, cut], w_lo[w][:, kt, cut],
                                             hi[:, kt], lo[:, kt], kt == 0, kt == KT - 1)
                else:
                    b = which % 2
                    cut = slice(512 * (which // 2), 512 * (which // 2) + 512)
                    for kt in range(KT):
                        ins = three_pass(pe, bank[:], ctx_hi[par][:, kt, b, :], ctx_lo[par][:, kt, b, :],
                                         w_hi["wv"][:, kt, cut], w_lo["wv"][:, kt, cut], kt == 0, kt == KT - 1)
                ins.then_inc(proj_done, 1)

            def tail_weights(ly):
                pe.wait_ge(diag_ready, 2 * (ly + 1))
                pe.wait_ge(norm.hT_ready, KT * (G * ly + 2))
                for j in range(4):
                    for c in range(4):
                        for w in (w_hi, w_lo):
                            ins = pe.matmul(AUX[32 * c:32 * c + PER, 0:256], diag[:, c, PER * j:PER * j + PER],
                                            w["wo"][:, 4 * j + c, :].bitcast(F32), start=(j == 0 and w is w_hi),
                                            stop=(j == 3 and w is w_lo))
                ins.then_inc(tail_w_done, 1)

            def step(ly, g, par, h, first, last):
                n = G * ly + g
                if found := unit(ly, g, h, 1, first):
                    u, head = found
                    s = head % 2
                    pe.wait_ge(qk_ready, 2 * u + 2)
                    pe.wait_ge(bias_k_ready, u + 1)
                    if not (first and h < 3):
                        pe.wait_ge(exp_done, u - 1)
                    for b in range(2):
                        ins = pe.matmul(SB[s][:, 256 * b:256 * b + P + 1], q_sb[s][:, b, :], k_sb[s][:, b, :],
                                        start=True, stop=True)
                    ins.then_inc(s_done, 1)
                if found := unit(ly, g, h, 2, first):
                    u, head = found
                    s = head % 2
                    pe.wait_ge(norm_done, u + 1)
                    if not (first and h < 3):
                        pe.wait_ge(pT_ready, u)
                    if head == 0 and not first:
                        pe.wait_ge(wbT_ready, n)
                    for b in range(2):
                        ins = pe.transpose(TB[:, P * b:P * b + P], probs[s][:, b, 0:P], ident[:])
                    if head == H - 1:
                        for b in range(2):
                            ins = pe.transpose(TB[:, 256 + P * b:256 + P * b + P], wb[:, b, :], ident[:])
                    ins.then_inc(t_done, 1)
                if (ended := ends_group(g, h, 3, first, last)) is not None:
                    e = G * ly + ended
                    pe.wait_ge(wbT_ready, e + 1)
                    pe.wait_ge(tail_w_ready, ly + 1)
                    pe.wait_ge(bo_in, 16 * (ly + 1))
                    pe.wait_ge(norm.hT_ready, KT * (e + 2))
                    for b in range(2):
                        ins = pe.matmul(AUX[:, 256 * b:256 * b + 256], wbT[:, b, :], tail_w[:], start=True, stop=True)
                    ins.then_inc(tail_done, 1)
                for i, (kind, which) in step_jobs(h):
                    project(ly, n, par, i, kind, which, first)
                if found := unit(ly, g, h, 2, first):
                    u, head = found
                    pe.wait_ge(pT_ready, u + 1)
                    pe.wait_ge(v_ready, 8 * (n - (1 if h < 2 else 0)) + 2 * (head // 4) + 2)
                    if not (first and h < 3):
                        pe.wait_ge(avlo_ready, u)
                    for b in range(2):
                        ins = pe.matmul(AVB[:, P * b:P * b + P], v_sb[:, b, P * head:P * head + P], probsT[:, b, :],
                                        start=True, stop=True)
                    ins.then_inc(av_done, 1)
                if found := unit(ly, g, h, 3, first):
                    u, head = found
                    pe.wait_ge(avlo_ready, u + 1)
                    if first:
                        pe.wait_ge(w_lo_out, piece_count(ly, pieces.index(("o", head // O_HEADS))))
                    if head == 0 and first:
                        pe.wait_ge(layer_open, ly + 1)
                    elif head == 0:
                        pe.wait_ge(out_added, n)
                    for b in range(2):
                        ins = three_pass(pe, OUT[:, 256 * b:256 * b + 256], av_hi[:, b, :], av_lo[:, b, :],
                                         w_hi["wo"][:, head, :], w_lo["wo"][:, head, :],
                                         head == 0 and b == 0, head == H - 1 and b == 1, skip=True)
                    ins.then_inc(o_done, 1)
                if h == NORM_TRANSPOSE:
                    if not first:
                        pe.wait_ge(tail_added, n)
                    norm.transpose(pe, n + 1, AUX, ident)
                if first and h == H - 1:
                    tail_weights(ly)

            layers(pe, lambda ly: None, step, lambda ly: None)



def mlp(nc, X, ident, banks, d, out, G, norm, start):
    KT, F, J = 2, 1024, 4
    N0 = 2 * G
    LAG = 2
    with ExitStack() as local:
        m = Mem(nc, local)
        w1_raw, w2_raw = m.sb("w1_raw", [P, KT, F]), m.sb("w2_raw", [P, 8, 256])
        w1_hi, w1_lo = m.sb("w1_hi", [P, KT, F], F32R), m.sb("w1_lo", [P, KT, F], F32R)
        w2_hi, w2_lo = m.sb("w2_hi", [P, 8, 256], F32R), m.sb("w2_lo", [P, 8, 256], F32R)
        warm = m.sb("m_warm", [P, 1])
        b1, b2 = m.sb("b1", [P, 8]), m.sb("b2", [P, 2, 256])
        act_f = [m.sb(f"gelu{i}", [P, 2, 256]) for i in range(J)]
        act_hi = [m.sb(f"gelu_hi{i}", [P, 2, 256], F32R) for i in range(J)]
        act_lo = [m.sb(f"gelu_lo{i}", [P, 2, 256], F32R) for i in range(J)]
        FC1, AUX, OUT = banks[0:2], banks[2], banks[3:5]
        (small_in, w_hi_out, w_lo_out, fc1_done, gelu_ready, act_hi_ready, act_lo_ready, b2_added, fc2_done, y_ready,
         stored) = m.sems(*(f"m_{n}" for n in (
             "small_in", "w_hi_out", "w_lo_out", "fc1_done", "gelu_ready", "act_hi_ready", "act_lo_ready", "b2_added",
             "fc2_done", "y_ready", "stored")))
        w1_in, w2_in = (start.mlp_in[i] + [m.sem(f"m_{w}_in{j}") for j in range(start.MLP_UNITS, J)] for i, w in enumerate(("w1", "w2")))

        pieces = []
        for j in range(J):
            cut, rows = slice(256 * j, 256 * j + 256), slice(2 * j, 2 * j + 2)
            raw = [r[j] for r in start.mlp_raw] if j < start.MLP_UNITS else (w1_raw[:, :, cut], w2_raw[:, rows])
            pieces.append((w1_in[j], raw[0], w1_hi[:, :, cut], w1_lo[:, :, cut]))
            pieces.append((w2_in[j], raw[1], w2_hi[:, rows], w2_lo[:, rows]))
        AHEAD = 3

        def step_pieces(j):
            return range(AHEAD + 2 * j, min(AHEAD + 2 * j + 2, 2 * J))

        def groups(eng, step):
            for j in range(J):
                step(0, 0, j, True, False)
            with eng.Fori(0, (G - 2) // 2) as t:
                for i in range(2):
                    for j in range(J):
                        step(2 * t + (1 + i), (1 + i) % 2, j, False, False)
            for j in range(J + LAG):
                step(G - 1, 1, j, False, True)

        def flat(t):
            return t.rearrange("p b l -> p (b l)")

        def Xg(g):
            return X[:, bass.ds(2 * g, 2), :]

        block = local.enter_context(nc.Block())

        @block.sync
        def _(sp):
            w1, w2 = d["w1"].rearrange("(t p) f -> p t f", p=P), d["w2"].rearrange("(t p) o -> p t o", p=P)
            sp.dma_start(b1[:], d["b1"]).then_inc(small_in, 16)
            for b in range(2):
                sp.dma_start(b2[:, b, :], d["b2"].to_broadcast([P, 256])).then_inc(small_in, 16)
            for j in range(start.MLP_UNITS, J):
                sp.dma_start(w1_raw[:, :, 256 * j:256 * j + 256], w1[:, :, 256 * j:256 * j + 256]).then_inc(w1_in[j], 16)
                sp.dma_start(w2_raw[:, 2 * j:2 * j + 2], w2[:, 2 * j:2 * j + 2]).then_inc(w2_in[j], 16)
            with sp.Fori(0, G) as g:
                sp.wait_ge(y_ready, g + 1)
                sp.dma_start(out[bass.ds(2 * g, 2)].rearrange("b q f -> q b f"), Xg(g)).then_inc(stored, 16)
            sp.wait_ge(stored, 16 * G)

        @block.gpsimd
        def _(pool):
            pool.wait_ge(small_in, 48)
            with pool.Fori(0, G) as g:
                pool.wait_ge(norm.xn_ready, 2 * (N0 + g + 1))
                pool.tensor_tensor(Xg(g), Xg(g), b2[:], ALU.add).then_inc(b2_added, 1)

        @block.scalar
        def _(act):
            def split_piece(i):
                loaded, raw, hi, _ = pieces[i]
                act.wait_ge(loaded, 16)
                act.activation(hi, raw, ACT.Copy).then_inc(w_hi_out, 1)

            split_piece(0)
            act.activation(warm[:], norm.y[:, 0:1], ACT.Gelu)
            for i in range(1, AHEAD):
                split_piece(i)
            act.wait_ge(small_in, 48)

            def step(g, par, j, first, last):
                if j >= J:
                    return
                u = J * g + j
                if j == 3 and not last:
                    norm.scale_offset(act, N0 + g + 1, 2, AUX)
                    norm.split_hi(act, N0 + g + 1, 1 - par)
                act.wait_ge(fc1_done, u + 1)
                if not first:
                    act.wait_ge(act_lo_ready, u - J + 1)
                for i in range(2):
                    ins = act.activation(act_f[j][:, i, :], FC1[j % 2][:, 256 * i:256 * i + 256], ACT.Gelu,
                                         bias=b1[:, 2 * j + i:2 * j + i + 1])
                ins.then_inc(gelu_ready, 1)
                act.wait_ge(gelu_ready, u + 1)
                if not first:
                    act.wait_ge(fc2_done, u - J + 1)
                act.activation(act_hi[j][:], act_f[j][:], ACT.Copy).then_inc(act_hi_ready, 1)
                if first:
                    for i in step_pieces(j):
                        split_piece(i)

            groups(act, step)

        @block.vector
        def _(dve):
            def split_piece(i):
                _, raw, hi, lo = pieces[i]
                dve.wait_ge(w_hi_out, i + 1)
                dve.tensor_tensor(lo, raw, hi.bitcast(F32), ALU.subtract).then_inc(w_lo_out, 1)

            for i in range(AHEAD):
                split_piece(i)

            norm_at = [((0, 1, 2, 3, 4, 5, 6, 7, 8, 9, 10), (11, 12), ()), ((13, 14), (), ()), ((), (), ()), ((), (), ())]

            def add_output(g, par):
                dve.wait_ge(fc2_done, J * (g + 1))
                dve.wait_ge(b2_added, g + 1)
                dve.tensor_tensor(flat(Xg(g)), flat(Xg(g)), OUT[par][:], ALU.add).then_inc(y_ready, 1)

            def step(g, par, j, first, last):
                u = J * g + j

                def norm_stage(place):
                    if j < J and not last:
                        for k in norm_at[j][place]:
                            norm.stage(dve, k, N0 + g + 1, g + 1)

                norm_stage(0)
                if j == 3 and not last:
                    norm.split_lo(dve, N0 + g + 1, 1 - par)
                if j < J:
                    dve.wait_ge(act_hi_ready, u + 1)
                    dve.tensor_tensor(act_lo[j][:], act_f[j][:], act_hi[j][:].bitcast(F32), ALU.subtract).then_inc(act_lo_ready, 1)
                    norm_stage(1)
                if j == LAG - 1 and not first:
                    add_output(g - 1, 1 - par)
                if first and j < J:
                    for i in step_pieces(j):
                        split_piece(i)
                norm_stage(2)

            groups(dve, step)
            add_output(G - 1, 1)

        @block.tensor
        def _(pe):
            def second(u, par, j, first):
                if first:
                    pe.wait_ge(w_lo_out, 2 * j + 2)
                pe.wait_ge(act_lo_ready, u + 1)
                for b in range(2):
                    for i in range(2):
                        cut = slice(P * b, P * b + P)
                        ins = three_pass(pe, OUT[par][:, 256 * b:256 * b + 256], act_hi[j][:, i, cut], act_lo[j][:, i, cut],
                                         w2_hi[:, 2 * j + i, :], w2_lo[:, 2 * j + i, :],
                                         j == 0 and b == 0 and i == 0, j == J - 1 and b == 1 and i == 1, skip=True)
                ins.then_inc(fc2_done, 1)

            def step(g, par, j, first, last):
                u = J * g + j
                if j == 0 and not first:
                    second(u - LAG, 1 - par, J - LAG, False)
                if j < J:
                    if j == 0:
                        pe.wait_ge(norm.lo_ready, N0 + g + 1)
                    if not (first and j < 2):
                        pe.wait_ge(gelu_ready, u - 1)
                    if first:
                        pe.wait_ge(w_lo_out, 2 * j + 1)
                    for i in range(2):
                        cut = slice(P * (2 * j + i), P * (2 * j + i) + P)
                        for kt in range(KT):
                            ins = three_pass(pe, FC1[j % 2][:, 256 * i:256 * i + 256], w1_hi[:, kt, cut], w1_lo[:, kt, cut],
                                             norm.hT_hi[par][:, kt], norm.hT_lo[par][:, kt], kt == 0, kt == KT - 1)
                    ins.then_inc(fc1_done, 1)
                if j >= LAG:
                    second(u - LAG, par, j - LAG, first)
                elif j > 0 and not first:
                    second(u - LAG, 1 - par, J + j - LAG, False)
                if j == 2 and not last:
                    norm.transpose(pe, N0 + g + 1, AUX, ident)

            groups(pe, step)


def sequence(nc, d, out):
    G = 8
    with ExitStack() as ctx:
        m = Mem(nc, ctx)
        X = m.sb("X", [P, 2 * G, 256])
        ident = m.sb("ident", [P, P])
        banks = [m.psum(f"bank{i}") for i in range(8)]
        norm, start = NormedInput(m, X, d), CrossStart(m, d)
        attention0(nc, X, ident, banks, d, G, norm, start)
        norm.add_second(m)
        cross_layers(nc, X, ident, banks, d, G, norm, start)
        mlp(nc, X, ident, banks, d, out, G, norm, start)



def _layout(inputs):
    import numpy as np

    a = {k: np.asarray(v) for k, v in inputs.items()}
    l0, l1 = (lambda n: a[f"L0_xattn_{n}"]), (lambda n: a[f"L1_xattn_{n}"])
    both = lambda n: np.stack([l1(f"{n}1"), l1(f"{n}2")])
    heads = lambda t: t.reshape(2, 16, P).transpose(0, 2, 1)
    ln = np.stack([np.stack([l1(f"{n}_scale"), l1(f"{n}_offset")]) for n in ("ln1", "ln2", "ln_mlp")])
    ln = ln.reshape(3, 2, 2, P).transpose(3, 0, 1, 2)
    params = np.stack([heads(both(n)) for n in ("bq", "bk", "bias_k", "bias_v", "bv")], axis=2).transpose(1, 0, 2, 3)
    ctx = a["ctx_2048"]
    arrays = {
        "x": a["x"], "u": ctx, "ctxT": ctx.transpose(2, 0, 1).reshape(2, P, 16, P).transpose(1, 0, 2, 3),
        "wz0": l0("Wqkv0").T, "wz1": l0("Wqkv1").T, "wu0": l0("Winj0").T, "wu1": l0("Winj1").T, "wo0": l0("Wo").T,
        "rwb": l0("r_w_bias").reshape(8, P).T, "bo0": l0("bo").reshape(P, 1), "ident": np.eye(P, dtype=np.float32),
        "wq": both("wq"), "wk": both("wk"), "wv": both("wv"), "wo": both("wo"),
        "params": params, "bo": both("bo"), "ln": ln,
        "w1": l1("w_fc1"), "b1": l1("b_fc1").reshape(8, P).T, "w2": l1("w_fc2"), "b2": l1("b_fc2").reshape(1, 256),
    }
    return {k: np.ascontiguousarray(v) for k, v in arrays.items()}


def kernel(**inputs):
    import concourse.bacc as bacc
    from concourse.bass_utils import run_bass_kernel_spmd

    nc = bacc.Bacc("TRN2", target_bir_lowering=False, num_devices=1)
    arrays = {f"in_{name}": a for name, a in _layout(inputs).items()}
    d = {name[3:]: nc.dram_tensor(name, a.shape, mybir.dt.from_np(a.dtype), kind="ExternalInput").ap()
         for name, a in arrays.items()}
    out = nc.dram_tensor("out", (16, P, 256), F32, kind="ExternalOutput").ap()
    sequence(nc, d, out)
    return run_bass_kernel_spmd(nc, [arrays], core_ids=[0]).results[0]["out"]
```
